# Optimizing a Trainium2 kernel written in Bass

```python
import numpy as np
import jax
import jax.numpy as jnp

def _softmax(x, axis=-1):
    return jax.nn.softmax(x, axis=axis)

def _gelu(x):
    return jax.nn.gelu(x, approximate=True)

def _silu(x):
    return jax.nn.silu(x)

def _sigmoid(x):
    return jax.nn.sigmoid(x)

def _layernorm(x, axis=-1, eps=1e-05):
    m = jnp.mean(x, axis=axis, keepdims=True)
    v = jnp.var(x, axis=axis, keepdims=True)
    return (x - m) / jnp.sqrt(v + eps)

def _scatter_add(tgt, idx, src, axis=0):
    return tgt.at[idx].add(src)

def _segment_sum(src, seg, n):
    return jax.ops.segment_sum(src, seg, n)
kernel_name = 'mk_conv_seq_d2_conv_nhwc256_r4_d8293d'

def setup_inputs(seed: int=0):
    np.random.seed(seed)
    _w = jnp.asarray

    def _rec_inputs():
        import jax
        import jax.numpy as jnp
        _gk = jax.random.key(seed)
        x = -0.0003957 + 1 * jax.random.normal(jax.random.fold_in(_gk, 1), (16, 28, 28, 64), jnp.float32)
        return x
    x = _rec_inputs()

    def _L0_conv_setup():
        import jax, jax.numpy as jnp
        import numpy as np
        WS = 7
        SHIFT = 3
        HEADS = 8
        EPS = 1.001e-05
        B, H, W, C = (16, 28, 28, 64)

        def _rel_index(ws):
            coords = np.arange(ws)
            gx, gy = np.meshgrid(coords, coords, indexing='ij')
            fx, fy = (gx.reshape(-1), gy.reshape(-1))
            rx = fx[:, None] - fx[None, :]
            ry = fy[:, None] - fy[None, :]
            return ((rx + ws - 1) * (2 * ws - 1) + (ry + ws - 1)).reshape(-1)
        REL_IDX = jnp.asarray(_rel_index(WS))

        def _shift_mask(hh, ww, ws, shift):
            img = np.zeros((hh, ww), dtype=np.int32)
            cnt = 0
            for hs in (slice(0, hh - ws), slice(hh - ws, hh - shift), slice(hh - shift, hh)):
                for wsl in (slice(0, ww - ws), slice(ww - ws, ww - shift), slice(ww - shift, ww)):
                    img[hs, wsl] = cnt
                    cnt += 1
            wins = img.reshape(hh // ws, ws, ww // ws, ws).transpose(0, 2, 1, 3).reshape(-1, ws * ws)
            diff = wins[:, None, :] - wins[:, :, None]
            return jnp.asarray(np.where(diff == 0, 0.0, -100.0).astype(np.float32))
        NW = H // WS * (W // WS)
        N = WS * WS
        MASK0 = jnp.zeros((NW, N, N), jnp.float32)
        MASK1 = _shift_mask(H, W, WS, SHIFT)

        def layer_norm(x, g, b):
            mu = jnp.mean(x, axis=-1, keepdims=True)
            var = jnp.var(x, axis=-1, keepdims=True)
            return (x - mu) * jax.lax.rsqrt(var + EPS) * g + b

        def swin_block_fn(x, shift, mask, ln1_g, ln1_b, qkv_w, qkv_b, bias_tab, proj_w, proj_b, ln2_g, ln2_b, fc1_w, fc1_b, fc2_w, fc2_b):
            Bn, Hh, Ww, Cc = x.shape
            hd = Cc // HEADS
            y = layer_norm(x, ln1_g, ln1_b)
            if shift:
                y = jnp.roll(y, (-shift, -shift), axis=(1, 2))
            wins = y.reshape(Bn, Hh // WS, WS, Ww // WS, WS, Cc)
            wins = wins.transpose(0, 1, 3, 2, 4, 5).reshape(-1, N, Cc)
            qkv = (wins @ qkv_w + qkv_b).reshape(-1, N, 3, HEADS, hd).transpose(2, 0, 3, 1, 4)
            q, k, v = (qkv[0], qkv[1], qkv[2])
            attn = jnp.einsum('whnd,whmd->whnm', q, k) * hd ** (-0.5)
            bias = bias_tab[REL_IDX].reshape(N, N, HEADS).transpose(2, 0, 1)
            attn = attn + bias[None]
            attn = attn.reshape(Bn, NW, HEADS, N, N) + mask[None, :, None]
            attn = jax.nn.softmax(attn.reshape(-1, HEADS, N, N), axis=-1)
            out = jnp.einsum('whnm,whmd->whnd', attn, v).transpose(0, 2, 1, 3).reshape(-1, N, Cc)
            out = out @ proj_w + proj_b
            out = out.reshape(Bn, Hh // WS, Ww // WS, WS, WS, Cc)
            out = out.transpose(0, 1, 3, 2, 4, 5).reshape(Bn, Hh, Ww, Cc)
            if shift:
                out = jnp.roll(out, (shift, shift), axis=(1, 2))
            x = x + out
            z = layer_norm(x, ln2_g, ln2_b)
            z = jax.nn.gelu(z @ fc1_w + fc1_b, approximate=False)
            return x + (z @ fc2_w + fc2_b)
        key = jax.random.key(seed)
        ks = jax.random.split(key, 16)

        def w(k, shape):
            return jax.random.normal(k, shape, jnp.float32) * 0.02
        inp = {'x': jax.random.normal(ks[0], (B, H, W, C), jnp.float32)}
        i = 1
        for b in range(2):
            inp[f'ln1_g{b}'] = jnp.ones((C,), jnp.float32)
            inp[f'ln1_b{b}'] = jnp.zeros((C,), jnp.float32)
            inp[f'qkv_w{b}'] = w(ks[i], (C, 3 * C))
            i += 1
            inp[f'qkv_b{b}'] = jnp.zeros((3 * C,), jnp.float32)
            inp[f'bias_tab{b}'] = w(ks[i], ((2 * WS - 1) ** 2, HEADS))
            i += 1
            inp[f'proj_w{b}'] = w(ks[i], (C, C))
            i += 1
            inp[f'proj_b{b}'] = jnp.zeros((C,), jnp.float32)
            inp[f'ln2_g{b}'] = jnp.ones((C,), jnp.float32)
            inp[f'ln2_b{b}'] = jnp.zeros((C,), jnp.float32)
            inp[f'fc1_w{b}'] = w(ks[i], (C, 4 * C))
            i += 1
            inp[f'fc1_b{b}'] = jnp.zeros((4 * C,), jnp.float32)
            inp[f'fc2_w{b}'] = w(ks[i], (4 * C, C))
            i += 1
            inp[f'fc2_b{b}'] = jnp.zeros((C,), jnp.float32)
        return inp
    _L0_conv_all = _L0_conv_setup()
    _L0_conv_in = {k: v for k, v in _L0_conv_all.items() if k in ('ln1_g0', 'ln1_b0', 'qkv_w0', 'qkv_b0', 'bias_tab0', 'proj_w0', 'proj_b0', 'ln2_g0', 'ln2_b0', 'fc1_w0', 'fc1_b0', 'fc2_w0', 'fc2_b0', 'ln1_g1', 'ln1_b1', 'qkv_w1', 'qkv_b1', 'bias_tab1', 'proj_w1', 'proj_b1', 'ln2_g1', 'ln2_b1', 'fc1_w1', 'fc1_b1', 'fc2_w1', 'fc2_b1')}
    del _L0_conv_all

    def _L1_conv_setup():
        import jax, jax.numpy as jnp
        import numpy as np
        EPS = 1e-05
        M_PER_GROUP = 16
        ITER_NUM = 5

        def _iter_norm_whiten(x, gamma, beta):
            B, H, W, C = x.shape
            g = C // M_PER_GROUP
            m = M_PER_GROUP
            N = B * H * W
            xt = jnp.transpose(x, (3, 0, 1, 2)).reshape(C, N)
            mu = jnp.mean(xt, axis=1, keepdims=True)
            f = xt - mu
            fg = f.reshape(g, m, N)
            cov = jnp.einsum('gmn,gkn->gmk', fg, fg) / (jnp.float32(N) - 1.0)
            eye = jnp.eye(m, dtype=x.dtype)
            cov = (1.0 - EPS) * cov + EPS * eye
            trace = jnp.trace(cov, axis1=1, axis2=2)[:, None, None]
            sigma = cov / trace
            P = jnp.broadcast_to(eye, (g, m, m))
            for _ in range(ITER_NUM):
                P = (3.0 * P - P @ P @ P @ sigma) / 2.0
            wm = P / jnp.sqrt(trace)
            f_hat = jnp.einsum('gmk,gkn->gmn', wm, fg).reshape(C, B, H, W)
            out = jnp.transpose(f_hat, (1, 2, 3, 0))
            return gamma * out + beta
        key = jax.random.key(seed)
        k1, = jax.random.split(key, 1)
        x = jax.random.normal(k1, (16, 56, 56, 64), dtype=jnp.float32)
        gamma = jnp.ones((1, 1, 1, 64), dtype=jnp.float32)
        beta = jnp.zeros((1, 1, 1, 64), dtype=jnp.float32)
        return {'x': x, 'gamma': gamma, 'beta': beta}
    _L1_conv_all = _L1_conv_setup()
    _L1_conv_in = {k: v for k, v in _L1_conv_all.items() if k in ('gamma', 'beta')}
    del _L1_conv_all
    return {'x': x, 'L0_conv_ln1_g0': _L0_conv_in['ln1_g0'], 'L0_conv_ln1_b0': _L0_conv_in['ln1_b0'], 'L0_conv_qkv_w0': _L0_conv_in['qkv_w0'], 'L0_conv_qkv_b0': _L0_conv_in['qkv_b0'], 'L0_conv_bias_tab0': _L0_conv_in['bias_tab0'], 'L0_conv_proj_w0': _L0_conv_in['proj_w0'], 'L0_conv_proj_b0': _L0_conv_in['proj_b0'], 'L0_conv_ln2_g0': _L0_conv_in['ln2_g0'], 'L0_conv_ln2_b0': _L0_conv_in['ln2_b0'], 'L0_conv_fc1_w0': _L0_conv_in['fc1_w0'], 'L0_conv_fc1_b0': _L0_conv_in['fc1_b0'], 'L0_conv_fc2_w0': _L0_conv_in['fc2_w0'], 'L0_conv_fc2_b0': _L0_conv_in['fc2_b0'], 'L0_conv_ln1_g1': _L0_conv_in['ln1_g1'], 'L0_conv_ln1_b1': _L0_conv_in['ln1_b1'], 'L0_conv_qkv_w1': _L0_conv_in['qkv_w1'], 'L0_conv_qkv_b1': _L0_conv_in['qkv_b1'], 'L0_conv_bias_tab1': _L0_conv_in['bias_tab1'], 'L0_conv_proj_w1': _L0_conv_in['proj_w1'], 'L0_conv_proj_b1': _L0_conv_in['proj_b1'], 'L0_conv_ln2_g1': _L0_conv_in['ln2_g1'], 'L0_conv_ln2_b1': _L0_conv_in['ln2_b1'], 'L0_conv_fc1_w1': _L0_conv_in['fc1_w1'], 'L0_conv_fc1_b1': _L0_conv_in['fc1_b1'], 'L0_conv_fc2_w1': _L0_conv_in['fc2_w1'], 'L0_conv_fc2_b1': _L0_conv_in['fc2_b1'], 'L1_conv_gamma': _L1_conv_in['gamma'], 'L1_conv_beta': _L1_conv_in['beta']}

def reference(x, L0_conv_ln1_g0, L0_conv_ln1_b0, L0_conv_qkv_w0, L0_conv_qkv_b0, L0_conv_bias_tab0, L0_conv_proj_w0, L0_conv_proj_b0, L0_conv_ln2_g0, L0_conv_ln2_b0, L0_conv_fc1_w0, L0_conv_fc1_b0, L0_conv_fc2_w0, L0_conv_fc2_b0, L0_conv_ln1_g1, L0_conv_ln1_b1, L0_conv_qkv_w1, L0_conv_qkv_b1, L0_conv_bias_tab1, L0_conv_proj_w1, L0_conv_proj_b1, L0_conv_ln2_g1, L0_conv_ln2_b1, L0_conv_fc1_w1, L0_conv_fc1_b1, L0_conv_fc2_w1, L0_conv_fc2_b1, L1_conv_gamma, L1_conv_beta):
    import jax
    import jax.numpy as jnp

    def _L0_conv_ref(x, ln1_g0, ln1_b0, qkv_w0, qkv_b0, bias_tab0, proj_w0, proj_b0, ln2_g0, ln2_b0, fc1_w0, fc1_b0, fc2_w0, fc2_b0, ln1_g1, ln1_b1, qkv_w1, qkv_b1, bias_tab1, proj_w1, proj_b1, ln2_g1, ln2_b1, fc1_w1, fc1_b1, fc2_w1, fc2_b1):
        import jax, jax.numpy as jnp
        import numpy as np
        WS = 7
        SHIFT = 3
        HEADS = 8
        EPS = 1.001e-05
        B, H, W, C = (16, 28, 28, 64)

        def _rel_index(ws):
            coords = np.arange(ws)
            gx, gy = np.meshgrid(coords, coords, indexing='ij')
            fx, fy = (gx.reshape(-1), gy.reshape(-1))
            rx = fx[:, None] - fx[None, :]
            ry = fy[:, None] - fy[None, :]
            return ((rx + ws - 1) * (2 * ws - 1) + (ry + ws - 1)).reshape(-1)
        REL_IDX = jnp.asarray(_rel_index(WS))

        def _shift_mask(hh, ww, ws, shift):
            img = np.zeros((hh, ww), dtype=np.int32)
            cnt = 0
            for hs in (slice(0, hh - ws), slice(hh - ws, hh - shift), slice(hh - shift, hh)):
                for wsl in (slice(0, ww - ws), slice(ww - ws, ww - shift), slice(ww - shift, ww)):
                    img[hs, wsl] = cnt
                    cnt += 1
            wins = img.reshape(hh // ws, ws, ww // ws, ws).transpose(0, 2, 1, 3).reshape(-1, ws * ws)
            diff = wins[:, None, :] - wins[:, :, None]
            return jnp.asarray(np.where(diff == 0, 0.0, -100.0).astype(np.float32))
        NW = H // WS * (W // WS)
        N = WS * WS
        MASK0 = jnp.zeros((NW, N, N), jnp.float32)
        MASK1 = _shift_mask(H, W, WS, SHIFT)

        def layer_norm(x, g, b):
            mu = jnp.mean(x, axis=-1, keepdims=True)
            var = jnp.var(x, axis=-1, keepdims=True)
            return (x - mu) * jax.lax.rsqrt(var + EPS) * g + b

        def swin_block_fn(x, shift, mask, ln1_g, ln1_b, qkv_w, qkv_b, bias_tab, proj_w, proj_b, ln2_g, ln2_b, fc1_w, fc1_b, fc2_w, fc2_b):
            Bn, Hh, Ww, Cc = x.shape
            hd = Cc // HEADS
            y = layer_norm(x, ln1_g, ln1_b)
            if shift:
                y = jnp.roll(y, (-shift, -shift), axis=(1, 2))
            wins = y.reshape(Bn, Hh // WS, WS, Ww // WS, WS, Cc)
            wins = wins.transpose(0, 1, 3, 2, 4, 5).reshape(-1, N, Cc)
            qkv = (wins @ qkv_w + qkv_b).reshape(-1, N, 3, HEADS, hd).transpose(2, 0, 3, 1, 4)
            q, k, v = (qkv[0], qkv[1], qkv[2])
            attn = jnp.einsum('whnd,whmd->whnm', q, k) * hd ** (-0.5)
            bias = bias_tab[REL_IDX].reshape(N, N, HEADS).transpose(2, 0, 1)
            attn = attn + bias[None]
            attn = attn.reshape(Bn, NW, HEADS, N, N) + mask[None, :, None]
            attn = jax.nn.softmax(attn.reshape(-1, HEADS, N, N), axis=-1)
            out = jnp.einsum('whnm,whmd->whnd', attn, v).transpose(0, 2, 1, 3).reshape(-1, N, Cc)
            out = out @ proj_w + proj_b
            out = out.reshape(Bn, Hh // WS, Ww // WS, WS, WS, Cc)
            out = out.transpose(0, 1, 3, 2, 4, 5).reshape(Bn, Hh, Ww, Cc)
            if shift:
                out = jnp.roll(out, (shift, shift), axis=(1, 2))
            x = x + out
            z = layer_norm(x, ln2_g, ln2_b)
            z = jax.nn.gelu(z @ fc1_w + fc1_b, approximate=False)
            return x + (z @ fc2_w + fc2_b)
        x = swin_block_fn(x, 0, MASK0, ln1_g0, ln1_b0, qkv_w0, qkv_b0, bias_tab0, proj_w0, proj_b0, ln2_g0, ln2_b0, fc1_w0, fc1_b0, fc2_w0, fc2_b0)
        x = swin_block_fn(x, SHIFT, MASK1, ln1_g1, ln1_b1, qkv_w1, qkv_b1, bias_tab1, proj_w1, proj_b1, ln2_g1, ln2_b1, fc1_w1, fc1_b1, fc2_w1, fc2_b1)
        return x

    def _L1_conv_ref(x, gamma, beta):
        import jax, jax.numpy as jnp
        import numpy as np
        EPS = 1e-05
        M_PER_GROUP = 16
        ITER_NUM = 5

        def _iter_norm_whiten(x, gamma, beta):
            B, H, W, C = x.shape
            g = C // M_PER_GROUP
            m = M_PER_GROUP
            N = B * H * W
            xt = jnp.transpose(x, (3, 0, 1, 2)).reshape(C, N)
            mu = jnp.mean(xt, axis=1, keepdims=True)
            f = xt - mu
            fg = f.reshape(g, m, N)
            cov = jnp.einsum('gmn,gkn->gmk', fg, fg) / (jnp.float32(N) - 1.0)
            eye = jnp.eye(m, dtype=x.dtype)
            cov = (1.0 - EPS) * cov + EPS * eye
            trace = jnp.trace(cov, axis1=1, axis2=2)[:, None, None]
            sigma = cov / trace
            P = jnp.broadcast_to(eye, (g, m, m))
            for _ in range(ITER_NUM):
                P = (3.0 * P - P @ P @ P @ sigma) / 2.0
            wm = P / jnp.sqrt(trace)
            f_hat = jnp.einsum('gmk,gkn->gmn', wm, fg).reshape(C, B, H, W)
            out = jnp.transpose(f_hat, (1, 2, 3, 0))
            return gamma * out + beta
        return _iter_norm_whiten(x, gamma, beta)

    def _gn(v, G=32, eps=1e-05):
        B_, H_, W_, C_ = v.shape
        g = v.reshape(B_, H_, W_, G, C_ // G)
        m = jnp.mean(g, axis=(1, 2, 4), keepdims=True)
        s = jnp.var(g, axis=(1, 2, 4), keepdims=True)
        return ((g - m) / jnp.sqrt(s + eps)).reshape(v.shape)

    def _ln_c(v, eps=1e-06):
        m = jnp.mean(v, axis=-1, keepdims=True)
        s = jnp.var(v, axis=-1, keepdims=True)
        return (v - m) / jnp.sqrt(s + eps)

    def _ln_t(v, eps=1e-05):
        m = jnp.mean(v, axis=-1, keepdims=True)
        s = jnp.var(v, axis=-1, keepdims=True)
        return (v - m) / jnp.sqrt(s + eps)

    def _to_tokens(v):
        B_, H_, W_, C_ = v.shape
        return v.reshape(B_, H_ * W_, C_)

    def _from_tokens(t, like):
        return t.reshape(like.shape)
    x = _L0_conv_ref(x, L0_conv_ln1_g0, L0_conv_ln1_b0, L0_conv_qkv_w0, L0_conv_qkv_b0, L0_conv_bias_tab0, L0_conv_proj_w0, L0_conv_proj_b0, L0_conv_ln2_g0, L0_conv_ln2_b0, L0_conv_fc1_w0, L0_conv_fc1_b0, L0_conv_fc2_w0, L0_conv_fc2_b0, L0_conv_ln1_g1, L0_conv_ln1_b1, L0_conv_qkv_w1, L0_conv_qkv_b1, L0_conv_bias_tab1, L0_conv_proj_w1, L0_conv_proj_b1, L0_conv_ln2_g1, L0_conv_ln2_b1, L0_conv_fc1_w1, L0_conv_fc1_b1, L0_conv_fc2_w1, L0_conv_fc2_b1)
    x = _L1_conv_ref(x, L1_conv_gamma, L1_conv_beta)
    return x

_drawn_inputs = setup_inputs


def setup_inputs(seed=0):
    import zlib

    import numpy as np

    out = dict(_drawn_inputs(seed))
    spreads = {'L0_conv_ln1_g0': (1.0, 0.6),
     'L0_conv_ln1_b0': (0.0, 0.8),
     'L0_conv_qkv_b0': (0.0, 0.8),
     'L0_conv_proj_b0': (0.0, 0.8),
     'L0_conv_ln2_g0': (1.0, 0.6),
     'L0_conv_ln2_b0': (0.0, 2.0),
     'L0_conv_fc1_b0': (0.0, 0.8),
     'L0_conv_fc2_b0': (0.0, 0.8),
     'L0_conv_ln1_g1': (1.0, 0.6),
     'L0_conv_ln1_b1': (0.0, 0.8),
     'L0_conv_qkv_b1': (0.0, 0.8),
     'L0_conv_proj_b1': (0.0, 2.0),
     'L0_conv_ln2_g1': (1.0, 0.6),
     'L0_conv_ln2_b1': (0.0, 2.0),
     'L0_conv_fc1_b1': (0.0, 2.0),
     'L0_conv_fc2_b1': (0.0, 2.0),
     'L1_conv_gamma': (1.0, 0.2),
     'L1_conv_beta': (0.0, 0.1)}
    factors = {'L0_conv_qkv_w0': 8.0,
     'L0_conv_bias_tab0': 8.0,
     'L0_conv_proj_w0': 8.0,
     'L0_conv_qkv_w1': 8.0,
     'L0_conv_bias_tab1': 8.0,
     'L0_conv_proj_w1': 8.0,
     'L0_conv_fc1_w1': 6.021,
     'L0_conv_fc2_w1': 5.76}
    for name, (base, spread) in spreads.items():
        noise = np.random.default_rng([zlib.crc32(name.encode()), seed]).standard_normal(out[name].shape)
        drawn = base * np.exp(spread * noise) if base else spread * noise
        out[name] = jnp.asarray(drawn.astype(out[name].dtype))
    for name, factor in factors.items():
        out[name] = (out[name] * factor).astype(out[name].dtype)
    return out
```

```python
import concourse.bass as bass
from concourse import mybir
from contextlib import ExitStack

F32 = mybir.dt.float32
F32R = mybir.dt.float32r
I32 = mybir.dt.int32
ACT = mybir.ActivationFunctionType
ALU = mybir.AluOpType
AX = mybir.AxisListType

IMAGES, SIDE, CH, HEADS, WS, SHIFT = 16, 28, 64, 8, 7, 3
HD = CH // HEADS
NTOK = WS * WS
WROW = SIDE // WS
PAIRS = IMAGES // 2
HALVES = 2 * PAIRS
WIN = 2 * WROW
TOK = WIN * NTOK
IMG_TOK = SIDE * SIDE
KROWS = 64 + NTOK
NROWS = 2 * NTOK
TA, TB = 4 * SIDE, 3 * SIDE
TILE = 4 * SIDE
TILES = IMG_TOK // TILE
LN_EPS = 1.001e-05
WH_EPS = 1e-05
WH_ITER = 5
GROUP = 16
MAGIC = float(0x5F3759DF)
NLINK = 11

PARAMS = ['ln1_g', 'ln1_b', 'qkv_w', 'qkv_b', 'bias_tab', 'proj_w', 'proj_b', 'ln2_g', 'ln2_b',
          'fc1_w', 'fc1_b', 'fc2_w', 'fc2_b']


def build(nc, x, par, gamma, beta, con, out):
    ctx = ExitStack()
    with ctx:
        def sb(name, shape, dt=F32):
            return ctx.enter_context(nc.sbuf_tensor(name, shape, dt))

        def sem(name):
            return ctx.enter_context(nc.semaphore(name))

        XW = [sb("XW0", [128, HALVES * TOK]), sb("XW1", [128, HALVES * TOK])]
        qexpb = sb("qexp", [128, 2, WIN, HEADS, NTOK])
        qexp = [qexpb[:, i] for i in range(2)]
        XA = XW[1][0:TA, 0:PAIRS * WROW * 128].rearrange("p (b i k) -> p b i k", b=PAIRS, i=WROW)
        XB = qexpb[0:TB].rearrange("p a w h n -> p (a w h n)")[:, 0:PAIRS * WROW * 128]\
            .rearrange("p (b i k) -> p b i k", b=PAIRS, i=WROW)
        XR = XW[0]
        centre = sb("centre", [128, 128])
        avg64 = sb("avg64", [128, 128])
        ident = sb("ident", [128, 128])
        ident_r = sb("ident_r", [128, 128], F32R)
        fold = sb("fold", [NROWS, 50])
        fold_r = sb("fold_r", [NROWS, 50], F32R)
        wmask = sb("wmask", [NROWS, 2])
        hmask = sb("hmask", [128, HEADS])
        hmask2 = sb("hmask2", [128, HEADS])
        hidb = sb("hid", [128, 4, TOK])
        hid = [hidb[:, i] for i in range(4)]
        sel_f = hidb[:].rearrange("p a b -> p (a b)")[:, 0:WIN * 128]
        sel_r = sb("sel_r", [128, WIN, 128], F32R)
        dsel = sb("dsel", [128, 128])
        maskn = sb("maskn", [NROWS, 4, NTOK])
        maskt = sb("maskt", [KROWS, 4, NTOK])
        dup = sb("dup", [128, 128])
        gsum = sb("gsum", [128, 128])
        P = []
        for k in range(2):
            P.append(dict(
                wq=sb(f"wq{k}", [128, 128]), wk=sb(f"wk{k}", [128, 128]), wv=sb(f"wv{k}", [128, 128]),
                wv2=sb(f"wv2{k}", [128, CH]), wp=sb(f"wp{k}", [128, 128]),
                wph=[sb(f"wph{k}{i}", [128, 128]) for i in range(2)],
                f1=sb(f"f1{k}", [128, 4, 128]), f2=sb(f"f2{k}", [128, 4, 128]),
                vec=sb(f"vec{k}", [128, 16]),
                bn=sb(f"bn{k}", [NROWS, 4 if k else 1, HEADS * NTOK], F32R),
                bh=sb(f"bh{k}", [KROWS, 4 if k else 1, HEADS * NTOK], F32R),
                bl=sb(f"bl{k}", [KROWS, 4 if k else 1, HEADS * NTOK], F32R)))
        G1, B1, G2, B2, QB, KB, VB, PB, F2B, FB = 0, 1, 2, 3, 4, 5, 6, 7, 8, 9
        turn = sb("turn", [NROWS, KROWS])
        sq = sb("sq", [128, TOK])
        lv = sb("lv", [128, TOK])
        ly = sb("ly", [128, TOK])
        lt = sb("lt", [128, TOK])
        z = sb("z", [128, TOK])
        qbd = sb("qbd", [128, WIN, NROWS], F32R)
        kexp = sb("kexp", [128, WIN, HEADS, NTOK], F32R)
        qsb = sb("qsb", [128, TOK])
        ksb = sb("ksb", [128, TOK])
        kbd = [sb(f"kbd{i}", [128, WIN, KROWS]) for i in range(2)]
        vbd = [sb(f"vbd{i}", [KROWS, WIN * HEADS, 32]) for i in range(2)]
        nmax = sb("nmax", [NROWS, WIN, HEADS])
        nmaxw = sb("nmaxw", [NROWS, WIN, 2, HEADS], F32R)
        rx = sb("rx", [128, HEADS, NTOK], F32R)
        pt = [sb(f"pt{i}", [KROWS, HEADS * NTOK]) for i in range(4)]
        osb = [sb(f"osb{i}", [128, 4 * NROWS]) for i in range(2)]
        rec = [sb(f"rec{i}", [128, 4 * NROWS]) for i in range(2)]
        att = sb("att", [128, WIN, NROWS])
        rawn = [osb[k][0:NROWS, :] for k in range(2)]
        rawt = [rec[k][0:KROWS, :] for k in range(2)]
        btmp = qsb[0:KROWS, :]
        tsb = [sb(f"tsb{i}", [TILE, 132]) for i in range(2)]
        wcol = sb("wcol", [128, 8])
        SUM0, SHIFTC, NMEAN, DIAG, TRACE, RTRACE, RSQ, EXPO = range(8)
        wrow = sb("wrow", [1, 256])
        fold2 = sb("fold2", [128, CH + 1])
        mom = sb("mom", [128, CH + 1])
        momc = sb("momc", [128, CH])
        cov = sb("cov", [128, 128])
        wtmp = sb("wtmp", [128, 128])
        psig = sb("psig", [128, 2, 128])
        prod = sb("prod", [128, 2, 128])
        wfin = sb("wfin", [128, 128])
        nmb = sb("nmb", [128, TILE])
        ones1 = sb("ones1", [1, TILE])
        gam = sb("gam", [128, CH])
        bet = sb("bet", [1, 128])
        biasb = sb("biasb", [TILE, 128])
        outs = [XW[1][0:TILE, b * TILES * 128:(b + 1) * TILES * 128].rearrange("p (t k) -> p t k", k=128)
                for b in range(PAIRS - 1)]
        outs.append(qexpb[0:TILE].rearrange("p a w h n -> p (a w h n)")[:, 0:TILES * 128]
                    .rearrange("p (t k) -> p t k", k=128))

        PS = [ctx.enter_context(nc.psum_tensor(f"PS{i}", [128, 512], F32)) for i in range(8)]
        bS, bST, bO, bG = PS[0], PS[1:3], PS[3:5], PS[5:8]

        s_con, s_par, s_bias = sem("s_con"), sem("s_par"), sem("s_bias")
        s_xin = [sem(f"s_xin{b}") for b in range(PAIRS)]
        s_zero = sem("s_zero")
        s_zero_q = sem("s_zero_q")
        s_round = sem("s_round")
        s_tp, s_tpcp = sem("s_tp"), sem("s_tpcp")
        s_fold, s_prep = sem("s_fold"), sem("s_prep")
        s_btab, tab_link = sem("s_btab"), sem("tab_link")
        s_turn = sem("s_turn")
        z_done, w_link = sem("z_done"), sem("w_link")
        mz_done = sem("mz_done")
        xc_ready, sq_done, var_ready, var_used, ln_link = (
            sem("xc_ready"), sem("sq_done"), sem("var_ready"), sem("var_used"), sem("ln_link"))
        q_ready, k_ready, v_ready, s_ready, mxt_ready, st_ready, av_ready, den_ready, proj_ready = (
            sem("q_ready"), sem("k_ready"), sem("v_ready"), sem("s_ready"), sem("mxt_ready"), sem("st_ready"),
            sem("av_ready"), sem("den_ready"), sem("proj_ready"))
        q_done, k_done, v_done, exp_done, osb_done = (
            sem("q_done"), sem("k_done"), sem("v_done"), sem("exp_done"), sem("osb_done"))
        kexp_done, max_done, nmaxw_done, rx_done, rec_done, res_done = (
            sem("kexp_done"), sem("max_done"), sem("nmaxw_done"), sem("rx_done"), sem("rec_done"), sem("res_done"))
        qexp_done, att_done = sem("qexp_done"), sem("att_done")
        mxc, msq, mvar, mvar_used, mlink = sem("mxc"), sem("msq"), sem("mvar"), sem("mvar_used"), sem("mlink")
        fc1_ready, gelu_done, fc2_ready, mres_done = (
            sem("fc1_ready"), sem("gelu_done"), sem("fc2_ready"), sem("mres_done"))
        relay_done = sem("relay_done")
        tt_ready, tt_done, cov_ready = sem("tt_ready"), sem("tt_done"), sem("cov_ready")
        w_pe, w_dve, w_pool = sem("w_pe"), sem("w_dve"), sem("w_pool")
        o_ready, o_done, s_out = sem("o_ready"), sem("o_done"), sem("s_out")

        def win_kind(blk, half_odd, win):
            if blk == 0:
                return 0
            return (1 if win % WROW == WROW - 1 else 0) + (2 if half_odd and win >= WROW else 0)

        def xcols(blk, g):
            return XW[blk][:, bass.ds(g * TOK, TOK)]

        NPREP = 6
        NCON, NPAR = 14, 2 * 2 * 28 + 4
        WSTEP = {n: i + 1 for i, n in enumerate(
            ["sum0", "shift", "fold2", "mom", "rows", "diag", "trace", "psig"]
            + [f"prod{i}" if j == 0 else f"p{i}" for i in range(WH_ITER) for j in range(2)]
            + ["wfin", "biasb"])}
        PSTEP = {n: i + 1 for i, n in enumerate(
            ["shift", "mom", "row", "outer", "trace"]
            + [f"prod{i}" if j == 0 else f"p{i}" for i in range(WH_ITER) for j in range(2)] + ["bias"])}
        block = ctx.enter_context(nc.Block())

        @block.sync
        def _(sp):
            for t, src in ((centre, "centre"), (avg64, "avg64"), (ident, "ident"), (fold, "fold"), (wmask, "wmask"),
                           (hmask, "hmask"), (hmask2, "hmask2"), (sel_f, "sel"), (dsel, "dsel"),
                           (maskn, "maskn"), (maskt, "maskt"), (dup, "dup"), (gsum, "gsum"), (turn, "turn")):
                sp.dma_start(t[:] if len(t.shape) == 2 else t[:].rearrange("p a b -> p (a b)"), con[src])\
                    .then_inc(s_con, 16)
            for b in range(PAIRS):
                for w in range(2):
                    img = x[b + PAIRS * w].rearrange("r q c -> (r q) c").rearrange("(i t) c -> t i c", i=WROW)
                    sp.dma_start(XA[:, b, :, CH * w:CH * w + CH], img[0:TA]).then_inc(s_xin[b], 16)
                    sp.dma_start(XB[:, b, :, CH * w:CH * w + CH], img[TA:TA + TB]).then_inc(s_xin[b], 16)
            for b in range(PAIRS):
                sp.wait_ge(o_done, 2 * (b + 1))
                for w in range(2):
                    dst = out[b + PAIRS * w].rearrange("r q c -> (r q) c").rearrange("(t p) c -> p t c", p=TILE)
                    sp.dma_start(dst, outs[b][:, :, CH * w:CH * w + CH]).then_inc(s_out, 16)
            sp.wait_ge(s_out, 16 * 2 * PAIRS)

        def pool_relay(pool, blk, b):
            src = XW[blk][:, bass.ds(b * 2 * TOK, 2 * TOK)].rearrange("p (i j r c) -> p i j r c", i=WROW, j=WROW, r=WS)
            if blk == 0:
                dst = XW[1][:, bass.ds(b * 2 * TOK, 2 * TOK)].rearrange("p (i j r c) -> p i j r c", i=WROW, j=WROW, r=WS)
                far = WS - SHIFT
                last = None
                for i in range(WROW):
                    for ro, rn, ri, si in ((0, far, SHIFT, i), (far, SHIFT, 0, (i + 1) % WROW)):
                        for jo, jn, co, cn, ji, ci in ((0, WROW, 0, far, 0, SHIFT),
                                                       (0, WROW - 1, far, SHIFT, 1, 0),
                                                       (WROW - 1, 1, far, SHIFT, 0, 0)):
                            last = nc.gpsimd.tensor_copy(
                                dst[:, i, jo:jo + jn, ro:ro + rn, co:co + cn],
                                src[:, si, ji:ji + jn, ri:ri + rn, ci:ci + cn])
                last.then_inc(relay_done, 1)
            else:
                dst = XR[:, bass.ds(b * 2 * TOK, 2 * TOK)].rearrange("p (y q) -> p y q", q=SIDE)
                last = None
                for i in range(WROW):
                    rows = ((0, WS, WS * i + SHIFT),) if i < WROW - 1 else \
                        ((0, WS - SHIFT, WS * i + SHIFT), (WS - SHIFT, SHIFT, 0))
                    for r0, rn, y0 in rows:
                        for j in range(WROW):
                            cols = ((0, WS, WS * j + SHIFT),) if j < WROW - 1 else \
                                ((0, WS - SHIFT, WS * j + SHIFT), (WS - SHIFT, SHIFT, 0))
                            for c0, cn, q0 in cols:
                                last = nc.gpsimd.tensor_tensor(
                                    dst[:, y0:y0 + rn, q0:q0 + cn], src[:, i, j, r0:r0 + rn, c0:c0 + cn],
                                    wcol[:, SHIFTC:SHIFTC + 1].rearrange("p (a b) -> p a b", a=1)
                                    .to_broadcast([128, rn, cn]), ALU.subtract)
                last.then_inc(relay_done, 1)

        @block.gpsimd
        def _(pool):
            for i in range(2):
                nc.gpsimd.memset(kbd[i][:, :, :], 0.0)
                nc.gpsimd.memset(vbd[i][:, :, :], 0.0)
            nc.gpsimd.memset(ones1[:, :], 1.0)
            for i in range(2):
                nc.gpsimd.memset(tsb[i][:, 128:129], 1.0)
            for k in range(2):
                for name in ("wq", "wk", "wv", "wp"):
                    nc.gpsimd.memset(P[k][name][:, :], 0.0)
                for i in range(2):
                    nc.gpsimd.memset(P[k]["wph"][i][:, :], 0.0)
                for name in ("f1", "f2"):
                    nc.gpsimd.memset(P[k][name][:, :, :], 0.0)
            nc.gpsimd.memset(wcol[:, EXPO:EXPO + 1], -0.5).then_inc(s_zero, 1)
            pool.wait_ge(s_zero, 1)
            for i in range(2):
                for w in range(2):
                    last = nc.gpsimd.memset(vbd[i][64 * w:64 * w + NTOK, :, 16 + w:17 + w], 1.0)
            last.then_inc(s_zero, 1)

            def qexpand(g1, buf):
                pool.wait_ge(q_done, 3 * g1 + 3)
                for w in range(WIN):
                    nc.gpsimd.tensor_tensor(
                        qexp[buf][:, w, :, :],
                        qsb[:, w * NTOK:(w + 1) * NTOK].rearrange("p (a n) -> p a n", a=1).to_broadcast([128, HEADS, NTOK]),
                        hmask[:, :].rearrange("p (h a) -> p h a", a=1).to_broadcast([128, HEADS, NTOK]),
                        ALU.mult).then_inc(qexp_done, 1)

            def attn(g, part):
                pool.wait_ge(rec_done, 2 * g + part + 1)
                if part == 0:
                    pool.wait_ge(proj_ready, g)
                nc.gpsimd.tensor_tensor(
                    att[:, 4 * part:4 * part + 4, :], osb[part][:, :].rearrange("p (a n) -> p a n", a=4),
                    rec[part][:, :].rearrange("p (a n) -> p a n", a=4), ALU.mult).then_inc(att_done, 1)

            def step(base, g, u, first, more):
                if not first:
                    attn(base + g - 1, 1)
                if more:
                    if not first:
                        pool.wait_ge(st_ready, WIN * (base + g))
                    qexpand(base + g + 1, (u + 1) % 2)
                attn(base + g, 0)

            pool.wait_ge(s_con, 16 * NCON)
            for blk in range(2):
                base = HALVES * blk
                if blk:
                    pool.wait_ge(st_ready, WIN * base)
                qexpand(base, 0)
                step(base, 0, 0, True, True)
                step(base, 1, 1, False, True)
                with pool.Fori(1, PAIRS - 1) as it:
                    for u in range(2):
                        step(base, it * 2 + u, u, False, True)
                step(base, HALVES - 2, 0, False, True)
                step(base, HALVES - 1, 1, False, False)
                attn(base + HALVES - 1, 1)
                if blk:
                    pool.wait_ge(w_dve, WSTEP["shift"])
                with pool.Fori(0, PAIRS) as it:
                    pool.wait_ge(mres_done, (it + 1) * 2 + base)
                    pool_relay(pool, blk, it)
            pool.wait_ge(w_dve, WSTEP["trace"])
            nc.gpsimd.tensor_tensor(wcol[:, RSQ:RSQ + 1], wcol[:, TRACE:TRACE + 1], wcol[:, EXPO:EXPO + 1], ALU.pow)\
                .then_inc(w_pool, 1)

        @block.scalar
        def _(act):
            for k in range(2):
                for w in range(2):
                    for a in range(WS):
                        act.dma_start(rawn[k][NTOK * w + WS * a:NTOK * w + WS * a + WS, :].rearrange("p (m s) -> p m s", m=WS),
                                      bass.AP(par[k]["bias_tab"].tensor, a * 13 * HEADS,
                                              [[HEADS, WS], [13 * HEADS, WS], [1, WS * HEADS]])).then_inc(s_bias, 16)
            act.wait_ge(s_zero, 1)
            for k in range(2):
                q = par[k]
                p = P[k]
                w_qkv = q["qkv_w"]

                def load(dst, src):
                    act.dma_start(dst, src).then_inc(s_par, 16)

                for w in range(2):
                    r = slice(CH * w, CH * w + CH)
                    load(p["wq"][r, r], w_qkv[:, 0:CH])
                    load(p["wk"][r, r], w_qkv[:, CH:2 * CH])
                    load(p["wv"][r, r], w_qkv[:, 2 * CH:3 * CH])
                    load(p["wv2"][r, :], w_qkv[:, 2 * CH:3 * CH])
                    load(p["wp"][r, r], q["proj_w"])
                    load(p["f1"][r, :, r], q["fc1_w"].rearrange("c (k j) -> c k j", j=CH))
                    load(p["f2"][r, :, r], q["fc2_w"].rearrange("(k j) c -> j k c", j=CH))
                    for hh in range(2):
                        for h4 in range(4):
                            ch = HD * (4 * hh + h4)
                            load(p["wph"][hh][32 * h4 + HD * w:32 * h4 + HD * w + HD, r], q["proj_w"][ch:ch + HD, :])
                    for col, name, lo in ((G1, "ln1_g", 0), (B1, "ln1_b", 0), (G2, "ln2_g", 0), (B2, "ln2_b", 0),
                                          (QB, "qkv_b", 0), (KB, "qkv_b", CH), (VB, "qkv_b", 2 * CH),
                                          (PB, "proj_b", 0), (F2B, "fc2_b", 0), (FB, "fc1_b", 0),
                                          (FB + 1, "fc1_b", CH), (FB + 2, "fc1_b", 2 * CH), (FB + 3, "fc1_b", 3 * CH)):
                        load(p["vec"][r, col:col + 1], q[name][lo:lo + CH].rearrange("(c a) -> c a", a=1))
            for w in range(2):
                act.dma_start(gam[CH * w:CH * w + CH, :], gamma.rearrange("a b c k -> (a b c) k").to_broadcast([CH, CH]))\
                    .then_inc(s_par, 16)
                act.dma_start(bet[:, CH * w:CH * w + CH], beta.rearrange("a b c k -> (a b c) k")).then_inc(s_par, 16)

            for b in range(PAIRS):
                for i in range(WROW):
                    n = b * WROW + i
                    act.wait_ge(s_tp, n + 1)
                    src = PS[n % 4][:, 0:WS * SIDE].rearrange("p (r j c) -> p r j c", r=WS, j=WROW)
                    dst = XW[0][:, n * WS * SIDE:(n + 1) * WS * SIDE].rearrange("p (j r c) -> p r j c", j=WROW, r=WS)
                    nc.scalar.activation(dst, src, ACT.Copy).then_inc(s_tpcp, 1)

            def square(g):
                act.wait_ge(xc_ready, g + 1)
                act.wait_ge(var_ready, g)
                nc.scalar.activation(sq[:, :], bG[2][:, 0:TOK], ACT.Square).then_inc(sq_done, 1)

            def evac_q(p, g1):
                act.wait_ge(q_ready, g1 + 1)
                act.wait_ge(qexp_done, WIN * g1)
                act.wait_ge(s_ready, WIN * g1)
                for w in range(2):
                    r = slice(64 * w, 64 * w + 64)
                    nc.scalar.activation(qbd[r, :, NTOK * w:NTOK * w + NTOK],
                                         bG[1][r, 0:TOK].rearrange("p (a n) -> p a n", n=NTOK),
                                         ACT.Identity, bias=p["vec"][r, QB:QB + 1]).then_inc(q_done, 1)
                nc.scalar.activation(qsb[:, :], bG[1][:, 0:TOK], ACT.Identity, bias=p["vec"][:, QB:QB + 1])\
                    .then_inc(q_done, 1)

            def evac_k(p, g1, buf, prologue=False):
                act.wait_ge(k_ready, g1 + 1)
                if not prologue:
                    act.wait_ge(st_ready, WIN * (g1 - 1))
                act.wait_ge(kexp_done, WIN * g1)
                nc.scalar.activation(ksb[:, :], bG[2][:, 0:TOK], ACT.Identity, bias=p["vec"][:, KB:KB + 1])\
                    .then_inc(k_done, 1)
                for w in range(2):
                    r = slice(64 * w, 64 * w + 64)
                    nc.scalar.activation(kbd[buf][r, :, 64 * w:64 * w + NTOK],
                                         bG[2][r, 0:TOK].rearrange("p (a n) -> p a n", n=NTOK),
                                         ACT.Identity, bias=p["vec"][r, KB:KB + 1]).then_inc(k_done, 1)

            def evac_v(g1, buf, prologue=False):
                act.wait_ge(v_ready, g1 + 1)
                if not prologue:
                    act.wait_ge(av_ready, WIN * (g1 - 1))
                for w in range(2):
                    nc.scalar.activation(vbd[buf][64 * w:64 * w + NTOK, :, HD * w:HD * w + HD],
                                         bG[1][64 * w:64 * w + NTOK, :].rearrange("p (a d) -> p a d", d=HD),
                                         ACT.Copy).then_inc(v_done, 1)

            def expo(g, w, first=False):
                act.wait_ge(st_ready, WIN * g + w + 1)
                if not (first and w < 4):
                    act.wait_ge(av_ready, WIN * g + w - 3)
                nc.scalar.activation(pt[w % 4][:, :], bST[w % 2][0:KROWS, 0:HEADS * NTOK], ACT.Exp)\
                    .then_inc(exp_done, 1)

            def o_copy(g, part, first=False):
                act.wait_ge(av_ready, WIN * g + 4 * part + 4)
                if not first:
                    act.wait_ge(att_done, 2 * (g - 1) + part + 1)
                nc.scalar.activation(osb[part][:, :], bO[part][:, 0:4 * NROWS], ACT.Copy).then_inc(osb_done, 1)

            def step(p, base, g, u, first, more, more2):
                G = base + g
                nb = (u + 1) % 2
                f = first and base == 0
                expo(G, 0, f)
                if more:
                    evac_q(p, G + 1)
                expo(G, 1, f)
                if more:
                    evac_k(p, G + 1, nb)
                expo(G, 2, f)
                expo(G, 3, f)
                if more:
                    evac_v(G + 1, nb)
                expo(G, 4)
                o_copy(G, 0, f)
                if more2:
                    square(G + 2)
                expo(G, 5)
                expo(G, 6)
                expo(G, 7)
                o_copy(G, 1, f)

            act.wait_ge(s_prep, NPREP)
            act.wait_ge(s_zero, 2)
            act.wait_ge(s_zero_q, 1)
            for blk in range(2):
                base = HALVES * blk
                p = P[blk]
                if blk:
                    act.wait_ge(relay_done, PAIRS)
                square(base)
                evac_q(p, base)
                evac_k(p, base, 0, True)
                evac_v(base, 0, True)
                square(base + 1)
                step(p, base, 0, 0, True, True, True)
                step(p, base, 1, 1, False, True, True)
                with act.Fori(1, PAIRS - 1) as it:
                    for u in range(2):
                        step(p, base, it * 2 + u, u, False, True, True)
                step(p, base, HALVES - 2, 0, False, True, False)
                step(p, base, HALVES - 1, 1, False, False, False)

                def msquare(g):
                    act.wait_ge(mxc, g + 1)
                    act.wait_ge(mvar, g)
                    nc.scalar.activation(sq[:, :], PS[0][:, 0:TOK], ACT.Square).then_inc(msq, 1)

                def gelus(g, m):
                    for c in (2 * m, 2 * m + 1):
                        act.wait_ge(fc1_ready, 4 * g + c + 1)
                        act.wait_ge(fc2_ready, g)
                        nc.scalar.activation(hid[c], PS[2 + c % 2][:, 0:TOK], ACT.Gelu,
                                             bias=p["vec"][:, FB + c:FB + c + 1]).then_inc(gelu_done, 1)

                msquare(base)
                with act.Fori(0, PAIRS - 1) as it:
                    for u in range(2):
                        g = base + it * 2 + u
                        gelus(g, 0)
                        msquare(g + 1)
                        gelus(g, 1)
                gelus(base + HALVES - 2, 0)
                msquare(base + HALVES - 1)
                gelus(base + HALVES - 2, 1)
                gelus(base + HALVES - 1, 0)
                gelus(base + HALVES - 1, 1)
            for n in range(PAIRS * TILES):
                act.wait_ge(tt_ready, n + 1)
                if n >= 2:
                    act.wait_ge(cov_ready, n - 1)
                nc.scalar.activation(tsb[n % 2][:, 0:128], PS[5 + n % 2][0:TILE, 0:128], ACT.Copy).then_inc(tt_done, 1)

        @block.vector
        def _(dve):
            nc.vector.memset(qbd[:, :, :].bitcast(F32), 0.0).then_inc(s_zero_q, 1)
            dve.wait_ge(s_con, 16 * NCON)
            nc.vector.tensor_copy(ident_r[:, :], ident[:, :])
            nc.vector.tensor_copy(fold_r[:, :], fold[:, :])
            nc.vector.tensor_copy(sel_r[:, :, :].rearrange("p a b -> p (a b)"), sel_f[:, :]).then_inc(s_round, 1)

            def chain(semaphore):
                count = [0]

                def link(ins):
                    count[0] += 1
                    ins.then_inc(semaphore, 1)
                    dve.wait_ge(semaphore, count[0])
                return link

            plink = chain(s_prep)
            for k in range(2):
                p = P[k]
                v = p["vec"]
                dve.wait_ge(s_fold, 2 * k + 1)
                ps = PS[4 + 2 * k]
                plink(nc.vector.tensor_tensor(v[:, VB:VB + 1], ps[:, 2:3], v[:, VB:VB + 1], ALU.add))
                nc.vector.tensor_tensor(v[:, KB:KB + 1], ps[:, 1:2], v[:, KB:KB + 1], ALU.add)
                nc.vector.tensor_tensor(v[:, FB:FB + 4], ps[:, 3:7], v[:, FB:FB + 4], ALU.add)
                plink(nc.vector.tensor_tensor(v[:, QB:QB + 1], ps[:, 0:1], v[:, QB:QB + 1], ALU.add))
                nc.vector.tensor_scalar(v[:, QB:QB + 1], v[:, QB:QB + 1], HD ** -0.5, None, ALU.mult)
                nc.vector.tensor_scalar(p["wq"][:, :], p["wq"][:, :], v[:, G1:G1 + 1], HD ** -0.5, ALU.mult, ALU.mult)
                nc.vector.tensor_scalar(p["wk"][:, :], p["wk"][:, :], v[:, G1:G1 + 1], None, ALU.mult)
                nc.vector.tensor_scalar(p["wv2"][:, :], p["wv2"][:, :], v[:, G1:G1 + 1], None, ALU.mult)
                nc.vector.tensor_scalar(p["f1"][:, :, :], p["f1"][:, :, :], v[:, G2:G2 + 1], None, ALU.mult)
                dve.wait_ge(s_fold, 2 * k + 2)
                plink(nc.vector.tensor_tensor(v[:, PB:PB + 1], PS[5 + 2 * k][:, 0:1], v[:, PB:PB + 1], ALU.add))

            tlink = chain(tab_link)

            def tables(k):
                p = P[k]
                if k == 0:
                    dve.wait_ge(s_bias, 16 * 28)
                    for i in range(2):
                        dve.wait_ge(s_turn, i + 1)
                        last = nc.vector.tensor_copy(rawt[i][:, :], PS[i][0:KROWS, 0:HEADS * NTOK])
                    tlink(last)
                for t in range(4 if k else 1):
                    tlink(nc.vector.tensor_copy(
                        btmp[0:NROWS, :].rearrange("p (h m) -> p h m", h=HEADS),
                        rawn[k][:, :].rearrange("p (m h) -> p h m", h=HEADS)[:, :, ::-1]))
                    tlink(nc.vector.tensor_tensor(
                        p["bn"][:, t, :].rearrange("p (h m) -> p h m", h=HEADS),
                        btmp[0:NROWS, :].rearrange("p (h m) -> p h m", h=HEADS),
                        maskn[:, t:t + 1, :].to_broadcast([NROWS, HEADS, NTOK]), ALU.add))
                    tlink(nc.vector.tensor_tensor(
                        btmp[:, :].rearrange("p (h m) -> p h m", h=HEADS),
                        rawt[k][:, :].rearrange("p (m h) -> p h m", h=HEADS),
                        maskt[:, t:t + 1, :].to_broadcast([KROWS, HEADS, NTOK]), ALU.add))
                    tlink(nc.vector.tensor_copy(p["bh"][:, t, :], btmp[:, :]))
                    tlink(nc.vector.tensor_tensor(p["bl"][:, t, :], btmp[:, :], p["bh"][:, t, :].bitcast(F32), ALU.subtract))
                nc.vector.memset(lt[:, 0:1], 0.0).then_inc(s_btab, 1)

            tables(0)
            tables(1)

            def norm(g, xps, vps, ready, used, link, done, zfree, after=None):
                dve.wait_ge(ready, g + 1)
                nc.vector.tensor_scalar(lv[:, :], vps[:, 0:TOK], LN_EPS, None, ALU.add).then_inc(used, 1)
                dve.wait_ge(used, g + 1)
                n = [0]

                def ln(ins):
                    n[0] += 1
                    ins.then_inc(link, 1)
                    if after and n[0] in after:
                        after[n[0]]()
                    dve.wait_ge(link, NLINK * g + n[0])

                ln(nc.vector.tensor_scalar(lt[:, :].bitcast(I32), lv[:, :].bitcast(I32), 1, None, ALU.logical_shift_right))
                ln(nc.vector.tensor_scalar(ly[:, :].bitcast(I32), lt[:, :].bitcast(I32), -1.0, MAGIC, ALU.mult, ALU.add))
                for _ in range(3):
                    ln(nc.vector.tensor_tensor(lt[:, :], ly[:, :], ly[:, :], ALU.mult))
                    ln(nc.vector.scalar_tensor_tensor(lt[:, :], lt[:, :], -0.5, lv[:, :], ALU.mult, ALU.mult))
                    ln(nc.vector.scalar_tensor_tensor(ly[:, :], lt[:, :], 1.5, ly[:, :], ALU.add, ALU.mult))
                assert n[0] == NLINK
                zfree()
                nc.vector.tensor_tensor(z[:, :], xps[:, 0:TOK], ly[:, :], ALU.mult).then_inc(done, 1)

            def anorm(g, after=None):
                norm(g, bG[2], bG[0], var_ready, var_used, ln_link, z_done, lambda: dve.wait_ge(v_ready, g), after)

            def kexpand(g1, w):
                if w == 0:
                    dve.wait_ge(k_done, 3 * g1 + 1)
                    dve.wait_ge(s_ready, WIN * g1)
                nc.vector.tensor_tensor(
                    kexp[:, w, :, :],
                    ksb[:, w * NTOK:(w + 1) * NTOK].rearrange("p (a n) -> p a n", a=1).to_broadcast([128, HEADS, NTOK]),
                    hmask[:, :].rearrange("p (h a) -> p h a", a=1).to_broadcast([128, HEADS, NTOK]),
                    ALU.mult).then_inc(kexp_done, 1)

            def rowmax(g1, w):
                dve.wait_ge(s_ready, WIN * g1 + w + 1)
                nc.vector.tensor_reduce(nmax[:, w, :], bS[0:NROWS, 0:HEADS * NTOK].rearrange("p (h m) -> p h m", h=HEADS),
                                        AX.X, ALU.max, negate=True).then_inc(max_done, 1)

            def split_max(g1):
                dve.wait_ge(max_done, WIN * (g1 + 1))
                dve.wait_ge(mxt_ready, g1)
                for w in range(2):
                    nc.vector.tensor_scalar(nmaxw[:, :, w, :], nmax[:, :, :], wmask[:, w:w + 1], None, ALU.mult)\
                        .then_inc(nmaxw_done, 1)

            def spread_max(g1):
                dve.wait_ge(mxt_ready, g1 + 1)
                dve.wait_ge(st_ready, WIN * g1)
                nc.vector.tensor_tensor(
                    rx[:, :, :], bG[1][:, 0:NTOK].rearrange("p (a n) -> p a n", a=1).to_broadcast([128, HEADS, NTOK]),
                    hmask2[:, :].rearrange("p (h a) -> p h a", a=1).to_broadcast([128, HEADS, NTOK]),
                    ALU.mult).then_inc(rx_done, 1)

            def recip(g, part, first=False):
                dve.wait_ge(den_ready, 2 * g + part + 1)
                if not first:
                    dve.wait_ge(att_done, 2 * g + part - 1)
                nc.vector.reciprocal(rec[part][:, :], bG[1 - part][:, 0:4 * NROWS]).then_inc(rec_done, 1)

            def residual(p, blk, base, g):
                dve.wait_ge(proj_ready, base + g + 1)
                nc.vector.scalar_tensor_tensor(xcols(blk, g), bG[0][:, 0:TOK], p["vec"][:, PB:PB + 1], xcols(blk, g),
                                               ALU.add, ALU.add).then_inc(res_done, 1)

            def step(p, blk, base, g, u, first, more, more2, second=False):
                G = base + g
                if not first:
                    recip(G - 1, 1, second)
                if more:
                    for w in range(4):
                        kexpand(G + 1, w)
                if not first:
                    residual(p, blk, base, g - 1)
                if more:
                    for w in range(4, WIN):
                        kexpand(G + 1, w)
                    for w in range(4):
                        rowmax(G + 1, w)
                recip(G, 0, first and base == 0)
                if more:
                    for w in range(4, WIN):
                        rowmax(G + 1, w)
                    split_max(G + 1)
                if more2:
                    anorm(G + 2, {2: lambda: spread_max(G + 1)})
                elif more:
                    spread_max(G + 1)

            for blk in range(2):
                base = HALVES * blk
                p = P[blk]
                anorm(base)
                for w in range(WIN):
                    kexpand(base, w)
                for w in range(WIN):
                    rowmax(base, w)
                split_max(base)
                spread_max(base)
                anorm(base + 1)
                step(p, blk, base, 0, 0, True, True, True)
                step(p, blk, base, 1, 1, False, True, True, second=blk == 0)
                with dve.Fori(1, PAIRS - 1) as it:
                    for u in range(2):
                        step(p, blk, base, it * 2 + u, u, False, True, True)
                step(p, blk, base, HALVES - 2, 0, False, True, False)
                step(p, blk, base, HALVES - 1, 1, False, False, False)
                recip(base + HALVES - 1, 1)
                residual(p, blk, base, HALVES - 1)

                if blk:
                    dve.wait_ge(res_done, 2 * HALVES)
                    nc.vector.tensor_reduce(wcol[:, SUM0:SUM0 + 1], XW[1][:, 0:TOK], AX.X, ALU.add).then_inc(w_dve, 1)
                    dve.wait_ge(w_pe, PSTEP["shift"])
                    nc.vector.scalar_tensor_tensor(wcol[:, SHIFTC:SHIFTC + 1], PS[7][:, 0:1], 1.0 / (2 * TOK),
                                                   p["vec"][:, F2B:F2B + 1], ALU.mult, ALU.add).then_inc(w_dve, 1)

                def mnorm(g):
                    norm(g, PS[0], PS[1], mvar, mvar_used, mlink, mz_done, lambda: dve.wait_ge(fc1_ready, 4 * g))

                def mresidual(g):
                    dve.wait_ge(fc2_ready, base + g + 1)
                    nc.vector.scalar_tensor_tensor(xcols(blk, g), PS[4][:, 0:TOK], p["vec"][:, F2B:F2B + 1],
                                                   xcols(blk, g), ALU.add, ALU.add).then_inc(mres_done, 1)

                mnorm(base)
                with dve.Fori(0, PAIRS - 1) as it:
                    for u in range(2):
                        g = it * 2 + u
                        mnorm(base + g + 1)
                        mresidual(g)
                mnorm(base + HALVES - 1)
                mresidual(HALVES - 2)
                mresidual(HALVES - 1)

            def wdone(ins, name):
                ins.then_inc(w_dve, 1)
                done.append(name)
                assert WSTEP[name] == len(done)
                dve.wait_ge(w_dve, WSTEP[name])

            done = ["sum0", "shift"]
            N = float(IMAGES * IMG_TOK)
            dve.wait_ge(cov_ready, PAIRS * TILES)
            nc.vector.tensor_copy(fold2[0:64, 0:CH], PS[7][0:64, 0:64])
            nc.vector.tensor_copy(fold2[64:128, 0:CH], PS[7][64:128, 64:128])
            wdone(nc.vector.tensor_copy(fold2[:, CH:CH + 1], PS[7][:, 128:129]), "fold2")
            dve.wait_ge(w_pe, PSTEP["mom"])
            wdone(nc.vector.tensor_copy(mom[:, :], PS[0][:, 0:CH + 1]), "mom")
            dve.wait_ge(w_pe, PSTEP["row"])
            nc.vector.tensor_copy(wrow[:, 0:128], PS[1][0:1, 0:128])
            nc.vector.tensor_scalar(wcol[:, NMEAN:NMEAN + 1], mom[:, CH:CH + 1], -1.0 / N, None, ALU.mult)
            wdone(nc.vector.tensor_scalar(wrow[:, 128:256], PS[1][0:1, 0:128], -1.0 / N, None, ALU.mult), "rows")
            dve.wait_ge(w_pe, PSTEP["outer"])
            wlink = chain(w_link)
            wlink(nc.vector.tensor_tensor(momc[:, :], PS[2][:, 0:CH], mom[:, 0:CH], ALU.add))
            wlink(nc.vector.scalar_tensor_tensor(
                cov[:, :].rearrange("p (w c) -> p w c", w=2),
                momc[:, :].rearrange("p (a c) -> p a c", a=1).to_broadcast([128, 2, CH]), (1.0 - WH_EPS) / (N - 1.0),
                gsum[:, :].rearrange("p (w c) -> p w c", w=2), ALU.mult, ALU.mult))
            wlink(nc.vector.scalar_tensor_tensor(cov[:, :], ident[:, :], WH_EPS, cov[:, :], ALU.mult, ALU.add))
            wlink(nc.vector.tensor_tensor(wtmp[:, :], cov[:, :], ident[:, :], ALU.mult))
            nc.vector.tensor_copy(psig[:, 0, :], ident[:, :])
            wdone(nc.vector.tensor_reduce(wcol[:, DIAG:DIAG + 1], wtmp[:, :], AX.X, ALU.add), "diag")
            dve.wait_ge(w_pe, PSTEP["trace"])
            nc.vector.tensor_copy(wcol[:, TRACE:TRACE + 1], PS[3][:, 0:1])
            wdone(nc.vector.reciprocal(wcol[:, RTRACE:RTRACE + 1], PS[3][:, 0:1]), "trace")
            wdone(nc.vector.tensor_scalar(psig[:, 1, :], cov[:, :], wcol[:, RTRACE:RTRACE + 1], -0.5, ALU.mult, ALU.mult),
                  "psig")
            for i in range(WH_ITER):
                dve.wait_ge(w_pe, PSTEP[f"prod{i}"])
                wdone(nc.vector.tensor_copy(prod[:, :, :].rearrange("p a c -> p (a c)"), PS[4][:, 0:256]), f"prod{i}")
                dve.wait_ge(w_pe, PSTEP[f"p{i}"])
                wdone(nc.vector.scalar_tensor_tensor(psig[:, 0, :], psig[:, 0, :], 1.5, PS[5][:, 0:128],
                                                     ALU.mult, ALU.add), f"p{i}")
            dve.wait_ge(w_pool, 1)
            dve.wait_ge(s_par, 16 * NPAR)
            nc.vector.tensor_copy(nmb[:, :], wcol[:, NMEAN:NMEAN + 1].to_broadcast([128, TILE]))
            wdone(nc.vector.scalar_tensor_tensor(
                wfin[:, :].rearrange("p (w c) -> p w c", w=2), psig[:, 0, :].rearrange("p (w c) -> p w c", w=2),
                wcol[:, RSQ:RSQ + 1], gam[:, :].rearrange("p (a c) -> p a c", a=1).to_broadcast([128, 2, CH]),
                ALU.mult, ALU.mult), "wfin")
            dve.wait_ge(w_pe, PSTEP["bias"])
            wdone(nc.vector.tensor_copy(biasb[:, :], PS[6][0:TILE, 0:128]), "biasb")
            for b in range(PAIRS):
                for part, (t0, tn) in enumerate(((0, 4), (4, 3))):
                    n = 2 * b + part
                    dve.wait_ge(o_ready, n + 1)
                    nc.vector.tensor_tensor(
                        outs[b][:, t0:t0 + tn, :],
                        PS[n % 4][0:TILE, 0:tn * 128].rearrange("p (t k) -> p t k", k=128),
                        biasb[:, :].rearrange("p (a k) -> p a k", a=1).to_broadcast([TILE, tn, 128]), ALU.add)\
                        .then_inc(o_done, 1)

        @block.tensor
        def _(pe):
            def mm(o, a, b, start=True, stop=True, **k):
                return nc.tensor.matmul(o, a, b, start=start, stop=stop, **k)

            pe.wait_ge(s_par, 16 * NPAR)
            for k in range(2):
                p = P[k]
                v = p["vec"]
                ps = PS[4 + 2 * k]
                mm(ps[:, 0:1], p["wq"][:, :], v[:, B1:B1 + 1])
                mm(ps[:, 1:2], p["wk"][:, :], v[:, B1:B1 + 1])
                mm(ps[:, 2:3], p["wv"][:, :], v[:, B1:B1 + 1])
                for c in range(4):
                    last = mm(ps[:, 3 + c:4 + c], p["f1"][:, c, :], v[:, B2:B2 + 1])
                last.then_inc(s_fold, 1)
                pe.wait_ge(s_prep, 3 * k + 1)
                mm(PS[5 + 2 * k][:, 0:1], p["wp"][:, :], v[:, VB:VB + 1]).then_inc(s_fold, 1)

            pe.wait_ge(s_con, 16 * NCON)
            pe.wait_ge(s_bias, 16 * 28)
            for k in range(2):
                mm(PS[k][0:KROWS, 0:HEADS * NTOK], turn[:, :], rawn[k][:, :]).then_inc(s_turn, 1)
            pe.wait_ge(tab_link, 1)

            for b in range(PAIRS):
                pe.wait_ge(s_xin[b], 16 * 4)
                for i in range(WROW):
                    n = b * WROW + i
                    if n >= 4:
                        pe.wait_ge(s_tpcp, n - 3)
                    nc.tensor.transpose(PS[n % 4][:, 0:TA], XA[:, b, i, :], ident[0:TA, 0:TA])
                    nc.tensor.transpose(PS[n % 4][:, TA:TA + TB], XB[:, b, i, :], ident[0:TB, 0:TB]).then_inc(s_tp, 1)

            pe.wait_ge(s_round, 1)
            pe.wait_ge(s_zero, 2)
            pe.wait_ge(s_prep, NPREP)

            def f_xc(blk, g, prologue=False):
                if prologue != 0:
                    pe.wait_ge(k_done, 3 * g)
                mm(bG[2][:, 0:TOK], centre[:, :], xcols(blk, g % HALVES if isinstance(g, int) else g - HALVES * blk))\
                    .then_inc(xc_ready, 1)

            def f_var(g):
                pe.wait_ge(sq_done, g + 1)
                mm(bG[0][:, 0:TOK], avg64[:, :], sq[:, :]).then_inc(var_ready, 1)

            def f_qk(p, g1):
                pe.wait_ge(z_done, g1 + 1)
                pe.wait_ge(rx_done, g1)
                mm(bG[1][:, 0:TOK], p["wq"][:, :], z[:, :]).then_inc(q_ready, 1)
                mm(bG[2][:, 0:TOK], p["wk"][:, :], z[:, :]).then_inc(k_ready, 1)

            def f_v(p, g1):
                for w in range(WIN):
                    for im in range(2):
                        r = slice(64 * im, 64 * im + 64)
                        last = mm(bG[1][64 * im:64 * im + NTOK, w * CH:(w + 1) * CH],
                                  z[r, w * NTOK:(w + 1) * NTOK], p["wv2"][r, :])
                last.then_inc(v_ready, 1)

            def scores(p, blk, odd, g1, w):
                pe.wait_ge(kexp_done, WIN * g1 + w + 1)
                pe.wait_ge(max_done, WIN * g1 + w)
                t = win_kind(blk, odd, w)
                mm(bS[0:NROWS, 0:HEADS * NTOK], qbd[:, w, :], kexp[:, w, :, :].rearrange("p h m -> p (h m)"),
                   True, False)
                mm(bS[0:NROWS, 0:HEADS * NTOK], ident_r[0:NROWS, 0:NROWS], p["bn"][:, t, :], False, True)\
                    .then_inc(s_ready, 1)

            def maxt(g1, prologue=False):
                pe.wait_ge(nmaxw_done, 2 * (g1 + 1))
                if prologue:
                    pe.wait_ge(v_done, 2 * (g1 + 1))
                else:
                    pe.wait_ge(rec_done, 2 * (g1 - 1) + 1)
                mm(bG[1][:, 0:50], nmaxw[:, :, :, :].rearrange("p a w h -> p (a w h)"), fold_r[:, :])\
                    .then_inc(mxt_ready, 1)

            def scores_t(p, blk, odd, g, w, buf, first):
                if w == 0:
                    pe.wait_ge(k_done, 3 * g + 3)
                    pe.wait_ge(rx_done, g + 1)
                pe.wait_ge(qexp_done, WIN * g + w + 1)
                if not (first and w < 2):
                    pe.wait_ge(exp_done, WIN * g + w - 1)
                t = win_kind(blk, odd, w)
                o = bST[w % 2][0:KROWS, 0:HEADS * NTOK]
                mm(o, kbd[buf][:, w, :], qexp[buf][:, w, :, :].rearrange("p h n -> p (h n)"), True, False)
                mm(o, ident_r[0:KROWS, 0:KROWS], p["bh"][:, t, :], False, False)
                mm(o, ident_r[0:KROWS, 0:KROWS], p["bl"][:, t, :], False, False)
                mm(o, sel_r[:, w, 0:KROWS], rx[:, :, :].rearrange("p h n -> p (h n)"), False, True)\
                    .then_inc(st_ready, 1)

            def pv(g, w, buf, first):
                pe.wait_ge(exp_done, WIN * g + w + 1)
                if w == 0:
                    pe.wait_ge(v_done, 2 * g + 2)
                if w in (0, 4) and not first:
                    pe.wait_ge(osb_done, 2 * g - 1 + w // 4)
                for h in range(HEADS):
                    hh, h4 = h // 4, h % 4
                    c0 = (w % 4) * NROWS + hh * NTOK
                    last = mm(bO[w // 4][32 * h4:32 * h4 + 32, c0:c0 + NTOK], vbd[buf][:, w * HEADS + h, :],
                              pt[w % 4][:, h * NTOK:(h + 1) * NTOK])
                last.then_inc(av_ready, 1)

            def den(g, part):
                pe.wait_ge(osb_done, 2 * g + part + 1)
                mm(bG[1 - part][:, 0:4 * NROWS], dsel[:, :], osb[part][:, :]).then_inc(den_ready, 1)

            def proj(p, g):
                pe.wait_ge(att_done, 2 * g + 2)
                for hh in range(2):
                    last = mm(bG[0][:, 0:TOK], p["wph"][hh][:, :], att[:, :, hh * NTOK:(hh + 1) * NTOK], hh == 0, hh == 1)
                last.then_inc(proj_ready, 1)

            def step(p, blk, g, u, first, more, more2, third=True):
                base = HALVES * blk
                G = base + g
                nb = (u + 1) % 2
                f = first and blk == 0
                scores_t(p, blk, u, G, 0, u, f)
                if not first:
                    if more:
                        pe.wait_ge(var_used, G + 2)
                    if third:
                        pe.wait_ge(res_done, G - 1)
                    den(G - 1, 1)
                scores_t(p, blk, u, G, 1, u, f)
                pv(G, 0, u, f)
                if more:
                    f_qk(p, G + 1)
                scores_t(p, blk, u, G, 2, u, f)
                pv(G, 1, u, f)
                if not first:
                    proj(p, G - 1)
                scores_t(p, blk, u, G, 3, u, f)
                if more:
                    pe.wait_ge(q_done, 3 * G + 6)
                pv(G, 2, u, f)
                if more:
                    f_v(p, G + 1)
                    scores(p, blk, nb, G + 1, 0)
                scores_t(p, blk, u, G, 4, u, f)
                pv(G, 3, u, f)
                if more2:
                    f_xc(blk, G + 2, True)
                if more:
                    scores(p, blk, nb, G + 1, 1)
                    scores(p, blk, nb, G + 1, 2)
                scores_t(p, blk, u, G, 5, u, f)
                pv(G, 4, u, f)
                if more:
                    pe.wait_ge(v_done, 2 * (G + 2))
                den(G, 0)
                if more:
                    for w in (3, 4, 5):
                        scores(p, blk, nb, G + 1, w)
                scores_t(p, blk, u, G, 6, u, f)
                pv(G, 5, u, f)
                if more2:
                    if not first:
                        pe.wait_ge(res_done, G)
                    f_var(G + 2)
                if more:
                    for w in (6, 7):
                        scores(p, blk, nb, G + 1, w)
                scores_t(p, blk, u, G, 7, u, f)
                pv(G, 6, u, f)
                if more:
                    maxt(G + 1)
                pv(G, 7, u, f)

            for blk in range(2):
                base = HALVES * blk
                p = P[blk]
                if blk:
                    pe.wait_ge(relay_done, PAIRS)
                else:
                    pe.wait_ge(s_tpcp, PAIRS * WROW)
                pe.wait_ge(s_btab, blk + 1)
                f_xc(blk, base)
                f_var(base)
                f_qk(p, base)
                pe.wait_ge(q_done, 3 * base + 3)
                f_v(p, base)
                f_xc(blk, base + 1, True)
                for w in range(WIN):
                    scores(p, blk, 0, base, w)
                maxt(base, True)
                pe.wait_ge(var_used, base + 1)
                f_var(base + 1)
                step(p, blk, 0, 0, True, True, True)
                step(p, blk, 1, 1, False, True, True, third=False)
                with pe.Fori(1, PAIRS - 1) as it:
                    for u in range(2):
                        step(p, blk, it * 2 + u, u, False, True, True)
                step(p, blk, HALVES - 2, 0, False, True, False)
                step(p, blk, HALVES - 1, 1, False, False, False)
                G = base + HALVES - 1
                pe.wait_ge(res_done, G)
                den(G, 1)
                proj(p, G)
                pe.wait_ge(res_done, G + 1)

                def m_xc(g):
                    pe.wait_ge(mz_done, base + g)
                    mm(PS[0][:, 0:TOK], centre[:, :], xcols(blk, g)).then_inc(mxc, 1)

                def m_var(g):
                    pe.wait_ge(msq, base + g + 1)
                    pe.wait_ge(mvar_used, base + g)
                    mm(PS[1][:, 0:TOK], avg64[:, :], sq[:, :]).then_inc(mvar, 1)

                def fc1(g, c):
                    if c == 0:
                        pe.wait_ge(mz_done, base + g + 1)
                    if c < 2:
                        pe.wait_ge(gelu_done, 4 * (base + g))
                    else:
                        pe.wait_ge(gelu_done, 4 * (base + g) + c - 1)
                    mm(PS[2 + c % 2][:, 0:TOK], p["f1"][:, c, :], z[:, :]).then_inc(fc1_ready, 1)

                def fc2(g, c):
                    if c == 0:
                        pe.wait_ge(mres_done, base + g)
                    pe.wait_ge(gelu_done, 4 * (base + g) + c + 1)
                    last = mm(PS[4][:, 0:TOK], p["f2"][:, c, :], hid[c], c == 0, c == 3)
                    if c == 3:
                        last.then_inc(fc2_ready, 1)

                def mstep(g, more):
                    fc1(g, 0)
                    fc1(g, 1)
                    if more:
                        m_xc(g + 1)
                    fc1(g, 2)
                    fc1(g, 3)
                    if more:
                        m_var(g + 1)
                    for c in range(4):
                        fc2(g, c)

                if blk:
                    pe.wait_ge(w_dve, WSTEP["sum0"])
                    mm(PS[7][:, 0:1], dup[:, :], wcol[:, SUM0:SUM0 + 1]).then_inc(w_pe, 1)
                m_xc(0)
                m_var(0)
                with pe.Fori(0, PAIRS - 1) as it:
                    for u in range(2):
                        mstep(it * 2 + u, True)
                mstep(HALVES - 2, True)
                mstep(HALVES - 1, False)

            pe.wait_ge(relay_done, 2 * PAIRS)

            def moments(n):
                pe.wait_ge(tt_done, n + 1)
                t = tsb[n % 2]
                mm(PS[7][:, 0:129], t[:, 0:128], t[:, 0:129], n == 0, n == PAIRS * TILES - 1).then_inc(cov_ready, 1)

            pe.wait_ge(w_dve, WSTEP["shift"])
            for n in range(PAIRS * TILES):
                if n >= 2:
                    pe.wait_ge(tt_done, n - 1)
                nc.tensor.transpose(PS[5 + n % 2][0:TILE, 0:128], XR[:, n * TILE:(n + 1) * TILE], ident[:, :])\
                    .then_inc(tt_ready, 1)
                if n >= 1:
                    moments(n - 1)
            moments(PAIRS * TILES - 1)

            pe.wait_ge(w_dve, WSTEP["fold2"])
            mm(PS[0][:, 0:CH + 1], dup[:, :], fold2[:, :]).then_inc(w_pe, 1)
            pe.wait_ge(w_dve, WSTEP["mom"])
            mm(PS[1][0:1, 0:128], mom[:, CH:CH + 1], ident[:, :]).then_inc(w_pe, 1)
            pe.wait_ge(w_dve, WSTEP["rows"])
            mm(PS[2][:, 0:CH], wrow[:, 0:128], wrow[:, 128:128 + CH]).then_inc(w_pe, 1)
            pe.wait_ge(w_dve, WSTEP["diag"])
            mm(PS[3][:, 0:1], gsum[:, :], wcol[:, DIAG:DIAG + 1]).then_inc(w_pe, 1)
            for i in range(WH_ITER):
                pe.wait_ge(w_dve, WSTEP[f"p{i - 1}" if i else "psig"])
                mm(PS[4][:, 0:256], psig[:, 0, :], psig[:, :, :].rearrange("p a c -> p (a c)")).then_inc(w_pe, 1)
                pe.wait_ge(w_dve, WSTEP[f"prod{i}"])
                mm(PS[5][:, 0:128], prod[:, 0, :], prod[:, 1, :]).then_inc(w_pe, 1)
            pe.wait_ge(w_dve, WSTEP["wfin"])
            mm(PS[6][0:TILE, 0:128], nmb[:, :], wfin[:, :], True, False)
            mm(PS[6][0:TILE, 0:128], ones1[:, :], bet[:, :], False, True).then_inc(w_pe, 1)

            for b in range(PAIRS):
                for part, (t0, tn) in enumerate(((0, 4), (4, 3))):
                    n = 2 * b + part
                    if n >= 4:
                        pe.wait_ge(o_done, n - 3)
                    for t in range(tn):
                        c0 = (b * TILES + t0 + t) * TILE
                        last = mm(PS[n % 4][0:TILE, 128 * t:128 * (t + 1)], XR[:, c0:c0 + TILE], wfin[:, :])
                    last.then_inc(o_ready, 1)


def constants():
    import numpy as np
    f = np.float32
    pw, pc = np.divmod(np.arange(128), CH)
    same_w = (pw[:, None] == pw[None, :])
    c = {}
    c["ident"] = np.eye(128, dtype=f)
    c["centre"] = (np.eye(128) - same_w / CH).astype(f)
    c["avg64"] = (same_w / CH).astype(f)
    c["dup"] = (pc[:, None] == pc[None, :]).astype(f)
    c["gsum"] = (same_w & (pc[:, None] // GROUP == pc[None, :] // GROUP)).astype(f)
    nw, nn = np.divmod(np.arange(NROWS), NTOK)
    fold = np.zeros((NROWS, 50), f)
    fold[np.arange(NROWS), nn] = 1
    c["fold"] = fold
    turn = np.zeros((NROWS, KROWS), f)
    turn[np.arange(NROWS), 64 * nw + NTOK - 1 - nn] = 1
    c["turn"] = turn
    c["wmask"] = np.stack([nw == 0, nw == 1], 1).astype(f)
    c["hmask"] = (pc[:, None] // HD == np.arange(HEADS)[None]).astype(f)
    win, rest = np.divmod(np.arange(128), 2 * HEADS)
    rw, rh = np.divmod(rest, HEADS)
    c["hmask2"] = (rh[:, None] == np.arange(HEADS)[None]).astype(f)
    sel = np.zeros((128, WIN, 128), f)
    for p in range(128):
        sel[p, win[p], 64 * rw[p]:64 * rw[p] + NTOK] = 1
    c["sel"] = sel.reshape(128, WIN * 128)
    d = np.zeros((128, 128), f)
    for h4 in range(4):
        for r in range(32):
            d[32 * h4 + 16 + (r // HD if r < 2 * HD else 0), 32 * h4 + r] = 1
    c["dsel"] = d
    r, q = np.divmod(np.arange(NTOK), WS)
    row = (r[:, None] >= WS - SHIFT) != (r[None] >= WS - SHIFT)
    col = (q[:, None] >= WS - SHIFT) != (q[None] >= WS - SHIFT)
    m = np.stack([np.zeros((NTOK, NTOK), bool), col, row, row | col], 1) * f(-100)
    maskn, maskt = np.zeros((NROWS, 4, NTOK), f), np.zeros((KROWS, 4, NTOK), f)
    for w in range(2):
        maskn[NTOK * w:NTOK * w + NTOK] = m
        maskt[64 * w:64 * w + NTOK] = m
    c["maskn"], c["maskt"] = maskn.reshape(NROWS, -1), maskt.reshape(KROWS, -1)
    return c


def kernel(**inputs):
    import numpy as _np
    import concourse.bacc as _bacc
    from concourse.bass_utils import run_bass_kernel_spmd as _run

    nc = _bacc.Bacc("TRN2", target_bir_lowering=False, num_devices=1)
    arrays = {}

    def put(name, a):
        a = _np.ascontiguousarray(a)
        arrays[name] = a
        return nc.dram_tensor(name, a.shape, mybir.dt.from_np(a.dtype), kind="ExternalInput").ap()

    x = put("x_dram", inputs["x"])
    par = [{n: put(f"{n}{k}_dram", inputs[f"L0_conv_{n}{k}"]) for n in PARAMS} for k in range(2)]
    gamma, beta = put("gamma_dram", inputs["L1_conv_gamma"]), put("beta_dram", inputs["L1_conv_beta"])
    con = {n: put(f"c_{n}_dram", a) for n, a in constants().items()}
    out = nc.dram_tensor("out_dram", (IMAGES, SIDE, SIDE, CH), F32, kind="ExternalOutput").ap()
    build(nc, x, par, gamma, beta, con, out)
    r = _run(nc, [arrays], core_ids=[0])
    return r.results[0]["out_dram"]
```

```python
import concourse.bass as bass
from concourse import mybir
from contextlib import ExitStack

F32 = mybir.dt.float32
F32R = mybir.dt.float32r
I32 = mybir.dt.int32
ACT = mybir.ActivationFunctionType
ALU = mybir.AluOpType
AX = mybir.AxisListType

IMAGES, SIDE, CH, HEADS, WS, SHIFT = 16, 28, 64, 8, 7, 3
HD = CH // HEADS
NTOK = WS * WS
WROW = SIDE // WS
PAIRS = IMAGES // 2
HALVES = 2 * PAIRS
WIN = 2 * WROW
TOK = WIN * NTOK
IMG_TOK = SIDE * SIDE
KROWS = 64 + NTOK
NROWS = 2 * NTOK
TA, TB = 4 * SIDE, 3 * SIDE
TILE = 4 * SIDE
TILES = IMG_TOK // TILE
LN_EPS = 1.001e-05
WH_EPS = 1e-05
WH_ITER = 5
GROUP = 16
THIRD = 3.0 / 8.0
MAGIC = float(0x5F3759DF)
NLINK = 8

PARAMS = ['ln1_g', 'ln1_b', 'qkv_w', 'qkv_b', 'bias_tab', 'proj_w', 'proj_b', 'ln2_g', 'ln2_b',
          'fc1_w', 'fc1_b', 'fc2_w', 'fc2_b']


def build(nc, x, par, gamma, beta, con, out):
    ctx = ExitStack()
    with ctx:
        def sb(name, shape, dt=F32):
            return ctx.enter_context(nc.sbuf_tensor(name, shape, dt))

        def sem(name):
            return ctx.enter_context(nc.semaphore(name))

        XW = [sb("XW0", [128, HALVES * TOK]), sb("XW1", [128, HALVES * TOK])]
        qexpb = sb("qexp", [128, 2, WIN, HEADS, NTOK])
        qexp = [qexpb[:, i] for i in range(2)]
        XA = XW[1][0:TA, 0:PAIRS * WROW * 128].rearrange("p (b i k) -> p b i k", b=PAIRS, i=WROW)
        XB = qexpb[0:TB].rearrange("p a w h n -> p (a w h n)")[:, 0:PAIRS * WROW * 128]\
            .rearrange("p (b i k) -> p b i k", b=PAIRS, i=WROW)
        XR = XW[0]
        centre = sb("centre", [128, 128])
        avg64 = sb("avg64", [128, 128])
        ident = sb("ident", [128, 128])
        ident_r = sb("ident_r", [128, 128], F32R)
        dup_r = sb("dup_r", [128, 128], F32R)
        fold = sb("fold", [NROWS, 50])
        fold_r = sb("fold_r", [NROWS, 50], F32R)
        wmask = sb("wmask", [NROWS, 2])
        hmask = sb("hmask", [128, HEADS])
        hmask2 = sb("hmask2", [128, HEADS])
        hidb = sb("hid", [128, 4, TOK])
        hid = [hidb[:, i] for i in range(4)]
        sel_f = hidb[:].rearrange("p a b -> p (a b)")[:, 0:WIN * 128]
        sel_r = sb("sel_r", [128, WIN, 128], F32R)
        dsel = sb("dsel", [128, 128])
        maskn = sb("maskn", [NROWS, 4, NTOK])
        maskt = sb("maskt", [KROWS, 4, NTOK])
        dup = sb("dup", [128, 128])
        gsum = sb("gsum", [128, 128])
        P = []
        for k in range(2):
            P.append(dict(
                wq=sb(f"wq{k}", [128, 128]), wk=sb(f"wk{k}", [128, 128]), wv=sb(f"wv{k}", [128, 128]),
                wv2=sb(f"wv2{k}", [128, CH]), wp=sb(f"wp{k}", [128, 128]),
                wph=[sb(f"wph{k}{i}", [128, 128]) for i in range(2)],
                f1=sb(f"f1{k}", [128, 4, 128]), f2=sb(f"f2{k}", [128, 4, 128]),
                vec=sb(f"vec{k}", [128, 16]),
                bn=sb(f"bn{k}", [NROWS, 4 if k else 1, HEADS * NTOK], F32R),
                bt=sb(f"bt{k}", [KROWS, 4 if k else 1, HEADS * NTOK], F32R)))
        G1, B1, G2, B2, QB, KB, VB, PB, F2B, FB = 0, 1, 2, 3, 4, 5, 6, 7, 8, 9
        turn = sb("turn", [NROWS, KROWS])
        epsc = sb("epsc", [128, 1])
        sq = sb("sq", [128, TOK])
        lv = sb("lv", [128, TOK])
        ly = sb("ly", [128, TOK])
        lt = sb("lt", [128, TOK])
        z = sb("z", [128, TOK])
        zb = [z, hidb[:, 3]]
        qbd = sb("qbd", [128, WIN, NROWS], F32R)
        kexp = sb("kexp", [128, WIN, HEADS, NTOK], F32R)
        qsb = sb("qsb", [128, TOK])
        ksb = sb("ksb", [128, TOK])
        kbd = [sb(f"kbd{i}", [128, WIN, KROWS]) for i in range(2)]
        vbd = [sb(f"vbd{i}", [KROWS, WIN * HEADS, 32]) for i in range(2)]
        nmax = sb("nmax", [NROWS, WIN, HEADS])
        nmaxw = sb("nmaxw", [NROWS, WIN, 2, HEADS], F32R)
        rx = sb("rx", [128, HEADS, NTOK], F32R)
        pt = [sb(f"pt{i}", [KROWS, HEADS * NTOK]) for i in range(4)]
        osb = [sb(f"osb{i}", [128, 4 * NROWS]) for i in range(2)]
        rec = [sb(f"rec{i}", [128, 4 * NROWS]) for i in range(2)]
        att = sb("att", [128, WIN, NROWS])
        rawn = [osb[k][0:NROWS, :] for k in range(2)]
        rawt = [rec[k][0:KROWS, :] for k in range(2)]
        btmp = qsb[0:KROWS, :]
        tsb = [sb(f"tsb{i}", [TILE, 132]) for i in range(2)]
        wcol = sb("wcol", [128, 8])
        SUM0, SHIFTC, NMEAN, DIAG, TRACE, RTRACE, RSQ, EXPO = range(8)
        wrow = sb("wrow", [1, 256])
        fold2 = sb("fold2", [128, CH + 1])
        mom = sb("mom", [128, CH + 1])
        momc = sb("momc", [128, CH])
        cov = sb("cov", [128, 128])
        wtmp = sb("wtmp", [128, 128])
        psig = sb("psig", [128, 2, 128])
        prod = sb("prod", [128, 2, 128])
        wfin = sb("wfin", [128, 128])
        nmb = sb("nmb", [128, TILE])
        ones1 = sb("ones1", [1, TILE])
        gam = sb("gam", [128, CH])
        bet = sb("bet", [1, 128])
        biasb = sb("biasb", [TILE, 128])
        outs = [XW[1][0:TILE, b * TILES * 128:(b + 1) * TILES * 128].rearrange("p (t k) -> p t k", k=128)
                for b in range(PAIRS - 1)]
        outs.append(qexpb[0:TILE].rearrange("p a w h n -> p (a w h n)")[:, 0:TILES * 128]
                    .rearrange("p (t k) -> p t k", k=128))

        PS = [ctx.enter_context(nc.psum_tensor(f"PS{i}", [128, 512], F32)) for i in range(8)]
        bST, bO, bG = PS[1:3], PS[3:5], PS[5:8]
        bS = [PS[0], bG[0]]

        s_con, s_par, s_bias = sem("s_con"), sem("s_par"), sem("s_bias")
        s_xin = [sem(f"s_xin{b}") for b in range(PAIRS)]
        s_zero = sem("s_zero")
        s_zero_q = sem("s_zero_q")
        s_round = sem("s_round")
        s_tp, s_tpcp = sem("s_tp"), sem("s_tpcp")
        s_fold, s_prep = sem("s_fold"), sem("s_prep")
        s_btab, tab_link = sem("s_btab"), sem("tab_link")
        s_turn = sem("s_turn")
        z_done, w_link = sem("z_done"), sem("w_link")
        mz_done = sem("mz_done")
        xc_ready, sq_done, var_ready, var_used, ln_link = (
            sem("xc_ready"), sem("sq_done"), sem("var_ready"), sem("var_used"), sem("ln_link"))
        q_ready, k_ready, v_ready, s_ready, mxt_ready, st_ready, av_ready, den_ready, proj_ready = (
            sem("q_ready"), sem("k_ready"), sem("v_ready"), sem("s_ready"), sem("mxt_ready"), sem("st_ready"),
            sem("av_ready"), sem("den_ready"), sem("proj_ready"))
        q_done, k_done, v_done, exp_done, osb_done = (
            sem("q_done"), sem("k_done"), sem("v_done"), sem("exp_done"), sem("osb_done"))
        kexp_dve = sem("kexp_dve")
        kexp_done, max_done, nmaxw_done, rx_done, rec_done, res_done = (
            sem("kexp_done"), sem("max_done"), sem("nmaxw_done"), sem("rx_done"), sem("rec_done"), sem("res_done"))
        qexp_done, att_done = sem("qexp_done"), sem("att_done")
        mxc, msq, mvar, mvar_used, mlink = sem("mxc"), sem("msq"), sem("mvar"), sem("mvar_used"), sem("mlink")
        fc1_ready, gelu_done, fc2_ready, mres_done = (
            sem("fc1_ready"), sem("gelu_done"), sem("fc2_ready"), sem("mres_done"))
        relay_done = sem("relay_done")
        tt_ready, tt_done, cov_ready = sem("tt_ready"), sem("tt_done"), sem("cov_ready")
        w_pe, w_dve, w_pool = sem("w_pe"), sem("w_dve"), sem("w_pool")
        o_ready, o_done, s_out = sem("o_ready"), sem("o_done"), sem("s_out")

        def win_kind(blk, half_odd, win):
            if blk == 0:
                return 0
            return (1 if win % WROW == WROW - 1 else 0) + (2 if half_odd and win >= WROW else 0)

        def xcols(blk, g):
            return XW[blk][:, bass.ds(g * TOK, TOK)]

        KH = 2
        NPREP = 6
        NCON, NPAR = 14, 2 * 2 * 28 + 4
        WSTEP = {n: i + 1 for i, n in enumerate(
            ["sum0", "shift", "fold2", "mom", "rows", "diag", "trace", "psig"]
            + [f"prod{i}" if j == 0 else f"p{i}" for i in range(WH_ITER) for j in range(2)]
            + ["wfin", "biasb"])}
        PSTEP = {n: i + 1 for i, n in enumerate(
            ["shift", "mom", "row", "outer", "trace"]
            + [f"prod{i}" if j == 0 else f"p{i}" for i in range(WH_ITER) for j in range(2)] + ["bias"])}
        block = ctx.enter_context(nc.Block())

        @block.sync
        def _(sp):
            for t, src in ((centre, "centre"), (avg64, "avg64"), (ident, "ident"), (fold, "fold"), (wmask, "wmask"),
                           (hmask, "hmask"), (hmask2, "hmask2"), (sel_f, "sel"), (dsel, "dsel"),
                           (maskn, "maskn"), (maskt, "maskt"), (dup, "dup"), (gsum, "gsum"), (turn, "turn")):
                sp.dma_start(t[:] if len(t.shape) == 2 else t[:].rearrange("p a b -> p (a b)"), con[src])\
                    .then_inc(s_con, 16)
            for b in range(PAIRS):
                for w in range(2):
                    img = x[b + PAIRS * w].rearrange("r q c -> (r q) c").rearrange("(i t) c -> t i c", i=WROW)
                    sp.dma_start(XA[:, b, :, CH * w:CH * w + CH], img[0:TA]).then_inc(s_xin[b], 16)
                    sp.dma_start(XB[:, b, :, CH * w:CH * w + CH], img[TA:TA + TB]).then_inc(s_xin[b], 16)
            for b in range(PAIRS):
                sp.wait_ge(o_done, 2 * (b + 1))
                for w in range(2):
                    dst = out[b + PAIRS * w].rearrange("r q c -> (r q) c").rearrange("(t p) c -> p t c", p=TILE)
                    sp.dma_start(dst, outs[b][:, :, CH * w:CH * w + CH]).then_inc(s_out, 16)
            sp.wait_ge(s_out, 16 * 2 * PAIRS)

        def pool_relay(pool, blk, b):
            src = XW[blk][:, bass.ds(b * 2 * TOK, 2 * TOK)].rearrange("p (i j r c) -> p i j r c", i=WROW, j=WROW, r=WS)
            if blk == 0:
                dst = XW[1][:, bass.ds(b * 2 * TOK, 2 * TOK)].rearrange("p (i j r c) -> p i j r c", i=WROW, j=WROW, r=WS)
                far = WS - SHIFT
                last = None
                for i in range(WROW):
                    for ro, rn, ri, si in ((0, far, SHIFT, i), (far, SHIFT, 0, (i + 1) % WROW)):
                        for jo, jn, co, cn, ji, ci in ((0, WROW, 0, far, 0, SHIFT),
                                                       (0, WROW - 1, far, SHIFT, 1, 0),
                                                       (WROW - 1, 1, far, SHIFT, 0, 0)):
                            last = nc.gpsimd.tensor_copy(
                                dst[:, i, jo:jo + jn, ro:ro + rn, co:co + cn],
                                src[:, si, ji:ji + jn, ri:ri + rn, ci:ci + cn])
                last.then_inc(relay_done, 1)
            else:
                dst = XR[:, bass.ds(b * 2 * TOK, 2 * TOK)].rearrange("p (y q) -> p y q", q=SIDE)
                last = None
                for i in range(WROW):
                    rows = ((0, WS, WS * i + SHIFT),) if i < WROW - 1 else \
                        ((0, WS - SHIFT, WS * i + SHIFT), (WS - SHIFT, SHIFT, 0))
                    for r0, rn, y0 in rows:
                        for j in range(WROW):
                            cols = ((0, WS, WS * j + SHIFT),) if j < WROW - 1 else \
                                ((0, WS - SHIFT, WS * j + SHIFT), (WS - SHIFT, SHIFT, 0))
                            for c0, cn, q0 in cols:
                                last = nc.gpsimd.tensor_tensor(
                                    dst[:, y0:y0 + rn, q0:q0 + cn], src[:, i, j, r0:r0 + rn, c0:c0 + cn],
                                    wcol[:, SHIFTC:SHIFTC + 1].rearrange("p (a b) -> p a b", a=1)
                                    .to_broadcast([128, rn, cn]), ALU.subtract)
                last.then_inc(relay_done, 1)

        @block.gpsimd
        def _(pool):
            for i in range(2):
                nc.gpsimd.memset(kbd[i][:, :, :], 0.0)
                nc.gpsimd.memset(vbd[i][:, :, :], 0.0)
            nc.gpsimd.memset(ones1[:, :], 1.0)
            for i in range(2):
                nc.gpsimd.memset(tsb[i][:, 128:129], 1.0)
            nc.gpsimd.memset(epsc[:, :], LN_EPS)
            for k in range(2):
                for name in ("wq", "wk", "wv", "wp"):
                    nc.gpsimd.memset(P[k][name][:, :], 0.0)
                for i in range(2):
                    nc.gpsimd.memset(P[k]["wph"][i][:, :], 0.0)
                for name in ("f1", "f2"):
                    nc.gpsimd.memset(P[k][name][:, :, :], 0.0)
            nc.gpsimd.memset(wcol[:, EXPO:EXPO + 1], -0.5).then_inc(s_zero, 1)
            pool.wait_ge(s_zero, 1)
            for i in range(2):
                for w in range(2):
                    last = nc.gpsimd.memset(vbd[i][64 * w:64 * w + NTOK, :, 16 + w:17 + w], 1.0)
            last.then_inc(s_zero, 1)

            def qexpand(g1, buf):
                pool.wait_ge(q_done, 3 * g1 + 3)
                for w in range(WIN):
                    nc.gpsimd.tensor_tensor(
                        qexp[buf][:, w, :, :],
                        qsb[:, w * NTOK:(w + 1) * NTOK].rearrange("p (a n) -> p a n", a=1).to_broadcast([128, HEADS, NTOK]),
                        hmask[:, :].rearrange("p (h a) -> p h a", a=1).to_broadcast([128, HEADS, NTOK]),
                        ALU.mult).then_inc(qexp_done, 1)

            def attn(g, part):
                pool.wait_ge(rec_done, 2 * g + part + 1)
                if part == 0:
                    pool.wait_ge(proj_ready, g)
                nc.gpsimd.tensor_tensor(
                    att[:, 4 * part:4 * part + 4, :], osb[part][:, :].rearrange("p (a n) -> p a n", a=4),
                    rec[part][:, :].rearrange("p (a n) -> p a n", a=4), ALU.mult).then_inc(att_done, 1)

            def step(base, g, u, first, more):
                if not first:
                    attn(base + g - 1, 0)
                    attn(base + g - 1, 1)
                if more:
                    if not first:
                        pool.wait_ge(st_ready, WIN * (base + g))
                    qexpand(base + g + 1, (u + 1) % 2)

            pool.wait_ge(s_con, 16 * NCON)
            for blk in range(2):
                base = HALVES * blk
                if blk:
                    pool.wait_ge(st_ready, WIN * base)
                qexpand(base, 0)
                step(base, 0, 0, True, True)
                step(base, 1, 1, False, True)
                with pool.Fori(1, PAIRS - 1) as it:
                    for u in range(2):
                        step(base, it * 2 + u, u, False, True)
                step(base, HALVES - 2, 0, False, True)
                step(base, HALVES - 1, 1, False, False)
                attn(base + HALVES - 1, 0)
                attn(base + HALVES - 1, 1)
                if blk:
                    pool.wait_ge(w_dve, WSTEP["shift"])
                with pool.Fori(0, PAIRS) as it:
                    pool.wait_ge(mres_done, (it + 1) * 2 + base)
                    pool_relay(pool, blk, it)
            pool.wait_ge(w_dve, WSTEP["trace"])
            nc.gpsimd.tensor_tensor(wcol[:, RSQ:RSQ + 1], wcol[:, TRACE:TRACE + 1], wcol[:, EXPO:EXPO + 1], ALU.pow)\
                .then_inc(w_pool, 1)

        @block.scalar
        def _(act):
            for k in range(2):
                for w in range(2):
                    for a in range(WS):
                        act.dma_start(rawn[k][NTOK * w + WS * a:NTOK * w + WS * a + WS, :].rearrange("p (m s) -> p m s", m=WS),
                                      bass.AP(par[k]["bias_tab"].tensor, a * 13 * HEADS,
                                              [[HEADS, WS], [13 * HEADS, WS], [1, WS * HEADS]])).then_inc(s_bias, 16)
            act.wait_ge(s_zero, 1)
            for k in range(2):
                q = par[k]
                p = P[k]
                w_qkv = q["qkv_w"]

                def load(dst, src):
                    act.dma_start(dst, src).then_inc(s_par, 16)

                for w in range(2):
                    r = slice(CH * w, CH * w + CH)
                    load(p["wq"][r, r], w_qkv[:, 0:CH])
                    load(p["wk"][r, r], w_qkv[:, CH:2 * CH])
                    load(p["wv"][r, r], w_qkv[:, 2 * CH:3 * CH])
                    load(p["wv2"][r, :], w_qkv[:, 2 * CH:3 * CH])
                    load(p["wp"][r, r], q["proj_w"])
                    load(p["f1"][r, :, r], q["fc1_w"].rearrange("c (k j) -> c k j", j=CH))
                    load(p["f2"][r, :, r], q["fc2_w"].rearrange("(k j) c -> j k c", j=CH))
                    for hh in range(2):
                        for h4 in range(4):
                            ch = HD * (4 * hh + h4)
                            load(p["wph"][hh][32 * h4 + HD * w:32 * h4 + HD * w + HD, r], q["proj_w"][ch:ch + HD, :])
                    for col, name, lo in ((G1, "ln1_g", 0), (B1, "ln1_b", 0), (G2, "ln2_g", 0), (B2, "ln2_b", 0),
                                          (QB, "qkv_b", 0), (KB, "qkv_b", CH), (VB, "qkv_b", 2 * CH),
                                          (PB, "proj_b", 0), (F2B, "fc2_b", 0), (FB, "fc1_b", 0),
                                          (FB + 1, "fc1_b", CH), (FB + 2, "fc1_b", 2 * CH), (FB + 3, "fc1_b", 3 * CH)):
                        load(p["vec"][r, col:col + 1], q[name][lo:lo + CH].rearrange("(c a) -> c a", a=1))
            for w in range(2):
                act.dma_start(gam[CH * w:CH * w + CH, :], gamma.rearrange("a b c k -> (a b c) k").to_broadcast([CH, CH]))\
                    .then_inc(s_par, 16)
                act.dma_start(bet[:, CH * w:CH * w + CH], beta.rearrange("a b c k -> (a b c) k")).then_inc(s_par, 16)

            for b in range(PAIRS):
                for i in range(WROW):
                    n = b * WROW + i
                    act.wait_ge(s_tp, n + 1)
                    src = PS[n % 4][:, 0:WS * SIDE].rearrange("p (r j c) -> p r j c", r=WS, j=WROW)
                    dst = XW[0][:, n * WS * SIDE:(n + 1) * WS * SIDE].rearrange("p (j r c) -> p r j c", j=WROW, r=WS)
                    nc.scalar.activation(dst, src, ACT.Copy).then_inc(s_tpcp, 1)

            def square(g):
                act.wait_ge(xc_ready, g + 1)
                act.wait_ge(var_ready, g)
                nc.scalar.activation(sq[:, :], bG[2][:, 0:TOK], ACT.Square).then_inc(sq_done, 1)

            def variance(g):
                act.wait_ge(var_ready, g + 1)
                act.wait_ge(z_done, g)
                nc.scalar.activation(lv[:, :], bG[1][:, 0:TOK], ACT.Identity, bias=epsc[:, 0:1]).then_inc(var_used, 1)

            def evac_k(p, g1):
                act.wait_ge(k_ready, g1 + 1)
                act.wait_ge(kexp_done, KH * g1)
                act.wait_ge(kexp_dve, (HEADS - KH) * g1)
                nc.scalar.activation(ksb[:, :], bG[2][:, 0:TOK], ACT.Identity, bias=p["vec"][:, KB:KB + 1])\
                    .then_inc(k_done, 1)

            def evac_q(p, g1):
                act.wait_ge(q_ready, g1 + 1)
                act.wait_ge(s_ready, WIN * g1)
                for w in range(2):
                    r = slice(64 * w, 64 * w + 64)
                    nc.scalar.activation(qbd[r, :, NTOK * w:NTOK * w + NTOK],
                                         bG[1][r, 0:TOK].rearrange("p (a n) -> p a n", n=NTOK),
                                         ACT.Identity, bias=p["vec"][r, QB:QB + 1]).then_inc(q_done, 1)
                act.wait_ge(qexp_done, WIN * g1)
                nc.scalar.activation(qsb[:, :], bG[1][:, 0:TOK], ACT.Identity, bias=p["vec"][:, QB:QB + 1])\
                    .then_inc(q_done, 1)

            def evac_kbd(p, g1, buf, prologue=False):
                if not prologue:
                    act.wait_ge(st_ready, WIN * (g1 - 1))
                for w in range(2):
                    r = slice(64 * w, 64 * w + 64)
                    nc.scalar.activation(kbd[buf][r, :, 64 * w:64 * w + NTOK],
                                         bG[2][r, 0:TOK].rearrange("p (a n) -> p a n", n=NTOK),
                                         ACT.Identity, bias=p["vec"][r, KB:KB + 1]).then_inc(k_done, 1)

            def kexpand(g1, heads):
                for h in heads:
                    if h == 0:
                        act.wait_ge(k_done, 3 * g1 + 1)
                        act.wait_ge(s_ready, WIN * g1)
                    nc.scalar.activation(kexp[:, :, h, :], ksb[:, :].rearrange("p (a n) -> p a n", n=NTOK), ACT.Copy,
                                         scale=hmask[:, h:h + 1]).then_inc(kexp_done, 1)

            def evac_v(g1, buf, prologue=False):
                act.wait_ge(v_ready, g1 + 1)
                if not prologue:
                    act.wait_ge(av_ready, WIN * (g1 - 1))
                for w in range(2):
                    nc.scalar.activation(vbd[buf][64 * w:64 * w + NTOK, :, HD * w:HD * w + HD],
                                         bG[0][64 * w:64 * w + NTOK, :].rearrange("p (a d) -> p a d", d=HD),
                                         ACT.Copy).then_inc(v_done, 1)

            def expo(g, w, first=False):
                act.wait_ge(st_ready, WIN * g + w + 1)
                if not (first and w < 4):
                    act.wait_ge(av_ready, WIN * g + w - 3)
                nc.scalar.activation(pt[w % 4][:, :], bST[w % 2][0:KROWS, 0:HEADS * NTOK], ACT.Exp)\
                    .then_inc(exp_done, 1)

            def o_copy(g, part, first=False):
                act.wait_ge(av_ready, WIN * g + 4 * part + 4)
                if not first:
                    act.wait_ge(att_done, 2 * (g - 1) + part + 1)
                nc.scalar.activation(osb[part][:, :], bO[part][:, 0:4 * NROWS], ACT.Copy).then_inc(osb_done, 1)

            def step(p, base, g, u, first, more, more2):
                G = base + g
                nb = (u + 1) % 2
                f = first and base == 0
                expo(G, 0, f)
                expo(G, 1, f)
                if more:
                    evac_k(p, G + 1)
                    evac_q(p, G + 1)
                expo(G, 2, f)
                if more:
                    kexpand(G + 1, range(KH))
                    evac_kbd(p, G + 1, nb)
                expo(G, 3, f)
                if more2:
                    square(G + 2)
                if more:
                    evac_v(G + 1, nb)
                if more2:
                    variance(G + 2)
                expo(G, 4)
                o_copy(G, 0, f)
                expo(G, 5)
                expo(G, 6)
                expo(G, 7)
                o_copy(G, 1, f)

            act.wait_ge(s_prep, NPREP)
            act.wait_ge(s_zero, 2)
            act.wait_ge(s_zero_q, 1)
            for blk in range(2):
                base = HALVES * blk
                p = P[blk]
                if blk:
                    act.wait_ge(relay_done, PAIRS)
                square(base)
                variance(base)
                evac_k(p, base)
                evac_q(p, base)
                evac_kbd(p, base, 0, True)
                kexpand(base, range(KH))
                evac_v(base, 0, True)
                square(base + 1)
                variance(base + 1)
                step(p, base, 0, 0, True, True, True)
                step(p, base, 1, 1, False, True, True)
                with act.Fori(1, PAIRS - 1) as it:
                    for u in range(2):
                        step(p, base, it * 2 + u, u, False, True, True)
                step(p, base, HALVES - 2, 0, False, True, False)
                step(p, base, HALVES - 1, 1, False, False, False)

                def msquare(g):
                    act.wait_ge(mxc, g + 1)
                    act.wait_ge(mvar, g)
                    nc.scalar.activation(sq[:, :], PS[0][:, 0:TOK], ACT.Square).then_inc(msq, 1)

                def mvariance(g):
                    act.wait_ge(mvar, g + 1)
                    act.wait_ge(mz_done, g)
                    nc.scalar.activation(lv[:, :], PS[1][:, 0:TOK], ACT.Identity, bias=epsc[:, 0:1])\
                        .then_inc(mvar_used, 1)

                def gelus(g, m):
                    for c in (2 * m, 2 * m + 1):
                        act.wait_ge(fc1_ready, 4 * g + c + 1)
                        act.wait_ge(fc2_ready, g)
                        nc.scalar.activation(hid[c], PS[2 + c % 2][:, 0:TOK], ACT.Gelu,
                                             bias=p["vec"][:, FB + c:FB + c + 1]).then_inc(gelu_done, 1)

                msquare(base)
                mvariance(base)
                with act.Fori(0, PAIRS - 1) as it:
                    for u in range(2):
                        g = base + it * 2 + u
                        gelus(g, 0)
                        msquare(g + 1)
                        gelus(g, 1)
                        mvariance(g + 1)
                gelus(base + HALVES - 2, 0)
                msquare(base + HALVES - 1)
                gelus(base + HALVES - 2, 1)
                mvariance(base + HALVES - 1)
                gelus(base + HALVES - 1, 0)
                gelus(base + HALVES - 1, 1)
            for n in range(PAIRS * TILES):
                act.wait_ge(tt_ready, n + 1)
                if n >= 2:
                    act.wait_ge(cov_ready, n - 1)
                nc.scalar.activation(tsb[n % 2][:, 0:128], PS[5 + n % 2][0:TILE, 0:128], ACT.Copy).then_inc(tt_done, 1)

        @block.vector
        def _(dve):
            nc.vector.memset(qbd[:, :, :].bitcast(F32), 0.0).then_inc(s_zero_q, 1)
            dve.wait_ge(s_con, 16 * NCON)
            nc.vector.tensor_copy(ident_r[:, :], ident[:, :])
            nc.vector.tensor_copy(dup_r[:, :], dup[:, :])
            nc.vector.tensor_copy(fold_r[:, :], fold[:, :])
            nc.vector.tensor_copy(sel_r[:, :, :].rearrange("p a b -> p (a b)"), sel_f[:, :]).then_inc(s_round, 1)

            def chain(semaphore):
                count = [0]

                def link(ins):
                    count[0] += 1
                    ins.then_inc(semaphore, 1)
                    dve.wait_ge(semaphore, count[0])
                return link

            plink = chain(s_prep)
            for k in range(2):
                p = P[k]
                v = p["vec"]
                dve.wait_ge(s_fold, 2 * k + 1)
                ps = PS[4 + 2 * k]
                plink(nc.vector.tensor_tensor(v[:, VB:VB + 1], ps[:, 2:3], v[:, VB:VB + 1], ALU.add))
                nc.vector.tensor_tensor(v[:, KB:KB + 1], ps[:, 1:2], v[:, KB:KB + 1], ALU.add)
                nc.vector.tensor_tensor(v[:, FB:FB + 4], ps[:, 3:7], v[:, FB:FB + 4], ALU.add)
                plink(nc.vector.tensor_tensor(v[:, QB:QB + 1], ps[:, 0:1], v[:, QB:QB + 1], ALU.add))
                nc.vector.tensor_scalar(v[:, QB:QB + 1], v[:, QB:QB + 1], HD ** -0.5, None, ALU.mult)
                nc.vector.tensor_scalar(p["wq"][:, :], p["wq"][:, :], v[:, G1:G1 + 1], HD ** -0.5, ALU.mult, ALU.mult)
                nc.vector.tensor_scalar(p["wk"][:, :], p["wk"][:, :], v[:, G1:G1 + 1], None, ALU.mult)
                nc.vector.tensor_scalar(p["wv2"][:, :], p["wv2"][:, :], v[:, G1:G1 + 1], None, ALU.mult)
                nc.vector.tensor_scalar(p["f1"][:, :, :], p["f1"][:, :, :], v[:, G2:G2 + 1], None, ALU.mult)
                dve.wait_ge(s_fold, 2 * k + 2)
                plink(nc.vector.tensor_tensor(v[:, PB:PB + 1], PS[5 + 2 * k][:, 0:1], v[:, PB:PB + 1], ALU.add))

            tlink = chain(tab_link)

            def tables(k):
                p = P[k]
                if k == 0:
                    dve.wait_ge(s_bias, 16 * 28)
                    for i in range(2):
                        dve.wait_ge(s_turn, i + 1)
                        last = nc.vector.tensor_copy(rawt[i][:, :], PS[i][0:KROWS, 0:HEADS * NTOK])
                    tlink(last)
                for t in range(4 if k else 1):
                    tlink(nc.vector.tensor_copy(
                        btmp[0:NROWS, :].rearrange("p (h m) -> p h m", h=HEADS),
                        rawn[k][:, :].rearrange("p (m h) -> p h m", h=HEADS)[:, :, ::-1]))
                    tlink(nc.vector.tensor_tensor(
                        p["bn"][:, t, :].rearrange("p (h m) -> p h m", h=HEADS),
                        btmp[0:NROWS, :].rearrange("p (h m) -> p h m", h=HEADS),
                        maskn[:, t:t + 1, :].to_broadcast([NROWS, HEADS, NTOK]), ALU.add))
                    tlink(nc.vector.tensor_tensor(
                        btmp[:, :].rearrange("p (h m) -> p h m", h=HEADS),
                        rawt[k][:, :].rearrange("p (m h) -> p h m", h=HEADS),
                        maskt[:, t:t + 1, :].to_broadcast([KROWS, HEADS, NTOK]), ALU.add))
                    tlink(nc.vector.tensor_copy(p["bt"][:, t, :], btmp[:, :]))
                    tlink(nc.vector.tensor_tensor(p["bt"][64:KROWS, t, :], btmp[64:KROWS, :],
                                                  p["bt"][64:KROWS, t, :].bitcast(F32), ALU.subtract))
                nc.vector.memset(lt[:, 0:1], 0.0).then_inc(s_btab, 1)

            tables(0)
            tables(1)

            def norm(g, zout, xps, used, link, done, zfree, after={}):
                dve.wait_ge(used, g + 1)
                n = [0]

                def ln(ins):
                    n[0] += 1
                    ins.then_inc(link, 1)
                    if n[0] in after:
                        after[n[0]]()
                    dve.wait_ge(link, NLINK * g + n[0])

                ln(nc.vector.tensor_scalar(ly[:, :].bitcast(I32), lv[:, :].bitcast(I32), -0.5, MAGIC, ALU.mult, ALU.add))
                ln(nc.vector.tensor_tensor(lt[:, :], ly[:, :], ly[:, :], ALU.mult))
                ln(nc.vector.tensor_tensor(lt[:, :], lt[:, :], lv[:, :], ALU.mult))
                ln(nc.vector.scalar_tensor_tensor(lt[:, :], lt[:, :], -10.0 / 3.0, lt[:, :], ALU.add, ALU.mult))
                ln(nc.vector.scalar_tensor_tensor(ly[:, :], lt[:, :], 5.0, ly[:, :], ALU.add, ALU.mult))
                ln(nc.vector.tensor_tensor(lt[:, :], ly[:, :], ly[:, :], ALU.mult))
                ln(nc.vector.scalar_tensor_tensor(lt[:, :], lt[:, :], -0.5 * THIRD ** 3, lv[:, :], ALU.mult, ALU.mult))
                ln(nc.vector.scalar_tensor_tensor(ly[:, :], lt[:, :], 1.5 * THIRD, ly[:, :], ALU.add, ALU.mult))
                assert n[0] == NLINK
                zfree()
                nc.vector.tensor_tensor(zout, xps[:, 0:TOK], ly[:, :], ALU.mult).then_inc(done, 1)

            def anorm(g, buf, after={}, first=False):
                norm(g, zb[buf][:, 0:TOK], bG[2], var_used, ln_link, z_done,
                     lambda: None if first else dve.wait_ge(v_ready, g - 1), after)

            def kexpand(g1):
                dve.wait_ge(k_done, 3 * g1 + 1)
                dve.wait_ge(s_ready, WIN * g1)
                for h in range(KH, HEADS):
                    nc.vector.tensor_scalar(kexp[:, :, h, :], ksb[:, :].rearrange("p (a n) -> p a n", n=NTOK),
                                            hmask[:, h:h + 1], None, ALU.mult).then_inc(kexp_dve, 1)

            def rowmax(g1, w):
                dve.wait_ge(s_ready, WIN * g1 + w + 1)
                nc.vector.tensor_reduce(nmax[:, w, :], bS[w % 2][0:NROWS, 0:HEADS * NTOK].rearrange("p (h m) -> p h m", h=HEADS),
                                        AX.X, ALU.max, negate=True).then_inc(max_done, 1)

            def split_max(g1):
                dve.wait_ge(max_done, WIN * (g1 + 1))
                dve.wait_ge(mxt_ready, g1)
                for w in range(2):
                    nc.vector.tensor_scalar(nmaxw[:, :, w, :], nmax[:, :, :], wmask[:, w:w + 1], None, ALU.mult)\
                        .then_inc(nmaxw_done, 1)

            def spread_max(g1):
                dve.wait_ge(mxt_ready, g1 + 1)
                dve.wait_ge(st_ready, WIN * g1)
                nc.vector.tensor_tensor(
                    rx[:, :, :], bG[1][:, 0:NTOK].rearrange("p (a n) -> p a n", a=1).to_broadcast([128, HEADS, NTOK]),
                    hmask2[:, :].rearrange("p (h a) -> p h a", a=1).to_broadcast([128, HEADS, NTOK]),
                    ALU.mult).then_inc(rx_done, 1)

            def recip(g, part, first=False):
                dve.wait_ge(den_ready, 2 * g + part + 1)
                if not first:
                    dve.wait_ge(att_done, 2 * g + part - 1)
                nc.vector.reciprocal(rec[part][:, :], bO[part][:, 0:4 * NROWS]).then_inc(rec_done, 1)

            def residual(p, blk, base, g):
                dve.wait_ge(proj_ready, base + g + 1)
                nc.vector.scalar_tensor_tensor(xcols(blk, g), bG[0][:, 0:TOK], p["vec"][:, PB:PB + 1], xcols(blk, g),
                                               ALU.add, ALU.add).then_inc(res_done, 1)

            def step(p, blk, base, g, u, first, more, more2, second=False):
                G = base + g
                if not first:
                    for part in range(2):
                        recip(G - 1, part, second)
                if more:
                    kexpand(G + 1)
                if not first:
                    residual(p, blk, base, g - 1)
                if more2:
                    rowmax(G + 1, 0)
                    anorm(G + 2, u, {2 * w: (lambda w=w: rowmax(G + 1, w)) for w in range(1, 5)})
                    for w in range(5, WIN):
                        rowmax(G + 1, w)
                elif more:
                    for w in range(WIN):
                        rowmax(G + 1, w)
                if more:
                    split_max(G + 1)
                    spread_max(G + 1)

            for blk in range(2):
                base = HALVES * blk
                p = P[blk]
                anorm(base, 0, first=blk == 0)
                kexpand(base)
                anorm(base + 1, 1, first=blk == 0)
                for w in range(WIN):
                    rowmax(base, w)
                split_max(base)
                spread_max(base)
                step(p, blk, base, 0, 0, True, True, True)
                step(p, blk, base, 1, 1, False, True, True, second=blk == 0)
                with dve.Fori(1, PAIRS - 1) as it:
                    for u in range(2):
                        step(p, blk, base, it * 2 + u, u, False, True, True)
                step(p, blk, base, HALVES - 2, 0, False, True, False)
                step(p, blk, base, HALVES - 1, 1, False, False, False)
                for part in range(2):
                    recip(base + HALVES - 1, part)
                residual(p, blk, base, HALVES - 1)

                if blk:
                    dve.wait_ge(res_done, 2 * HALVES)
                    nc.vector.tensor_reduce(wcol[:, SUM0:SUM0 + 1], XW[1][:, 0:TOK], AX.X, ALU.add).then_inc(w_dve, 1)
                    dve.wait_ge(w_pe, PSTEP["shift"])
                    nc.vector.scalar_tensor_tensor(wcol[:, SHIFTC:SHIFTC + 1], PS[7][:, 0:1], 1.0 / (2 * TOK),
                                                   p["vec"][:, F2B:F2B + 1], ALU.mult, ALU.add).then_inc(w_dve, 1)

                def mnorm(g):
                    norm(g, z[:, :], PS[0], mvar_used, mlink, mz_done, lambda: dve.wait_ge(fc1_ready, 4 * g))

                def mresidual(g):
                    dve.wait_ge(fc2_ready, base + g + 1)
                    nc.vector.scalar_tensor_tensor(xcols(blk, g), PS[4][:, 0:TOK], p["vec"][:, F2B:F2B + 1],
                                                   xcols(blk, g), ALU.add, ALU.add).then_inc(mres_done, 1)

                mnorm(base)
                with dve.Fori(0, PAIRS - 1) as it:
                    for u in range(2):
                        g = it * 2 + u
                        mnorm(base + g + 1)
                        mresidual(g)
                mnorm(base + HALVES - 1)
                mresidual(HALVES - 2)
                mresidual(HALVES - 1)

            def wdone(ins, name):
                ins.then_inc(w_dve, 1)
                done.append(name)
                assert WSTEP[name] == len(done)
                dve.wait_ge(w_dve, WSTEP[name])

            done = ["sum0", "shift"]
            N = float(IMAGES * IMG_TOK)
            dve.wait_ge(cov_ready, PAIRS * TILES)
            nc.vector.tensor_copy(fold2[0:64, 0:CH], PS[7][0:64, 0:64])
            nc.vector.tensor_copy(fold2[64:128, 0:CH], PS[7][64:128, 64:128])
            wdone(nc.vector.tensor_copy(fold2[:, CH:CH + 1], PS[7][:, 128:129]), "fold2")
            dve.wait_ge(w_pe, PSTEP["mom"])
            wdone(nc.vector.tensor_copy(mom[:, :], PS[0][:, 0:CH + 1]), "mom")
            dve.wait_ge(w_pe, PSTEP["row"])
            nc.vector.tensor_copy(wrow[:, 0:128], PS[1][0:1, 0:128])
            nc.vector.tensor_scalar(wcol[:, NMEAN:NMEAN + 1], mom[:, CH:CH + 1], -1.0 / N, None, ALU.mult)
            wdone(nc.vector.tensor_scalar(wrow[:, 128:256], PS[1][0:1, 0:128], -1.0 / N, None, ALU.mult), "rows")
            dve.wait_ge(w_pe, PSTEP["outer"])
            wlink = chain(w_link)
            wlink(nc.vector.tensor_tensor(momc[:, :], PS[2][:, 0:CH], mom[:, 0:CH], ALU.add))
            wlink(nc.vector.scalar_tensor_tensor(
                cov[:, :].rearrange("p (w c) -> p w c", w=2),
                momc[:, :].rearrange("p (a c) -> p a c", a=1).to_broadcast([128, 2, CH]), (1.0 - WH_EPS) / (N - 1.0),
                gsum[:, :].rearrange("p (w c) -> p w c", w=2), ALU.mult, ALU.mult))
            wlink(nc.vector.scalar_tensor_tensor(cov[:, :], ident[:, :], WH_EPS, cov[:, :], ALU.mult, ALU.add))
            wlink(nc.vector.tensor_tensor(wtmp[:, :], cov[:, :], ident[:, :], ALU.mult))
            nc.vector.tensor_copy(psig[:, 0, :], ident[:, :])
            wdone(nc.vector.tensor_reduce(wcol[:, DIAG:DIAG + 1], wtmp[:, :], AX.X, ALU.add), "diag")
            dve.wait_ge(w_pe, PSTEP["trace"])
            nc.vector.tensor_copy(wcol[:, TRACE:TRACE + 1], PS[3][:, 0:1])
            wdone(nc.vector.reciprocal(wcol[:, RTRACE:RTRACE + 1], PS[3][:, 0:1]), "trace")
            wdone(nc.vector.tensor_scalar(psig[:, 1, :], cov[:, :], wcol[:, RTRACE:RTRACE + 1], -0.5, ALU.mult, ALU.mult),
                  "psig")
            for i in range(WH_ITER):
                dve.wait_ge(w_pe, PSTEP[f"prod{i}"])
                wdone(nc.vector.tensor_copy(prod[:, :, :].rearrange("p a c -> p (a c)"), PS[4][:, 0:256]), f"prod{i}")
                dve.wait_ge(w_pe, PSTEP[f"p{i}"])
                wdone(nc.vector.scalar_tensor_tensor(psig[:, 0, :], psig[:, 0, :], 1.5, PS[5][:, 0:128],
                                                     ALU.mult, ALU.add), f"p{i}")
            dve.wait_ge(w_pool, 1)
            dve.wait_ge(s_par, 16 * NPAR)
            nc.vector.tensor_copy(nmb[:, :], wcol[:, NMEAN:NMEAN + 1].to_broadcast([128, TILE]))
            wdone(nc.vector.scalar_tensor_tensor(
                wfin[:, :].rearrange("p (w c) -> p w c", w=2), psig[:, 0, :].rearrange("p (w c) -> p w c", w=2),
                wcol[:, RSQ:RSQ + 1], gam[:, :].rearrange("p (a c) -> p a c", a=1).to_broadcast([128, 2, CH]),
                ALU.mult, ALU.mult), "wfin")
            dve.wait_ge(w_pe, PSTEP["bias"])
            wdone(nc.vector.tensor_copy(biasb[:, :], PS[6][0:TILE, 0:128]), "biasb")
            for b in range(PAIRS):
                for part, (t0, tn) in enumerate(((0, 4), (4, 3))):
                    n = 2 * b + part
                    dve.wait_ge(o_ready, n + 1)
                    nc.vector.tensor_tensor(
                        outs[b][:, t0:t0 + tn, :],
                        PS[n % 4][0:TILE, 0:tn * 128].rearrange("p (t k) -> p t k", k=128),
                        biasb[:, :].rearrange("p (a k) -> p a k", a=1).to_broadcast([TILE, tn, 128]), ALU.add)\
                        .then_inc(o_done, 1)

        @block.tensor
        def _(pe):
            def mm(o, a, b, start=True, stop=True, **k):
                return nc.tensor.matmul(o, a, b, start=start, stop=stop, **k)

            pe.wait_ge(s_par, 16 * NPAR)
            for k in range(2):
                p = P[k]
                v = p["vec"]
                ps = PS[4 + 2 * k]
                mm(ps[:, 0:1], p["wq"][:, :], v[:, B1:B1 + 1])
                mm(ps[:, 1:2], p["wk"][:, :], v[:, B1:B1 + 1])
                mm(ps[:, 2:3], p["wv"][:, :], v[:, B1:B1 + 1])
                for c in range(4):
                    last = mm(ps[:, 3 + c:4 + c], p["f1"][:, c, :], v[:, B2:B2 + 1])
                last.then_inc(s_fold, 1)
                pe.wait_ge(s_prep, 3 * k + 1)
                mm(PS[5 + 2 * k][:, 0:1], p["wp"][:, :], v[:, VB:VB + 1]).then_inc(s_fold, 1)

            pe.wait_ge(s_con, 16 * NCON)
            pe.wait_ge(s_bias, 16 * 28)
            for k in range(2):
                mm(PS[k][0:KROWS, 0:HEADS * NTOK], turn[:, :], rawn[k][:, :]).then_inc(s_turn, 1)
            pe.wait_ge(tab_link, 1)

            for b in range(PAIRS):
                pe.wait_ge(s_xin[b], 16 * 4)
                for i in range(WROW):
                    n = b * WROW + i
                    if n >= 4:
                        pe.wait_ge(s_tpcp, n - 3)
                    nc.tensor.transpose(PS[n % 4][:, 0:TA], XA[:, b, i, :], ident[0:TA, 0:TA])
                    nc.tensor.transpose(PS[n % 4][:, TA:TA + TB], XB[:, b, i, :], ident[0:TB, 0:TB]).then_inc(s_tp, 1)

            pe.wait_ge(s_round, 1)
            pe.wait_ge(s_zero, 2)
            pe.wait_ge(s_prep, NPREP)

            def f_xc(blk, g, prologue=False):
                if prologue != 0:
                    pe.wait_ge(k_done, 3 * g)
                mm(bG[2][:, 0:TOK], centre[:, :], xcols(blk, g % HALVES if isinstance(g, int) else g - HALVES * blk))\
                    .then_inc(xc_ready, 1)

            def f_var(g):
                pe.wait_ge(sq_done, g + 1)
                mm(bG[1][:, 0:TOK], avg64[:, :], sq[:, :]).then_inc(var_ready, 1)

            def f_qk(p, g1, buf):
                pe.wait_ge(z_done, g1 + 1)
                pe.wait_ge(rx_done, g1)
                mm(bG[2][:, 0:TOK], p["wk"][:, :], zb[buf][:, 0:TOK]).then_inc(k_ready, 1)
                mm(bG[1][:, 0:TOK], p["wq"][:, :], zb[buf][:, 0:TOK]).then_inc(q_ready, 1)

            def f_v(p, buf, wins):
                for w in wins:
                    for im in range(2):
                        r = slice(64 * im, 64 * im + 64)
                        last = mm(bG[0][64 * im:64 * im + NTOK, w * CH:(w + 1) * CH],
                                  zb[buf][r, w * NTOK:(w + 1) * NTOK], p["wv2"][r, :])
                if w == WIN - 1:
                    last.then_inc(v_ready, 1)

            def scores(p, blk, odd, g1, w):
                if w == 0:
                    pe.wait_ge(kexp_done, KH * (g1 + 1))
                    pe.wait_ge(kexp_dve, (HEADS - KH) * (g1 + 1))
                if w == 1:
                    pe.wait_ge(v_done, 2 * g1 + 2)
                if w > 1:
                    pe.wait_ge(max_done, WIN * g1 + w - 1)
                t = win_kind(blk, odd, w)
                mm(bS[w % 2][0:NROWS, 0:HEADS * NTOK], qbd[:, w, :], kexp[:, w, :, :].rearrange("p h m -> p (h m)"),
                   True, False)
                mm(bS[w % 2][0:NROWS, 0:HEADS * NTOK], ident_r[0:NROWS, 0:NROWS], p["bn"][:, t, :], False, True)\
                    .then_inc(s_ready, 1)

            def maxt(g1):
                pe.wait_ge(nmaxw_done, 2 * (g1 + 1))
                pe.wait_ge(v_done, 2 * (g1 + 1))
                mm(bG[1][:, 0:50], nmaxw[:, :, :, :].rearrange("p a w h -> p (a w h)"), fold_r[:, :])\
                    .then_inc(mxt_ready, 1)

            def scores_t(p, blk, odd, g, w, buf, first):
                if w == 0:
                    pe.wait_ge(k_done, 3 * g + 3)
                    pe.wait_ge(rx_done, g + 1)
                pe.wait_ge(qexp_done, WIN * g + w + 1)
                if not (first and w < 2):
                    pe.wait_ge(exp_done, WIN * g + w - 1)
                t = win_kind(blk, odd, w)
                o = bST[w % 2][0:KROWS, 0:HEADS * NTOK]
                mm(o, kbd[buf][:, w, :], qexp[buf][:, w, :, :].rearrange("p h n -> p (h n)"), True, False)
                mm(o, dup_r[0:KROWS, 0:KROWS], p["bt"][:, t, :], False, False)
                mm(o, sel_r[:, w, 0:KROWS], rx[:, :, :].rearrange("p h n -> p (h n)"), False, True)\
                    .then_inc(st_ready, 1)

            def pv(g, w, buf, first):
                pe.wait_ge(exp_done, WIN * g + w + 1)
                if w == 0:
                    pe.wait_ge(v_done, 2 * g + 2)
                if w in (0, 4) and not first:
                    pe.wait_ge(rec_done, 2 * g - 1 + w // 4)
                for h in range(HEADS):
                    hh, h4 = h // 4, h % 4
                    c0 = (w % 4) * NROWS + hh * NTOK
                    last = mm(bO[w // 4][32 * h4:32 * h4 + 32, c0:c0 + NTOK], vbd[buf][:, w * HEADS + h, :],
                              pt[w % 4][:, h * NTOK:(h + 1) * NTOK])
                last.then_inc(av_ready, 1)

            def den(g, part):
                pe.wait_ge(osb_done, 2 * g + part + 1)
                mm(bO[part][:, 0:4 * NROWS], dsel[:, :], osb[part][:, :]).then_inc(den_ready, 1)

            def proj(p, g):
                pe.wait_ge(att_done, 2 * g + 2)
                for hh in range(2):
                    last = mm(bG[0][:, 0:TOK], p["wph"][hh][:, :], att[:, :, hh * NTOK:(hh + 1) * NTOK], hh == 0, hh == 1)
                last.then_inc(proj_ready, 1)

            def step(p, blk, g, u, first, more, more2):
                G = HALVES * blk + g
                nb = (u + 1) % 2
                f = first and blk == 0

                def ahead(*wins):
                    if more:
                        for w in wins:
                            scores(p, blk, nb, G + 1, w)

                scores_t(p, blk, u, G, 0, u, f)
                if not first:
                    den(G - 1, 1)
                scores_t(p, blk, u, G, 1, u, f)
                pv(G, 0, u, f)
                if more:
                    f_qk(p, G + 1, nb)
                scores_t(p, blk, u, G, 2, u, f)
                pv(G, 1, u, f)
                if not first:
                    proj(p, G - 1)
                scores_t(p, blk, u, G, 3, u, f)
                if more2:
                    f_xc(blk, G + 2, True)
                if more and not first:
                    pe.wait_ge(res_done, G)
                ahead(0)
                pv(G, 2, u, f)
                if more:
                    f_v(p, nb, range(WIN))
                if more2:
                    pe.wait_ge(q_done, 3 * G + 6)
                    f_var(G + 2)
                scores_t(p, blk, u, G, 4, u, f)
                ahead(1)
                pv(G, 3, u, f)
                ahead(2)
                scores_t(p, blk, u, G, 5, u, f)
                ahead(3)
                pv(G, 4, u, f)
                ahead(4)
                den(G, 0)
                ahead(5)
                scores_t(p, blk, u, G, 6, u, f)
                ahead(6)
                pv(G, 5, u, f)
                ahead(7)
                scores_t(p, blk, u, G, 7, u, f)
                if more:
                    maxt(G + 1)
                pv(G, 6, u, f)
                pv(G, 7, u, f)

            for blk in range(2):
                base = HALVES * blk
                p = P[blk]
                if blk:
                    pe.wait_ge(relay_done, PAIRS)
                else:
                    pe.wait_ge(s_tpcp, PAIRS * WROW)
                pe.wait_ge(s_btab, blk + 1)
                f_xc(blk, base)
                f_var(base)
                f_qk(p, base, 0)
                f_v(p, 0, range(WIN))
                pe.wait_ge(q_done, 3 * base + 3)
                f_xc(blk, base + 1, True)
                f_var(base + 1)
                for w in range(WIN):
                    scores(p, blk, 0, base, w)
                maxt(base)
                step(p, blk, 0, 0, True, True, True)
                step(p, blk, 1, 1, False, True, True)
                with pe.Fori(1, PAIRS - 1) as it:
                    for u in range(2):
                        step(p, blk, it * 2 + u, u, False, True, True)
                step(p, blk, HALVES - 2, 0, False, True, False)
                step(p, blk, HALVES - 1, 1, False, False, False)
                G = base + HALVES - 1
                den(G, 1)
                proj(p, G)
                pe.wait_ge(res_done, G + 1)

                def m_xc(g):
                    pe.wait_ge(mz_done, base + g)
                    mm(PS[0][:, 0:TOK], centre[:, :], xcols(blk, g)).then_inc(mxc, 1)

                def m_var(g):
                    pe.wait_ge(msq, base + g + 1)
                    pe.wait_ge(mvar_used, base + g)
                    mm(PS[1][:, 0:TOK], avg64[:, :], sq[:, :]).then_inc(mvar, 1)

                def fc1(g, c):
                    if c == 0:
                        pe.wait_ge(mz_done, base + g + 1)
                    if c < 2:
                        pe.wait_ge(gelu_done, 4 * (base + g))
                    else:
                        pe.wait_ge(gelu_done, 4 * (base + g) + c - 1)
                    mm(PS[2 + c % 2][:, 0:TOK], p["f1"][:, c, :], z[:, :]).then_inc(fc1_ready, 1)

                def fc2(g, c):
                    if c == 0:
                        pe.wait_ge(mres_done, base + g)
                    pe.wait_ge(gelu_done, 4 * (base + g) + c + 1)
                    last = mm(PS[4][:, 0:TOK], p["f2"][:, c, :], hid[c], c == 0, c == 3)
                    if c == 3:
                        last.then_inc(fc2_ready, 1)

                def mstep(g, more):
                    fc1(g, 0)
                    fc1(g, 1)
                    if more:
                        m_xc(g + 1)
                    fc1(g, 2)
                    fc1(g, 3)
                    if more:
                        m_var(g + 1)
                    for c in range(4):
                        fc2(g, c)

                if blk:
                    pe.wait_ge(w_dve, WSTEP["sum0"])
                    mm(PS[7][:, 0:1], dup[:, :], wcol[:, SUM0:SUM0 + 1]).then_inc(w_pe, 1)
                m_xc(0)
                m_var(0)
                with pe.Fori(0, PAIRS - 1) as it:
                    for u in range(2):
                        mstep(it * 2 + u, True)
                mstep(HALVES - 2, True)
                mstep(HALVES - 1, False)

            pe.wait_ge(relay_done, 2 * PAIRS)

            def moments(n):
                pe.wait_ge(tt_done, n + 1)
                t = tsb[n % 2]
                mm(PS[7][:, 0:129], t[:, 0:128], t[:, 0:129], n == 0, n == PAIRS * TILES - 1).then_inc(cov_ready, 1)

            pe.wait_ge(w_dve, WSTEP["shift"])
            for n in range(PAIRS * TILES):
                if n >= 2:
                    pe.wait_ge(tt_done, n - 1)
                nc.tensor.transpose(PS[5 + n % 2][0:TILE, 0:128], XR[:, n * TILE:(n + 1) * TILE], ident[:, :])\
                    .then_inc(tt_ready, 1)
                if n >= 1:
                    moments(n - 1)
            moments(PAIRS * TILES - 1)

            pe.wait_ge(w_dve, WSTEP["fold2"])
            mm(PS[0][:, 0:CH + 1], dup[:, :], fold2[:, :]).then_inc(w_pe, 1)
            pe.wait_ge(w_dve, WSTEP["mom"])
            mm(PS[1][0:1, 0:128], mom[:, CH:CH + 1], ident[:, :]).then_inc(w_pe, 1)
            pe.wait_ge(w_dve, WSTEP["rows"])
            mm(PS[2][:, 0:CH], wrow[:, 0:128], wrow[:, 128:128 + CH]).then_inc(w_pe, 1)
            pe.wait_ge(w_dve, WSTEP["diag"])
            mm(PS[3][:, 0:1], gsum[:, :], wcol[:, DIAG:DIAG + 1]).then_inc(w_pe, 1)
            for i in range(WH_ITER):
                pe.wait_ge(w_dve, WSTEP[f"p{i - 1}" if i else "psig"])
                mm(PS[4][:, 0:256], psig[:, 0, :], psig[:, :, :].rearrange("p a c -> p (a c)")).then_inc(w_pe, 1)
                pe.wait_ge(w_dve, WSTEP[f"prod{i}"])
                mm(PS[5][:, 0:128], prod[:, 0, :], prod[:, 1, :]).then_inc(w_pe, 1)
            pe.wait_ge(w_dve, WSTEP["wfin"])
            mm(PS[6][0:TILE, 0:128], nmb[:, :], wfin[:, :], True, False)
            mm(PS[6][0:TILE, 0:128], ones1[:, :], bet[:, :], False, True).then_inc(w_pe, 1)

            for b in range(PAIRS):
                for part, (t0, tn) in enumerate(((0, 4), (4, 3))):
                    n = 2 * b + part
                    if n >= 4:
                        pe.wait_ge(o_done, n - 3)
                    for t in range(tn):
                        c0 = (b * TILES + t0 + t) * TILE
                        last = mm(PS[n % 4][0:TILE, 128 * t:128 * (t + 1)], XR[:, c0:c0 + TILE], wfin[:, :])
                    last.then_inc(o_ready, 1)


def constants():
    import numpy as np
    f = np.float32
    pw, pc = np.divmod(np.arange(128), CH)
    same_w = (pw[:, None] == pw[None, :])
    c = {}
    c["ident"] = np.eye(128, dtype=f)
    c["centre"] = (np.eye(128) - same_w / CH).astype(f)
    c["avg64"] = (same_w / CH).astype(f)
    c["dup"] = (pc[:, None] == pc[None, :]).astype(f)
    c["gsum"] = (same_w & (pc[:, None] // GROUP == pc[None, :] // GROUP)).astype(f)
    nw, nn = np.divmod(np.arange(NROWS), NTOK)
    fold = np.zeros((NROWS, 50), f)
    fold[np.arange(NROWS), nn] = 1
    c["fold"] = fold
    turn = np.zeros((NROWS, KROWS), f)
    turn[np.arange(NROWS), 64 * nw + NTOK - 1 - nn] = 1
    c["turn"] = turn
    c["wmask"] = np.stack([nw == 0, nw == 1], 1).astype(f)
    c["hmask"] = (pc[:, None] // HD == np.arange(HEADS)[None]).astype(f)
    win, rest = np.divmod(np.arange(128), 2 * HEADS)
    rw, rh = np.divmod(rest, HEADS)
    c["hmask2"] = (rh[:, None] == np.arange(HEADS)[None]).astype(f)
    sel = np.zeros((128, WIN, 128), f)
    for p in range(128):
        sel[p, win[p], 64 * rw[p]:64 * rw[p] + NTOK] = 1
    c["sel"] = sel.reshape(128, WIN * 128)
    d = np.zeros((128, 128), f)
    for h4 in range(4):
        for r in range(32):
            d[32 * h4 + 16 + (r // HD if r < 2 * HD else 0), 32 * h4 + r] = 1
    c["dsel"] = d
    r, q = np.divmod(np.arange(NTOK), WS)
    row = (r[:, None] >= WS - SHIFT) != (r[None] >= WS - SHIFT)
    col = (q[:, None] >= WS - SHIFT) != (q[None] >= WS - SHIFT)
    m = np.stack([np.zeros((NTOK, NTOK), bool), col, row, row | col], 1) * f(-100)
    maskn, maskt = np.zeros((NROWS, 4, NTOK), f), np.zeros((KROWS, 4, NTOK), f)
    for w in range(2):
        maskn[NTOK * w:NTOK * w + NTOK] = m
        maskt[64 * w:64 * w + NTOK] = m
    c["maskn"], c["maskt"] = maskn.reshape(NROWS, -1), maskt.reshape(KROWS, -1)
    return c


def kernel(**inputs):
    import numpy as _np
    import concourse.bacc as _bacc
    from concourse.bass_utils import run_bass_kernel_spmd as _run

    nc = _bacc.Bacc("TRN2", target_bir_lowering=False, num_devices=1)
    arrays = {}

    def put(name, a):
        a = _np.ascontiguousarray(a)
        arrays[name] = a
        return nc.dram_tensor(name, a.shape, mybir.dt.from_np(a.dtype), kind="ExternalInput").ap()

    x = put("x_dram", inputs["x"])
    par = [{n: put(f"{n}{k}_dram", inputs[f"L0_conv_{n}{k}"]) for n in PARAMS} for k in range(2)]
    gamma, beta = put("gamma_dram", inputs["L1_conv_gamma"]), put("beta_dram", inputs["L1_conv_beta"])
    con = {n: put(f"c_{n}_dram", a) for n, a in constants().items()}
    out = nc.dram_tensor("out_dram", (IMAGES, SIDE, SIDE, CH), F32, kind="ExternalOutput").ap()
    build(nc, x, par, gamma, beta, con, out)
    r = _run(nc, [arrays], core_ids=[0])
    return r.results[0]["out_dram"]
```

```python
import concourse.bass as bass
from concourse import mybir
from contextlib import ExitStack

F32 = mybir.dt.float32
F32R = mybir.dt.float32r
I32 = mybir.dt.int32
ACT = mybir.ActivationFunctionType
ALU = mybir.AluOpType
AX = mybir.AxisListType

IMAGES, SIDE, CH, HEADS, WS, SHIFT = 16, 28, 64, 8, 7, 3
HD = CH // HEADS
NTOK = WS * WS
WROW = SIDE // WS
PAIRS = IMAGES // 2
HALVES = 2 * PAIRS
WIN = 2 * WROW
TOK = WIN * NTOK
IMG_TOK = SIDE * SIDE
KROWS = 64 + NTOK
NROWS = 2 * NTOK
TILE = 4 * SIDE
TILES = IMG_TOK // TILE
PAIR_COLS = TILES * 128
LN_EPS = 1.001e-05
WH_EPS = 1e-05
WH_ITER = 5
GROUP = 16
THIRD = 3.0 / 8.0
MAGIC = float(0x5F3759DF)
NLINK = 8

VECTORS = ['ln1_g', 'ln1_b', 'ln2_g', 'ln2_b', 'qkv_b', 'proj_b', 'fc2_b', 'fc1_b']

CON_AT, CON_COLS = {}, 0
for _name, _n in (("ident", 128), ("centre", 128), ("avg64", 128), ("dup", 128), ("gsum", 128), ("dsel", 128),
                  ("perm0", 128), ("perm1", 128), ("fold", 50), ("spread", NROWS), ("turn", KROWS), ("wmask", 2),
                  ("hmask", HEADS), ("hmask2", HEADS), ("nmask", 2), ("maskn", 4 * NTOK), ("maskt", 4 * NTOK)):
    CON_AT[_name] = (CON_COLS, _n)
    CON_COLS += _n
NRAW = 12 * CH
NVEC = 13
WGROUPS = ((0, 4), (4, 3))
XGROUPS = ((0, 1), (1, 4), (4, PAIRS))


def build(nc, x, par, gamma, beta, con, out):
    ctx = ExitStack()
    with ctx:
        def sb(name, shape, dt=F32):
            return ctx.enter_context(nc.sbuf_tensor(name, shape, dt))

        def sem(name):
            return ctx.enter_context(nc.semaphore(name))

        XW = [sb("XW0", [128, HALVES * TOK]), sb("XW1", [128, HALVES * TOK])]
        qexpb = sb("qexp", [128, 2, WIN, HEADS, NTOK])
        qexp = [qexpb[:, i] for i in range(2)]
        qflat = qexpb[:].rearrange("p a w h n -> p (a w h n)")
        pair_tok = [XW[1][0:TILE, b * PAIR_COLS:(b + 1) * PAIR_COLS] for b in range(PAIRS - 1)]
        pair_tok.append(qflat[0:TILE, 0:PAIR_COLS])
        XR = XW[0]
        conb = sb("conb", [128, CON_COLS])

        def con_view(name, rows=128):
            lo, n = CON_AT[name]
            return conb[0:rows, lo:lo + n]

        ident = con_view("ident")
        centre = con_view("centre")
        avg64 = con_view("avg64")
        dup = con_view("dup")
        gsum = con_view("gsum")
        dsel = con_view("dsel")
        perm = [con_view(f"perm{i}") for i in range(2)]
        fold = con_view("fold", NROWS)
        spread = con_view("spread", NTOK)
        turn = con_view("turn", NTOK)
        wmask = con_view("wmask", NROWS)
        hmask = con_view("hmask")
        hmask2 = con_view("hmask2")
        nmask = con_view("nmask")
        maskn = con_view("maskn", NROWS).rearrange("p (k m) -> p k m", k=4)
        maskt = con_view("maskt", KROWS).rearrange("p (k m) -> p k m", k=4)
        ident_r = sb("ident_r", [128, 128], F32R)
        centre_r = sb("centre_r", [128, 128], F32R)
        dup_r = sb("dup_r", [128, 128], F32R)
        dsel_r = sb("dsel_r", [128, 128], F32R)
        fold_r = sb("fold_r", [NROWS, 50], F32R)
        hidb = sb("hid", [128, 4, TOK])
        hid = [hidb[:, i] for i in range(4)]
        sel_f = hidb[:].rearrange("p a b -> p (a b)")[:, 0:WIN * 128]
        sel_r = sb("sel_r", [128, WIN, 128], F32R)
        G1, B1, G2, B2, QB, KB, VB, PB, F2B, FB = 0, 1, 2, 3, 4, 5, 6, 7, 8, 9
        vecb = sb("vecb", [128, 2, NVEC])
        P = []
        for k in range(2):
            P.append(dict(
                wq=sb(f"wq{k}", [128, 128]), wk=sb(f"wk{k}", [128, 128]),
                wv2=sb(f"wv2{k}", [128, CH]),
                wph=sb(f"wph{k}", [128, 2, 128]),
                f1=sb(f"f1{k}", [128, 4, 128]), f2=sb(f"f2{k}", [128, 4, 128]),
                vec=vecb[:, k, :],
                bn=sb(f"bn{k}", [NROWS, 4 if k else 1, HEADS * NTOK], F32R),
                bt=sb(f"bt{k}", [KROWS, 4 if k else 1, HEADS * NTOK], F32R)))
        epsc = sb("epsc", [128, 1])
        xh = sb("xh", [128, TOK], F32R)
        xl = sb("xl", [128, TOK], F32R)
        sq = sb("sq", [128, TOK])
        lv = [sb(f"lv{i}", [128, TOK]) for i in range(2)]
        ly = sb("ly", [128, TOK])
        lt = sb("lt", [128, TOK])
        z = [sb(f"z{i}", [128, TOK]) for i in range(2)]
        qbd = sb("qbd", [128, WIN, NROWS], F32R)
        kexp = sb("kexp", [128, WIN, HEADS, NTOK], F32R)
        qsb = sb("qsb", [128, TOK])
        ksb = sb("ksb", [128, TOK])
        kbd = [sb(f"kbd{i}", [128, WIN, KROWS]) for i in range(2)]
        vbd = [sb(f"vbd{i}", [KROWS, WIN * HEADS, 32]) for i in range(2)]
        nmax = sb("nmax", [NROWS, WIN, HEADS])
        nmaxw = sb("nmaxw", [NROWS, WIN, 2, HEADS], F32R)
        rx = sb("rx", [128, HEADS, NTOK], F32R)
        pt = [sb(f"pt{i}", [KROWS, HEADS * NTOK]) for i in range(4)]
        osb = [sb(f"osb{i}", [128, 4 * NROWS]) for i in range(2)]
        osh = sb("osh", [128, 4 * NROWS], F32R)
        osl = sb("osl", [128, 4 * NROWS], F32R)
        rec = [sb(f"rec{i}", [128, 4 * NROWS]) for i in range(2)]
        att = sb("att", [128, WIN, NROWS])
        rawb = [osb[1][0:NTOK, :], rec[1][0:NTOK, :]]
        tabn = [osb[0][0:NROWS, :], sb("tabn1", [NROWS, HEADS * NTOK])]
        tabt = [rec[0][0:KROWS, :], sb("tabt1", [KROWS, HEADS * NTOK])]
        btmp = sb("btmp", [KROWS, HEADS * NTOK])
        wraw = [qflat[:, PAIR_COLS + k * NRAW:PAIR_COLS + (k + 1) * NRAW]
                for k in range(2)]
        tsb = [sb(f"tsb{i}", [TILE, 4, 2, CH + 1]) for i in range(2)]
        wcol = sb("wcol", [128, 8])
        SUM0, SHIFTC, NMEAN, DIAG, TRACE, RTRACE, RSQ, EXPO = range(8)
        wrow = lt[0:1, 128:384]
        fold2 = sb("fold2", [128, CH + 1])
        mom = sb("mom", [128, CH + 1])
        momc = ly[:, TILE:TILE + CH]
        wbuf = kbd[0][:].rearrange("p a b -> p (a b)")
        psig = wbuf[:, 0:256].rearrange("p (a c) -> p a c", a=2)
        prod = wbuf[:, 256:512].rearrange("p (a c) -> p a c", a=2)
        cov, wtmp, wfin = (wbuf[:, 512 + 128 * i:640 + 128 * i] for i in range(3))
        nmb = ly[:, 0:TILE]
        ones1 = sb("ones1", [1, TILE])
        gam = sb("gam", [128, CH])
        bet = sb("bet", [1, 128])
        biasb = lt[0:TILE, 0:128]
        PS = [ctx.enter_context(nc.psum_tensor(f"PS{i}", [128, 512], F32)) for i in range(8)]
        bST, bO, bG = PS[1:3], PS[3:5], PS[5:8]
        bS = [PS[0], bG[0]]
        mX, mV, mF1, mF2 = [PS[6], PS[0]], PS[7], PS[1:3], PS[3]

        s_stat = sem("s_stat")
        s_ident, s_con, s_par, s_bias, s_gb = sem("s_ident"), sem("s_con"), sem("s_par"), sem("s_bias"), sem("s_gb")
        s_xin = [sem(f"s_xin{i}") for i in range(len(XGROUPS))]
        s_zero = sem("s_zero")
        s_zero_q = sem("s_zero_q")
        s_round = sem("s_round")
        s_tp, s_tpcp = sem("s_tp"), sem("s_tpcp")
        s_fold, s_prep = sem("s_fold"), sem("s_prep")
        s_btab, tab_link = sem("s_btab"), sem("tab_link")
        s_turn = sem("s_turn")
        z_done, mz_done = sem("z_done"), sem("mz_done")
        w_link = sem("w_link")
        xc_ready, sq_done, var_ready, var_used, ln_link = (
            sem("xc_ready"), sem("sq_done"), sem("var_ready"), sem("var_used"), sem("ln_link"))
        xh_done, xl_done = sem("xh_done"), sem("xl_done")
        q_ready, k_ready, v_ready, s_ready, mxt_ready, st_ready, av_ready, den_ready, proj_ready = (
            sem("q_ready"), sem("k_ready"), sem("v_ready"), sem("s_ready"), sem("mxt_ready"), sem("st_ready"),
            sem("av_ready"), sem("den_ready"), sem("proj_ready"))
        q_done, k_done, v_done, exp_done, osb_done = (
            sem("q_done"), sem("k_done"), sem("v_done"), sem("exp_done"), sem("osb_done"))
        kexp_done, max_done, nmaxw_done, rx_done, rec_done, res_done = (
            sem("kexp_done"), sem("max_done"), sem("nmaxw_done"), sem("rx_done"), sem("rec_done"), sem("res_done"))
        osh_done, osl_done = sem("osh_done"), sem("osl_done")
        qexp_done, att_done = sem("qexp_done"), sem("att_done")
        mxc, msq, mvar, mvar_used, mlink = sem("mxc"), sem("msq"), sem("mvar"), sem("mvar_used"), sem("mlink")
        fc1_ready, gelu_done, fc2_ready, mres_done = (
            sem("fc1_ready"), sem("gelu_done"), sem("fc2_ready"), sem("mres_done"))
        relay_done = sem("relay_done")
        tt_ready, tt_done, cov_ready = sem("tt_ready"), sem("tt_done"), sem("cov_ready")
        w_pe, w_dve, w_pool = sem("w_pe"), sem("w_dve"), sem("w_pool")
        o_ready, o_done, s_out = sem("o_ready"), sem("o_done"), sem("s_out")

        def win_kind(blk, half_odd, win):
            if blk == 0:
                return 0
            return (1 if win % WROW == WROW - 1 else 0) + (2 if half_odd and win >= WROW else 0)

        def xcols(blk, g):
            return XW[blk][:, bass.ds(g * TOK, TOK)]

        NSPLIT = HALVES - 2
        NPREP = 6
        NCON, NPAR = 2, 3
        WSTEP = {n: i + 1 for i, n in enumerate(
            ["sum0", "shift", "fold2", "mom", "rows", "diag", "trace", "psig", "p0"]
            + [f"prod{i}" if j == 0 else f"p{i}" for i in range(1, WH_ITER) for j in range(2)]
            + ["wfin", "biasb"])}
        PSTEP = {n: i + 1 for i, n in enumerate(
            ["shift", "mom", "row", "outer", "trace"]
            + [f"prod{i}" if j == 0 else f"p{i}" for i in range(1, WH_ITER) for j in range(2)] + ["bias"])}
        block = ctx.enter_context(nc.Block())

        @block.sync
        def _(sp):
            lo, n = CON_AT["ident"]
            sp.dma_start(conb[:, lo:lo + n], con["all"][:, lo:lo + n]).then_inc(s_ident, 16)
            for i, (b0, b1) in enumerate(XGROUPS):
                for b in range(b0, b1):
                    for w in range(2):
                        src = x[b + PAIRS * w].rearrange("r q c -> (r q) c").rearrange("(p t) c -> p t c", p=TILE)
                        sp.dma_start(pair_tok[b].rearrange("p (t k) -> p t k", k=128)[:, :, CH * w:CH * w + CH], src)\
                            .then_inc(s_xin[i], 16)
            for k in range(2):
                for a in range(WS):
                    sp.dma_start(rawb[k][WS * a:WS * a + WS, :].rearrange("p (m s) -> p m s", m=WS),
                                 bass.AP(par["bias_tab"][k].tensor, a * 13 * HEADS,
                                         [[HEADS, WS], [13 * HEADS, WS], [1, WS * HEADS]])).then_inc(s_bias, 16)
            for b in range(PAIRS):
                sp.wait_ge(o_done, 2 * (b + 1))
                for w in range(2):
                    dst = out[b + PAIRS * w].rearrange("r q c -> (r q c)").rearrange("(p k) -> p k", p=TILE)
                    sp.dma_start(dst, pair_tok[b].rearrange("p (w k) -> p w k", w=2)[:, w, :]).then_inc(s_out, 16)
            sp.wait_ge(s_out, 16 * 2 * PAIRS)

        def pool_relay(pool, blk, b):
            src = XW[blk][:, bass.ds(b * 2 * TOK, 2 * TOK)].rearrange("p (i j r c) -> p i j r c", i=WROW, j=WROW, r=WS)
            if blk == 0:
                dst = XW[1][:, bass.ds(b * 2 * TOK, 2 * TOK)].rearrange("p (i j r c) -> p i j r c", i=WROW, j=WROW, r=WS)
                far = WS - SHIFT
                last = None
                for i in range(WROW):
                    for ro, rn, ri, si in ((0, far, SHIFT, i), (far, SHIFT, 0, (i + 1) % WROW)):
                        for jo, jn, co, cn, ji, ci in ((0, WROW, 0, far, 0, SHIFT),
                                                       (0, WROW - 1, far, SHIFT, 1, 0),
                                                       (WROW - 1, 1, far, SHIFT, 0, 0)):
                            last = nc.gpsimd.tensor_copy(
                                dst[:, i, jo:jo + jn, ro:ro + rn, co:co + cn],
                                src[:, si, ji:ji + jn, ri:ri + rn, ci:ci + cn])
                last.then_inc(relay_done, 1)
            else:
                dst = XR[:, bass.ds(b * 2 * TOK, 2 * TOK)].rearrange("p (y q) -> p y q", q=SIDE)
                last = None
                for i in range(WROW):
                    if i % 2 == 0:
                        pool.wait_ge(mres_done, b * 2 + HALVES + i // 2 + 1)
                    rows = ((0, WS, WS * i + SHIFT),) if i < WROW - 1 else \
                        ((0, WS - SHIFT, WS * i + SHIFT), (WS - SHIFT, SHIFT, 0))
                    for r0, rn, y0 in rows:
                        for j in range(WROW):
                            cols = ((0, WS, WS * j + SHIFT),) if j < WROW - 1 else \
                                ((0, WS - SHIFT, WS * j + SHIFT), (WS - SHIFT, SHIFT, 0))
                            for c0, cn, q0 in cols:
                                last = nc.gpsimd.tensor_tensor(
                                    dst[:, y0:y0 + rn, q0:q0 + cn], src[:, i, j, r0:r0 + rn, c0:c0 + cn],
                                    wcol[:, SHIFTC:SHIFTC + 1].rearrange("p (a b) -> p a b", a=1)
                                    .to_broadcast([128, rn, cn]), ALU.subtract)
                last.then_inc(relay_done, 1)

        @block.gpsimd
        def _(pool):
            for k in range(2):
                for name in ("wq", "wk"):
                    nc.gpsimd.memset(P[k][name][:, :], 0.0)
                for name in ("f1", "f2"):
                    nc.gpsimd.memset(P[k][name][:, :, :], 0.0)
            nc.gpsimd.memset(wcol[:, EXPO:EXPO + 1], -0.5).then_inc(s_zero, 1)
            for i in range(2):
                nc.gpsimd.memset(kbd[i][:, :, :], 0.0)
                nc.gpsimd.memset(vbd[i][:, :, :], 0.0)
            nc.gpsimd.memset(ones1[:, :], 1.0)
            for i in range(2):
                nc.gpsimd.memset(tsb[i][:, :, :, CH:CH + 1], 1.0)
            nc.gpsimd.memset(epsc[:, :], LN_EPS).then_inc(s_zero, 1)
            pool.wait_ge(s_zero, 2)
            for i in range(2):
                for w in range(2):
                    last = nc.gpsimd.memset(vbd[i][64 * w:64 * w + NTOK, :, 16 + w:17 + w], 1.0)
            last.then_inc(s_zero, 1)

            def qexpand(g1, buf):
                pool.wait_ge(q_done, 3 * g1 + 3)
                for w in range(WIN):
                    nc.gpsimd.tensor_tensor(
                        qexp[buf][:, w, :, :],
                        qsb[:, w * NTOK:(w + 1) * NTOK].rearrange("p (a n) -> p a n", a=1).to_broadcast([128, HEADS, NTOK]),
                        hmask[:, :].rearrange("p (h a) -> p h a", a=1).to_broadcast([128, HEADS, NTOK]),
                        ALU.mult).then_inc(qexp_done, 1)

            def den_low(g, part, first=False):
                pool.wait_ge(osh_done, 2 * g + part + 1)
                pool.wait_ge(osb_done, 2 * g + part + 1)
                if not first:
                    pool.wait_ge(den_ready, 2 * g + part)
                nc.gpsimd.tensor_tensor(osl[:, :], osb[part][:, :], osh[:, :].bitcast(F32), ALU.subtract)\
                    .then_inc(osl_done, 1)

            def x_low(blk, g):
                pool.wait_ge(xh_done, NSPLIT * blk + g + 1)
                pool.wait_ge(xc_ready, HALVES * blk + g + 2)
                nc.gpsimd.tensor_tensor(xl[:, :], xcols(blk, g + 2), xh[:, :].bitcast(F32), ALU.subtract)\
                    .then_inc(xl_done, 1)

            def attn(g, part):
                pool.wait_ge(rec_done, 2 * g + part + 1)
                if part == 0:
                    pool.wait_ge(proj_ready, g)
                nc.gpsimd.tensor_tensor(
                    att[:, 4 * part:4 * part + 4, :], osb[part][:, :].rearrange("p (a n) -> p a n", a=4),
                    rec[part][:, :].rearrange("p (a n) -> p a n", a=4), ALU.mult).then_inc(att_done, 1)

            def step(base, g, u, first, more, more2):
                if not first:
                    den_low(base + g - 1, 1)
                    attn(base + g - 1, 0)
                if more2:
                    x_low(base // HALVES, g)
                if not first:
                    attn(base + g - 1, 1)
                if more:
                    if not first:
                        pool.wait_ge(st_ready, WIN * (base + g))
                    qexpand(base + g + 1, (u + 1) % 2)
                den_low(base + g, 0, first and base == 0)

            pool.wait_ge(s_con, 16 * NCON)
            for blk in range(2):
                base = HALVES * blk
                if blk:
                    pool.wait_ge(st_ready, WIN * base)
                qexpand(base, 0)
                step(base, 0, 0, True, True, True)
                step(base, 1, 1, False, True, True)
                with pool.Fori(1, PAIRS - 1) as it:
                    for u in range(2):
                        step(base, it * 2 + u, u, False, True, True)
                step(base, HALVES - 2, 0, False, True, False)
                step(base, HALVES - 1, 1, False, False, False)
                den_low(base + HALVES - 1, 1)
                attn(base + HALVES - 1, 0)
                attn(base + HALVES - 1, 1)
                if blk:
                    pool.wait_ge(w_dve, WSTEP["shift"])
                with pool.Fori(0, PAIRS) as it:
                    if blk == 0:
                        pool.wait_ge(mres_done, (it + 1) * 2)
                    pool_relay(pool, blk, it)
            pool.wait_ge(w_dve, WSTEP["trace"])
            nc.gpsimd.tensor_tensor(wcol[:, RSQ:RSQ + 1], wcol[:, TRACE:TRACE + 1], wcol[:, EXPO:EXPO + 1], ALU.pow)\
                .then_inc(w_pool, 1)

        @block.scalar
        def _(act):
            lo = CON_AT["centre"][0]
            mid = CON_AT["avg64"][0] + CON_AT["avg64"][1]
            act.dma_start(conb[:, lo:mid], con["all"][:, lo:mid]).then_inc(s_stat, 16)
            act.dma_start(conb[:, mid:CON_COLS], con["all"][:, mid:CON_COLS]).then_inc(s_con, 16)
            act.dma_start(vecb[:, :, :].rearrange("p k v -> p (k v)"), par["vec"]).then_inc(s_par, 16)
            for k in range(2):
                act.dma_start(wraw[k], par["w"][k]).then_inc(s_par, 16)
            act.dma_start(sel_f, con["sel"]).then_inc(s_con, 16)
            act.dma_start(gam[:, :], gamma.rearrange("a b c k -> (a b c) k").to_broadcast([128, CH])).then_inc(s_gb, 16)
            for w in range(2):
                act.dma_start(bet[:, CH * w:CH * w + CH], beta.rearrange("a b c k -> (a b c) k")).then_inc(s_gb, 16)

            def window_order(i):
                for b in range(*XGROUPS[i]):
                    dst = XW[0][:, b * IMG_TOK:(b + 1) * IMG_TOK]\
                        .rearrange("p (i j r c) -> p i r j c", i=WROW, j=WROW, r=WS)
                    for part, (t0, tn) in enumerate(WGROUPS):
                        n = 2 * b + part
                        act.wait_ge(s_tp, n + 1)
                        for t in range(tn):
                            src = PS[1 + n % 4][:, TILE * t:TILE * (t + 1)].rearrange("p (i r j) -> p i r j", i=WROW, r=WS)
                            last = nc.scalar.activation(dst[:, :, :, :, t0 + t], src, ACT.Copy)
                        last.then_inc(s_tpcp, 1)

            def square(g):
                act.wait_ge(xc_ready, g + 1)
                act.wait_ge(var_ready, g)
                nc.scalar.activation(sq[:, :], bG[2][:, 0:TOK], ACT.Square).then_inc(sq_done, 1)

            def variance(g, buf, first=False):
                act.wait_ge(var_ready, g + 1)
                if not first:
                    act.wait_ge(z_done, g - 1)
                nc.scalar.activation(lv[buf][:, :], bG[1][:, 0:TOK], ACT.Identity, bias=epsc[:, 0:1]).then_inc(var_used, 1)

            def x_high(blk, g):
                act.wait_ge(xc_ready, HALVES * blk + g + 2)
                act.wait_ge(xl_done, NSPLIT * blk + g)
                nc.scalar.activation(xh[:, :], xcols(blk, g + 2), ACT.Copy).then_inc(xh_done, 1)

            def evac_k(p, g1):
                act.wait_ge(k_ready, g1 + 1)
                act.wait_ge(kexp_done, HEADS * g1)
                act.wait_ge(k_done, 3 * g1)
                nc.scalar.activation(ksb[:, :], bG[2][:, 0:TOK], ACT.Identity, bias=p["vec"][:, KB:KB + 1])\
                    .then_inc(k_done, 1)

            def evac_q(p, g1):
                act.wait_ge(q_ready, g1 + 1)
                act.wait_ge(s_ready, WIN * g1)
                for w in range(2):
                    r = slice(64 * w, 64 * w + 64)
                    nc.scalar.activation(qbd[r, :, NTOK * w:NTOK * w + NTOK],
                                         bG[1][r, 0:TOK].rearrange("p (a n) -> p a n", n=NTOK),
                                         ACT.Identity, bias=p["vec"][r, QB:QB + 1]).then_inc(q_done, 1)
                act.wait_ge(qexp_done, WIN * g1)
                nc.scalar.activation(qsb[:, :], bG[1][:, 0:TOK], ACT.Identity, bias=p["vec"][:, QB:QB + 1])\
                    .then_inc(q_done, 1)

            def evac_kbd(g1, buf, prologue=False):
                if not prologue:
                    act.wait_ge(st_ready, WIN * (g1 - 1))
                act.wait_ge(k_done, 3 * g1 + 1)
                for w in range(2):
                    r = slice(64 * w, 64 * w + 64)
                    nc.scalar.activation(kbd[buf][r, :, 64 * w:64 * w + NTOK],
                                         ksb[r, :].rearrange("p (a n) -> p a n", n=NTOK), ACT.Copy)\
                        .then_inc(k_done, 1)

            def evac_v(g1, buf, prologue=False):
                act.wait_ge(v_ready, g1 + 1)
                if not prologue:
                    act.wait_ge(av_ready, WIN * (g1 - 1))
                for w in range(2):
                    nc.scalar.activation(vbd[buf][64 * w:64 * w + NTOK, :, HD * w:HD * w + HD],
                                         bG[0][64 * w:64 * w + NTOK, :].rearrange("p (a d) -> p a d", d=HD),
                                         ACT.Copy).then_inc(v_done, 1)

            def expo(g, w, first=False):
                act.wait_ge(st_ready, WIN * g + w + 1)
                if not (first and w < 4):
                    act.wait_ge(av_ready, WIN * g + w - 3)
                nc.scalar.activation(pt[w % 4][:, :], bST[w % 2][0:KROWS, 0:HEADS * NTOK], ACT.Exp)\
                    .then_inc(exp_done, 1)

            def o_copy(g, part, first=False):
                act.wait_ge(av_ready, WIN * g + 4 * part + 4)
                if not first:
                    act.wait_ge(att_done, 2 * (g - 1) + part + 1)
                nc.scalar.activation(osb[part][:, :], bO[part][:, 0:4 * NROWS], ACT.Copy).then_inc(osb_done, 1)
                if not (first and part == 0):
                    act.wait_ge(den_ready, 2 * g + part)
                    act.wait_ge(osl_done, 2 * g + part)
                nc.scalar.activation(osh[:, :], bO[part][:, 0:4 * NROWS], ACT.Copy).then_inc(osh_done, 1)

            def step(p, base, g, u, first, more, more2, tail=None):
                G = base + g
                nb = (u + 1) % 2
                f = first and base == 0
                expo(G, 0, f)
                expo(G, 1, f)
                if more2:
                    x_high(base // HALVES, g)
                if more:
                    evac_k(p, G + 1)
                    evac_q(p, G + 1)
                expo(G, 2, f)
                if more2:
                    square(G + 2)
                if more:
                    evac_kbd(G + 1, nb)
                if more2:
                    variance(G + 2, u)
                expo(G, 3, f)
                if tail:
                    tail[0]()
                if more:
                    evac_v(G + 1, nb)
                expo(G, 4)
                o_copy(G, 0, f)
                expo(G, 5)
                if tail:
                    tail[1]()
                expo(G, 6)
                expo(G, 7)
                o_copy(G, 1, f)

            def start(p, base):
                evac_k(p, base)
                evac_q(p, base)
                evac_kbd(base, 0, True)
                evac_v(base, 0, True)
                if base:
                    square(base + 1)
                    act.wait_ge(mz_done, base)
                    variance(base + 1, 1)

            window_order(0)
            act.wait_ge(s_zero, 3)
            square(0)
            variance(0, 0, True)
            window_order(1)
            square(1)
            variance(1, 1, True)
            window_order(2)
            act.wait_ge(s_tpcp, 2 * PAIRS)
            act.wait_ge(s_prep, NPREP)
            act.wait_ge(s_zero_q, 1)
            start(P[0], 0)
            for blk in range(2):
                base = HALVES * blk
                p = P[blk]
                step(p, base, 0, 0, True, True, True)
                step(p, base, 1, 1, False, True, True)
                with act.Fori(1, PAIRS - 1) as it:
                    for u in range(2):
                        step(p, base, it * 2 + u, u, False, True, True)
                def mstats(g, buf, first=False):
                    def msquare():
                        act.wait_ge(mxc, g + 1)
                        if not (blk == 0 and first and buf == 0):
                            act.wait_ge(mvar, g)
                        nc.scalar.activation(sq[:, :], mX[buf][:, 0:TOK], ACT.Square).then_inc(msq, 1)

                    def mvariance():
                        act.wait_ge(mvar, g + 1)
                        if first:
                            act.wait_ge(z_done, base + HALVES)
                        else:
                            act.wait_ge(mz_done, g - 1)
                        nc.scalar.activation(lv[buf][:, :], mV[:, 0:TOK], ACT.Identity, bias=epsc[:, 0:1])\
                            .then_inc(mvar_used, 1)
                    return msquare, mvariance

                def gelus(g, m, first=False):
                    for c in (2 * m, 2 * m + 1):
                        act.wait_ge(fc1_ready, 4 * g + c + 1)
                        if not first:
                            act.wait_ge(fc2_ready, g)
                        nc.scalar.activation(hid[c], mF1[c % 2][:, 0:TOK], ACT.Gelu,
                                             bias=p["vec"][:, FB + c:FB + c + 1]).then_inc(gelu_done, 1)

                def mstep(g, u, stats=None, first=False):
                    gelus(g, 0, first)
                    if stats:
                        stats[0]()
                    gelus(g, 1, first)
                    if stats:
                        stats[1]()

                def first_stats(u):
                    msquare, mvariance = mstats(base + u, u, True)
                    msquare()
                    mvariance()

                step(p, base, HALVES - 2, 0, False, True, False)
                step(p, base, HALVES - 1, 1, False, False, False,
                     tail=[lambda: first_stats(0), lambda: first_stats(1)])
                for u in range(2):
                    mstep(base + u, u, mstats(base + u + 2, u), first=blk == 0 and u == 0)
                with act.Fori(1, PAIRS - 1) as it:
                    for u in range(2):
                        mstep(base + it * 2 + u, u, mstats(base + it * 2 + u + 2, u))
                nxt = base + HALVES
                if blk == 0:
                    def next_variance():
                        act.wait_ge(mz_done, nxt - 1)
                        variance(nxt, 0, True)
                    mstep(nxt - 2, 0, [lambda: square(nxt), next_variance])
                else:
                    mstep(nxt - 2, 0)
                mstep(nxt - 1, 1)
                if blk == 0:
                    start(P[1], nxt)
            for b in range(PAIRS):
                for part, (t0, tn) in enumerate(WGROUPS):
                    n = 2 * b + part
                    act.wait_ge(tt_ready, n + 1)
                    if n >= 2:
                        act.wait_ge(cov_ready, n - 1)
                    nc.scalar.activation(tsb[part][:, 0:tn, :, 0:CH],
                                         PS[4 + part][0:TILE, 0:tn * 128].rearrange("p (t w c) -> p t w c", w=2, c=CH),
                                         ACT.Copy)\
                        .then_inc(tt_done, 1)

        @block.vector
        def _(dve):
            nc.vector.memset(qbd[:, :, :].bitcast(F32), 0.0).then_inc(s_zero_q, 1)
            dve.wait_ge(s_ident, 16)
            dve.wait_ge(s_stat, 16)
            dve.wait_ge(s_con, 16 * NCON)
            nc.vector.tensor_copy(centre_r[:, :], centre[:, :])
            nc.vector.tensor_copy(ident_r[:, :], ident[:, :])
            nc.vector.tensor_copy(dup_r[:, :], dup[:, :])
            nc.vector.tensor_copy(dsel_r[:, :], dsel[:, :])
            nc.vector.tensor_copy(fold_r[:, :], fold[:, :])
            nc.vector.tensor_copy(sel_r[:, :, :].rearrange("p a b -> p (a b)"), sel_f[:, :]).then_inc(s_round, 1)

            def chain(semaphore):
                count = [0]

                def link(ins):
                    count[0] += 1
                    ins.then_inc(semaphore, 1)
                    dve.wait_ge(semaphore, count[0])
                return link

            plink = chain(s_prep)

            def fold_weights(k):
                p = P[k]
                v = p["vec"]
                raw = wraw[k]
                if k == 0:
                    dve.wait_ge(s_zero, 1)
                dve.wait_ge(s_fold, 2 * k + 1)
                ps = PS[5 * k]
                plink(nc.vector.tensor_tensor(v[:, VB:VB + 1], ps[:, 2:3], v[:, VB:VB + 1], ALU.add))
                nc.vector.tensor_tensor(v[:, KB:KB + 1], ps[:, 1:2], v[:, KB:KB + 1], ALU.add)
                nc.vector.tensor_tensor(v[:, FB:FB + 4], ps[:, 3:7], v[:, FB:FB + 4], ALU.add)
                plink(nc.vector.tensor_tensor(v[:, QB:QB + 1], ps[:, 0:1], v[:, QB:QB + 1], ALU.add))
                nc.vector.tensor_scalar(v[:, QB:QB + 1], v[:, QB:QB + 1], HD ** -0.5, None, ALU.mult)
                for w in range(2):
                    r = slice(CH * w, CH * w + CH)
                    g1, g2 = v[r, G1:G1 + 1], v[r, G2:G2 + 1]
                    nc.vector.tensor_scalar(p["wq"][r, r], raw[r, 0:CH], g1, HD ** -0.5, ALU.mult, ALU.mult)
                    nc.vector.tensor_scalar(p["wk"][r, r], raw[r, CH:2 * CH], g1, None, ALU.mult)
                    nc.vector.tensor_scalar(p["f1"][r, :, r], raw[r, 4 * CH:8 * CH].rearrange("p (k j) -> p k j", k=4),
                                            g2, None, ALU.mult)
                    nc.vector.tensor_copy(p["f2"][r, :, r], raw[r, 8 * CH:12 * CH].rearrange("p (k j) -> p k j", k=4))
                nc.vector.tensor_scalar(p["wv2"][:, :], raw[:, 2 * CH:3 * CH], v[:, G1:G1 + 1], None, ALU.mult)
                for w in range(2):
                    nc.vector.tensor_scalar(p["wph"][:, :, CH * w:CH * w + CH],
                                            ps[:, CH:3 * CH].rearrange("p (a c) -> p a c", a=2),
                                            nmask[:, w:w + 1], None, ALU.mult)
                dve.wait_ge(s_fold, 2 * k + 2)
                plink(nc.vector.tensor_tensor(v[:, PB:PB + 1], PS[5 - 5 * k][:, 0:1], v[:, PB:PB + 1], ALU.add))

            tlink = chain(tab_link)

            def table_copies(k):
                dve.wait_ge(s_turn, k + 1)
                nc.vector.tensor_copy(tabn[k][:, :], PS[0][0:NROWS, 0:HEADS * NTOK])
                tlink(nc.vector.tensor_copy(tabt[k][:, :], PS[5][0:KROWS, 0:HEADS * NTOK]))

            def table(k, t):
                p = P[k]
                tlink(nc.vector.tensor_copy(
                    btmp[0:NROWS, :].rearrange("p (h m) -> p h m", h=HEADS),
                    tabn[k][:, :].rearrange("p (m h) -> p h m", h=HEADS)[:, :, ::-1]))
                tlink(nc.vector.tensor_tensor(
                    p["bn"][:, t, :].rearrange("p (h m) -> p h m", h=HEADS),
                    btmp[0:NROWS, :].rearrange("p (h m) -> p h m", h=HEADS),
                    maskn[:, t:t + 1, :].to_broadcast([NROWS, HEADS, NTOK]), ALU.add))
                tlink(nc.vector.tensor_tensor(
                    btmp[:, :].rearrange("p (h m) -> p h m", h=HEADS),
                    tabt[k][:, :].rearrange("p (m h) -> p h m", h=HEADS),
                    maskt[:, t:t + 1, :].to_broadcast([KROWS, HEADS, NTOK]), ALU.add))
                tlink(nc.vector.tensor_copy(p["bt"][:, t, :], btmp[:, :]))
                tlink(nc.vector.tensor_tensor(p["bt"][64:KROWS, t, :], btmp[64:KROWS, :],
                                              p["bt"][64:KROWS, t, :].bitcast(F32), ALU.subtract))

            def norm(g, buf, xps, used, link, done, zfree, after={}):
                dve.wait_ge(used, g + 1)
                if not (isinstance(g, int) and g == 0):
                    dve.wait_ge(done, g)
                n = [0]
                v = lv[buf]

                def ln(ins):
                    n[0] += 1
                    ins.then_inc(link, 1)
                    if n[0] in after:
                        after[n[0]]()
                    dve.wait_ge(link, NLINK * g + n[0])

                ln(nc.vector.tensor_scalar(ly[:, :].bitcast(I32), v[:, :].bitcast(I32), -0.5, MAGIC, ALU.mult, ALU.add))
                ln(nc.vector.tensor_tensor(lt[:, :], ly[:, :], ly[:, :], ALU.mult))
                ln(nc.vector.tensor_tensor(lt[:, :], lt[:, :], v[:, :], ALU.mult))
                ln(nc.vector.scalar_tensor_tensor(lt[:, :], lt[:, :], -10.0 / 3.0, lt[:, :], ALU.add, ALU.mult))
                ln(nc.vector.scalar_tensor_tensor(ly[:, :], lt[:, :], 5.0, ly[:, :], ALU.add, ALU.mult))
                ln(nc.vector.tensor_tensor(lt[:, :], ly[:, :], ly[:, :], ALU.mult))
                ln(nc.vector.scalar_tensor_tensor(lt[:, :], lt[:, :], -0.5 * THIRD ** 3, v[:, :], ALU.mult, ALU.mult))
                ln(nc.vector.scalar_tensor_tensor(ly[:, :], lt[:, :], 1.5 * THIRD, ly[:, :], ALU.add, ALU.mult))
                assert n[0] == NLINK
                zfree()
                nc.vector.tensor_tensor(z[buf][:, :], xps[:, 0:TOK], ly[:, :], ALU.mult).then_inc(done, 1)

            def anorm(g, buf, after={}, first=False):
                norm(g, buf, bG[2], var_used, ln_link, z_done,
                     lambda: None if first else dve.wait_ge(v_ready, g - 1), after)

            def kexpand(g1):
                dve.wait_ge(k_done, 3 * g1 + 1)
                dve.wait_ge(s_ready, WIN * g1)
                for h in range(HEADS):
                    nc.vector.tensor_scalar(kexp[:, :, h, :], ksb[:, :].rearrange("p (a n) -> p a n", n=NTOK),
                                            hmask[:, h:h + 1], None, ALU.mult).then_inc(kexp_done, 1)

            def rowmax(g1, w):
                dve.wait_ge(s_ready, WIN * g1 + w + 1)
                nc.vector.tensor_reduce(nmax[:, w, :], bS[w % 2][0:NROWS, 0:HEADS * NTOK].rearrange("p (h m) -> p h m", h=HEADS),
                                        AX.X, ALU.max, negate=True).then_inc(max_done, 1)

            def split_max(g1):
                dve.wait_ge(max_done, WIN * (g1 + 1))
                dve.wait_ge(mxt_ready, g1)
                for w in range(2):
                    nc.vector.tensor_scalar(nmaxw[:, :, w, :], nmax[:, :, :], wmask[:, w:w + 1], None, ALU.mult)\
                        .then_inc(nmaxw_done, 1)

            def spread_max(g1):
                dve.wait_ge(mxt_ready, g1 + 1)
                dve.wait_ge(st_ready, WIN * g1)
                nc.vector.tensor_tensor(
                    rx[:, :, :], bG[1][:, 0:NTOK].rearrange("p (a n) -> p a n", a=1).to_broadcast([128, HEADS, NTOK]),
                    hmask2[:, :].rearrange("p (h a) -> p h a", a=1).to_broadcast([128, HEADS, NTOK]),
                    ALU.mult).then_inc(rx_done, 1)

            def recip(g, part, first=False):
                dve.wait_ge(den_ready, 2 * g + part + 1)
                if not first:
                    dve.wait_ge(att_done, 2 * g + part - 1)
                nc.vector.reciprocal(rec[part][:, :], bO[part][:, 0:4 * NROWS]).then_inc(rec_done, 1)

            def residual(p, blk, base, g):
                dve.wait_ge(proj_ready, base + g + 1)
                nc.vector.scalar_tensor_tensor(xcols(blk, g), bG[0][:, 0:TOK], p["vec"][:, PB:PB + 1], xcols(blk, g),
                                               ALU.add, ALU.add).then_inc(res_done, 1)

            def step(p, blk, base, g, u, first, more, more2, second=False):
                G = base + g
                if not first:
                    for part in range(2):
                        recip(G - 1, part, second)
                if more:
                    kexpand(G + 1)
                if not first:
                    residual(p, blk, base, g - 1)
                if more2:
                    rowmax(G + 1, 0)
                    anorm(G + 2, u, {NLINK - 4 + w: (lambda w=w: rowmax(G + 1, w)) for w in range(1, 5)})
                    for w in range(5, WIN):
                        rowmax(G + 1, w)
                elif more:
                    for w in range(WIN):
                        rowmax(G + 1, w)
                if more:
                    split_max(G + 1)
                    spread_max(G + 1)

            def start(base):
                for w in range(WIN):
                    rowmax(base, w)
                split_max(base)
                spread_max(base)
                if base:
                    dve.wait_ge(fc1_ready, 4 * base)
                    anorm(base + 1, 1)

            anorm(0, 0, first=True)
            fold_weights(0)
            fold_weights(1)
            anorm(1, 1, first=True)
            table_copies(0)
            table_copies(1)
            table(0, 0)
            nc.vector.memset(lt[:, 0:1], 0.0).then_inc(s_btab, 1)
            kexpand(0)
            start(0)
            for blk in range(2):
                base = HALVES * blk
                p = P[blk]

                def mnorm(g, buf, after={}, first=False):
                    norm(g, buf, mX[buf], mvar_used, mlink, mz_done,
                         lambda: dve.wait_ge(v_ready, base + HALVES) if first else dve.wait_ge(fc1_ready, 4 * (g - 1)),
                         after)

                def mresidual(g):
                    dve.wait_ge(fc2_ready, base + g + 1)
                    nc.vector.scalar_tensor_tensor(xcols(blk, g), mF2[:, 0:TOK], p["vec"][:, F2B:F2B + 1],
                                                   xcols(blk, g), ALU.add, ALU.add).then_inc(mres_done, 1)

                step(p, blk, base, 0, 0, True, True, True)
                if blk == 0:
                    table(1, 0)
                step(p, blk, base, 1, 1, False, True, True, second=blk == 0)
                if blk == 0:
                    table(1, 1)
                with dve.Fori(1, PAIRS - 1) as it:
                    for u in range(2):
                        step(p, blk, base, it * 2 + u, u, False, True, True)
                step(p, blk, base, HALVES - 2, 0, False, True, False)
                if blk == 0:
                    table(1, 2)
                step(p, blk, base, HALVES - 1, 1, False, False, False)
                dve.wait_ge(z_done, base + HALVES)
                mnorm(base, 0, first=True)
                for part in range(2):
                    recip(base + HALVES - 1, part)
                mnorm(base + 1, 1, first=True)
                if blk == 0:
                    table(1, 3)
                    nc.vector.memset(lt[:, 0:1], 0.0).then_inc(s_btab, 1)
                residual(p, blk, base, HALVES - 1)
                if blk:
                    dve.wait_ge(res_done, 2 * HALVES)
                    nc.vector.tensor_reduce(wcol[:, SUM0:SUM0 + 1], XW[1][:, 0:TOK], AX.X, ALU.add).then_inc(w_dve, 1)
                for u in range(2):
                    mnorm(base + u + 2, u, {6: lambda: mresidual(u)})
                if blk:
                    dve.wait_ge(w_pe, PSTEP["shift"])
                    nc.vector.scalar_tensor_tensor(wcol[:, SHIFTC:SHIFTC + 1], PS[4][:, 0:1], 1.0 / (2 * TOK),
                                                   p["vec"][:, F2B:F2B + 1], ALU.mult, ALU.add).then_inc(w_dve, 1)
                with dve.Fori(1, PAIRS - 1) as it:
                    for u in range(2):
                        mnorm(base + it * 2 + u + 2, u, {6: lambda: mresidual(it * 2 + u)})
                if blk == 0:
                    nxt = base + HALVES
                    dve.wait_ge(fc1_ready, 4 * (nxt - 1))
                    dve.wait_ge(mz_done, nxt)
                    anorm(nxt, 0, {6: lambda: mresidual(HALVES - 2)})
                    kexpand(nxt)
                    mresidual(HALVES - 1)
                    start(nxt)
                else:
                    mresidual(HALVES - 2)
                    mresidual(HALVES - 1)

            def wdone(ins, name):
                ins.then_inc(w_dve, 1)
                done.append(name)
                assert WSTEP[name] == len(done)
                dve.wait_ge(w_dve, WSTEP[name])

            done = ["sum0", "shift"]
            N = float(IMAGES * IMG_TOK)
            dve.wait_ge(cov_ready, 2 * PAIRS)
            wdone(nc.vector.tensor_copy(fold2[:, :], PS[7][:, 0:CH + 1]), "fold2")
            dve.wait_ge(w_pe, PSTEP["mom"])
            wdone(nc.vector.tensor_copy(mom[:, :], PS[0][:, 0:CH + 1]), "mom")
            dve.wait_ge(w_pe, PSTEP["row"])
            nc.vector.tensor_copy(wrow[:, 0:128], PS[1][0:1, 0:128])
            nc.vector.tensor_scalar(wcol[:, NMEAN:NMEAN + 1], mom[:, CH:CH + 1], -1.0 / N, None, ALU.mult)
            wdone(nc.vector.tensor_scalar(wrow[:, 128:256], PS[1][0:1, 0:128], -1.0 / N, None, ALU.mult), "rows")
            dve.wait_ge(w_pe, PSTEP["outer"])
            wlink = chain(w_link)
            wlink(nc.vector.tensor_tensor(momc[:, :], PS[2][:, 0:CH], mom[:, 0:CH], ALU.add))
            wlink(nc.vector.scalar_tensor_tensor(
                cov[:, :].rearrange("p (w c) -> p w c", w=2),
                momc[:, :].rearrange("p (a c) -> p a c", a=1).to_broadcast([128, 2, CH]), (1.0 - WH_EPS) / (N - 1.0),
                gsum[:, :].rearrange("p (w c) -> p w c", w=2), ALU.mult, ALU.mult))
            wlink(nc.vector.scalar_tensor_tensor(cov[:, :], ident[:, :], WH_EPS, cov[:, :], ALU.mult, ALU.add))
            wlink(nc.vector.tensor_tensor(wtmp[:, :], cov[:, :], ident[:, :], ALU.mult))
            wdone(nc.vector.tensor_reduce(wcol[:, DIAG:DIAG + 1], wtmp[:, :], AX.X, ALU.add), "diag")
            dve.wait_ge(w_pe, PSTEP["trace"])
            nc.vector.tensor_copy(wcol[:, TRACE:TRACE + 1], PS[3][:, 0:1])
            wdone(nc.vector.reciprocal(wcol[:, RTRACE:RTRACE + 1], PS[3][:, 0:1]), "trace")
            wdone(nc.vector.tensor_scalar(psig[:, 1, :], cov[:, :], wcol[:, RTRACE:RTRACE + 1], -0.5, ALU.mult, ALU.mult),
                  "psig")
            wdone(nc.vector.scalar_tensor_tensor(psig[:, 0, :], ident[:, :], 1.5, psig[:, 1, :], ALU.mult, ALU.add), "p0")
            for i in range(1, WH_ITER):
                dve.wait_ge(w_pe, PSTEP[f"prod{i}"])
                wdone(nc.vector.tensor_copy(prod[:, :, :].rearrange("p a c -> p (a c)"), PS[4][:, 0:256]), f"prod{i}")
                dve.wait_ge(w_pe, PSTEP[f"p{i}"])
                wdone(nc.vector.scalar_tensor_tensor(psig[:, 0, :], psig[:, 0, :], 1.5, PS[5][:, 0:128],
                                                     ALU.mult, ALU.add), f"p{i}")
            dve.wait_ge(w_pool, 1)
            dve.wait_ge(s_gb, 16 * 3)
            nc.vector.tensor_copy(nmb[:, :], wcol[:, NMEAN:NMEAN + 1].to_broadcast([128, TILE]))
            wdone(nc.vector.scalar_tensor_tensor(
                wfin[:, :].rearrange("p (w c) -> p w c", w=2), psig[:, 0, :].rearrange("p (w c) -> p w c", w=2),
                wcol[:, RSQ:RSQ + 1], gam[:, :].rearrange("p (a c) -> p a c", a=1).to_broadcast([128, 2, CH]),
                ALU.mult, ALU.mult), "wfin")
            dve.wait_ge(w_pe, PSTEP["bias"])
            wdone(nc.vector.tensor_copy(biasb[:, :], PS[6][0:TILE, 0:128]), "biasb")
            for b in range(PAIRS):
                for part, (t0, tn) in enumerate(WGROUPS):
                    n = 2 * b + part
                    dve.wait_ge(o_ready, n + 1)
                    nc.vector.tensor_tensor(
                        pair_tok[b].rearrange("p (w t c) -> p t w c", w=2, c=CH)[:, t0:t0 + tn],
                        PS[n % 4][0:TILE, 0:tn * 128].rearrange("p (t w c) -> p t w c", w=2, c=CH),
                        biasb[:, :].rearrange("p (a w c) -> p a w c", a=1, w=2).to_broadcast([TILE, tn, 2, CH]), ALU.add)\
                        .then_inc(o_done, 1)

        @block.tensor
        def _(pe):
            def mm(o, a, b, start=True, stop=True, **k):
                return nc.tensor.matmul(o, a, b, start=start, stop=stop, **k)

            def f_xc(blk, g, behind_k=False):
                if behind_k:
                    pe.wait_ge(k_done, 3 * g - 2)
                mm(bG[2][:, 0:TOK], centre[:, :], xcols(blk, g - HALVES * blk)).then_inc(xc_ready, 1)

            def f_xc_split(blk, g):
                pe.wait_ge(k_done, 3 * (HALVES * blk + g) + 4)
                pe.wait_ge(xl_done, NSPLIT * blk + g + 1)
                mm(bG[2][:, 0:TOK], centre_r[:, :], xh[:, :], True, False)
                mm(bG[2][:, 0:TOK], centre_r[:, :], xl[:, :], False, True).then_inc(xc_ready, 1)

            def f_var(g):
                pe.wait_ge(sq_done, g + 1)
                mm(bG[1][:, 0:TOK], avg64[:, :], sq[:, :]).then_inc(var_ready, 1)

            def f_qk(p, g1, buf):
                pe.wait_ge(z_done, g1 + 1)
                pe.wait_ge(rx_done, g1)
                mm(bG[2][:, 0:TOK], p["wk"][:, :], z[buf][:, :]).then_inc(k_ready, 1)
                mm(bG[1][:, 0:TOK], p["wq"][:, :], z[buf][:, :]).then_inc(q_ready, 1)

            def f_v(p, buf, wins):
                for w in wins:
                    for im in range(2):
                        r = slice(64 * im, 64 * im + 64)
                        last = mm(bG[0][64 * im:64 * im + NTOK, w * CH:(w + 1) * CH],
                                  z[buf][r, w * NTOK:(w + 1) * NTOK], p["wv2"][r, :])
                if w == WIN - 1:
                    last.then_inc(v_ready, 1)

            def scores(p, blk, odd, g1, w):
                if w == 0:
                    pe.wait_ge(kexp_done, HEADS * (g1 + 1))
                    pe.wait_ge(q_done, 3 * g1 + 2)
                if w == 1:
                    pe.wait_ge(v_done, 2 * g1 + 2)
                if w > 1:
                    pe.wait_ge(max_done, WIN * g1 + w - 1)
                t = win_kind(blk, odd, w)
                mm(bS[w % 2][0:NROWS, 0:HEADS * NTOK], qbd[:, w, :], kexp[:, w, :, :].rearrange("p h m -> p (h m)"),
                   True, False)
                mm(bS[w % 2][0:NROWS, 0:HEADS * NTOK], ident_r[0:NROWS, 0:NROWS], p["bn"][:, t, :], False, True)\
                    .then_inc(s_ready, 1)

            def maxt(g1):
                pe.wait_ge(nmaxw_done, 2 * (g1 + 1))
                pe.wait_ge(v_done, 2 * (g1 + 1))
                mm(bG[1][:, 0:50], nmaxw[:, :, :, :].rearrange("p a w h -> p (a w h)"), fold_r[:, :])\
                    .then_inc(mxt_ready, 1)

            def scores_t(p, blk, odd, g, w, buf, first):
                if w == 0:
                    pe.wait_ge(k_done, 3 * g + 3)
                    pe.wait_ge(rx_done, g + 1)
                pe.wait_ge(qexp_done, WIN * g + w + 1)
                if not (first and w < 2):
                    pe.wait_ge(exp_done, WIN * g + w - 1)
                t = win_kind(blk, odd, w)
                o = bST[w % 2][0:KROWS, 0:HEADS * NTOK]
                mm(o, kbd[buf][:, w, :], qexp[buf][:, w, :, :].rearrange("p h n -> p (h n)"), True, False)
                mm(o, dup_r[0:KROWS, 0:KROWS], p["bt"][:, t, :], False, False)
                mm(o, sel_r[:, w, 0:KROWS], rx[:, :, :].rearrange("p h n -> p (h n)"), False, True)\
                    .then_inc(st_ready, 1)

            def pv(g, w, buf, first):
                pe.wait_ge(exp_done, WIN * g + w + 1)
                if w == 0:
                    pe.wait_ge(v_done, 2 * g + 2)
                if w in (0, 4) and not first:
                    pe.wait_ge(rec_done, 2 * g - 1 + w // 4)
                for h in range(HEADS):
                    hh, h4 = h // 4, h % 4
                    c0 = (w % 4) * NROWS + hh * NTOK
                    last = mm(bO[w // 4][32 * h4:32 * h4 + 32, c0:c0 + NTOK], vbd[buf][:, w * HEADS + h, :],
                              pt[w % 4][:, h * NTOK:(h + 1) * NTOK])
                last.then_inc(av_ready, 1)

            def den(g, part):
                pe.wait_ge(osh_done, 2 * g + part + 1)
                pe.wait_ge(osl_done, 2 * g + part + 1)
                mm(bO[part][:, 0:4 * NROWS], dsel_r[:, :], osh[:, :], True, False)
                mm(bO[part][:, 0:4 * NROWS], dsel_r[:, :], osl[:, :], False, True).then_inc(den_ready, 1)

            def proj(p, g):
                pe.wait_ge(att_done, 2 * g + 2)
                for hh in range(2):
                    last = mm(bG[0][:, 0:TOK], p["wph"][:, hh, :], att[:, :, hh * NTOK:(hh + 1) * NTOK], hh == 0, hh == 1)
                last.then_inc(proj_ready, 1)

            def step(p, blk, g, u, first, more, more2, tail=None):
                G = HALVES * blk + g
                nb = (u + 1) % 2
                f = first and blk == 0

                def ahead(*wins):
                    if more:
                        for w in wins:
                            scores(p, blk, nb, G + 1, w)

                scores_t(p, blk, u, G, 0, u, f)
                scores_t(p, blk, u, G, 1, u, f)
                if not first:
                    den(G - 1, 1)
                pv(G, 0, u, f)
                if more:
                    f_qk(p, G + 1, nb)
                scores_t(p, blk, u, G, 2, u, f)
                pv(G, 1, u, f)
                scores_t(p, blk, u, G, 3, u, f)
                if more2:
                    f_xc_split(blk, g)
                if not first:
                    proj(p, G - 1)
                if more2:
                    pe.wait_ge(q_done, 3 * G + 6)
                    f_var(G + 2)
                ahead(0)
                if more and not first:
                    pe.wait_ge(res_done, G)
                if tail:
                    tail[0]()
                pv(G, 2, u, f)
                if more:
                    f_v(p, nb, range(WIN))
                if tail:
                    tail[1]()
                scores_t(p, blk, u, G, 4, u, f)
                ahead(1)
                pv(G, 3, u, f)
                ahead(2)
                scores_t(p, blk, u, G, 5, u, f)
                ahead(3)
                pv(G, 4, u, f)
                if tail:
                    tail[2]()
                ahead(4)
                den(G, 0)
                ahead(5)
                scores_t(p, blk, u, G, 6, u, f)
                ahead(6)
                ahead(7)
                pv(G, 5, u, f)
                scores_t(p, blk, u, G, 7, u, f)
                if more:
                    maxt(G + 1)
                if tail:
                    tail[3]()
                pv(G, 6, u, f)
                pv(G, 7, u, f)

            def start(blk):
                base, p = HALVES * blk, P[blk]
                f_v(p, 0, range(WIN))
                if blk:
                    pe.wait_ge(q_done, 3 * base + 3)
                    f_xc(blk, base + 1, True)
                    f_var(base + 1)
                pe.wait_ge(s_btab, blk + 1)
                for w in range(WIN):
                    scores(p, blk, 0, base, w)
                if blk:
                    pe.wait_ge(var_used, base + 2)
                maxt(base)

            def to_channels(i):
                pe.wait_ge(s_xin[i], 16 * 2 * (XGROUPS[i][1] - XGROUPS[i][0]))
                for b in range(*XGROUPS[i]):
                    src = pair_tok[b].rearrange("p (t k) -> p t k", k=128)
                    for part, (t0, tn) in enumerate(WGROUPS):
                        n = 2 * b + part
                        if n >= 4:
                            pe.wait_ge(s_tpcp, n - 3)
                        for t in range(tn):
                            last = nc.tensor.transpose(PS[1 + n % 4][:, TILE * t:TILE * (t + 1)], src[:, t0 + t, :],
                                                       ident[0:TILE, 0:TILE])
                        last.then_inc(s_tp, 1)

            pe.wait_ge(s_ident, 16)
            to_channels(0)
            pe.wait_ge(s_stat, 16)
            pe.wait_ge(s_tpcp, 2 * XGROUPS[0][1])
            f_xc(0, 0)
            f_var(0)

            pe.wait_ge(s_par, 16 * NPAR)

            def offsets(k):
                if k:
                    pe.wait_ge(s_prep, 3)
                raw, v, ps = wraw[k], P[k]["vec"], PS[5 * k]
                for w in range(2):
                    r = slice(CH * w, CH * w + CH)
                    for c in range(7):
                        lo, off = (CH * c, B1) if c < 3 else (CH * (c + 1), B2)
                        mm(ps[r, c:c + 1], raw[r, lo:lo + CH], v[r, off:off + 1])
                for hh in range(2):
                    last = mm(ps[:, CH * (1 + hh):CH * (2 + hh)], perm[hh][:, :], raw[:, 3 * CH:4 * CH])
                last.then_inc(s_fold, 1)
                pe.wait_ge(s_prep, 3 * k + 1)
                for w in range(2):
                    r = slice(CH * w, CH * w + CH)
                    last = mm(PS[5 - 5 * k][r, 0:1], raw[r, 3 * CH:4 * CH], v[r, VB:VB + 1])
                last.then_inc(s_fold, 1)

            pe.wait_ge(s_con, 16 * NCON)
            offsets(0)
            to_channels(1)
            offsets(1)
            pe.wait_ge(z_done, 1)
            f_xc(0, 1)
            f_var(1)
            to_channels(2)
            pe.wait_ge(s_bias, 16 * 2 * WS)
            pe.wait_ge(s_prep, NPREP)
            for k in range(2):
                if k:
                    pe.wait_ge(tab_link, 1)
                mm(PS[0][0:NROWS, 0:HEADS * NTOK], spread[:, :], rawb[k][:, :])
                mm(PS[5][0:KROWS, 0:HEADS * NTOK], turn[:, :], rawb[k][:, :]).then_inc(s_turn, 1)

            pe.wait_ge(s_round, 1)
            pe.wait_ge(s_zero, 3)
            pe.wait_ge(s_tpcp, 2 * PAIRS)
            pe.wait_ge(s_prep, NPREP)
            pe.wait_ge(tab_link, 2)
            pe.wait_ge(z_done, 2)
            f_qk(P[0], 0, 0)
            start(0)
            for blk in range(2):
                base = HALVES * blk
                p = P[blk]

                def m_xc(g, buf, first=False):
                    if not first:
                        pe.wait_ge(mz_done, base + g - 1)
                    mm(mX[buf][:, 0:TOK], centre[:, :], xcols(blk, g)).then_inc(mxc, 1)

                def m_var(g, first=False):
                    pe.wait_ge(msq, base + g + 1)
                    if not first:
                        pe.wait_ge(mvar_used, base + g)
                    mm(mV[:, 0:TOK], avg64[:, :], sq[:, :]).then_inc(mvar, 1)

                def fc1(g, c, buf, first):
                    if c == 0:
                        pe.wait_ge(mz_done, base + g + 1)
                    if not (first and c < 2):
                        pe.wait_ge(gelu_done, 4 * (base + g) + c - 1)
                    mm(mF1[c % 2][:, 0:TOK], p["f1"][:, c, :], z[buf][:, :]).then_inc(fc1_ready, 1)

                def fc2(g, c, first):
                    if c == 0 and not first:
                        pe.wait_ge(mres_done, base + g)
                    pe.wait_ge(gelu_done, 4 * (base + g) + c + 1)
                    last = mm(mF2[:, 0:TOK], p["f2"][:, c, :], hid[c], c == 0, c == 3)
                    if c == 3:
                        last.then_inc(fc2_ready, 1)

                def mstep(g, u, stats=None, first=False, before=None, between=None):
                    fc1(g, 0, u, first)
                    fc1(g, 1, u, first)
                    if stats:
                        stats[0]()
                    fc1(g, 2, u, first)
                    fc1(g, 3, u, first)
                    if stats:
                        stats[1]()
                    if before:
                        before()
                    fc2(g, 0, first)
                    fc2(g, 1, first)
                    if between:
                        between()
                    fc2(g, 2, first)
                    fc2(g, 3, first)

                def mstats(g, u):
                    return [lambda: m_xc(g, u), lambda: m_var(g)]

                step(p, blk, 0, 0, True, True, True)
                if blk:
                    pe.wait_ge(relay_done, PAIRS)
                step(p, blk, 1, 1, False, True, True)
                with pe.Fori(1, PAIRS - 1) as it:
                    for u in range(2):
                        step(p, blk, it * 2 + u, u, False, True, True)
                step(p, blk, HALVES - 2, 0, False, True, False)
                step(p, blk, HALVES - 1, 1, False, False, False,
                     tail=[lambda: m_xc(0, 0, True), lambda: m_var(0, blk == 0),
                           lambda: m_xc(1, 1, True), lambda: m_var(1)])
                G = base + HALVES - 1
                den(G, 1)

                def last_proj():
                    pe.wait_ge(rec_done, 2 * G + 1)
                    proj(p, G)

                def shift_sum():
                    if blk:
                        pe.wait_ge(w_dve, WSTEP["sum0"])
                        mm(PS[4][:, 0:1], dup[:, :], wcol[:, SUM0:SUM0 + 1]).then_inc(w_pe, 1)

                mstep(0, 0, mstats(2, 0), first=blk == 0, before=last_proj)
                mstep(1, 1, mstats(3, 1), between=shift_sum)
                with pe.Fori(1, PAIRS - 1) as it:
                    for u in range(2):
                        mstep(it * 2 + u, u, mstats(it * 2 + u + 2, u))
                if blk == 0:
                    def next_xc():
                        pe.wait_ge(relay_done, 1)
                        pe.wait_ge(mvar_used, HALVES)
                        f_xc(1, HALVES)

                    def next_var():
                        pe.wait_ge(mz_done, HALVES - 1)
                        f_var(HALVES)
                    mstep(HALVES - 2, 0, [next_xc, next_var])
                    mstep(HALVES - 1, 1, between=lambda: f_qk(P[1], HALVES, 0))
                    start(1)
                else:
                    mstep(HALVES - 2, 0)
                    mstep(HALVES - 1, 1)

            def moments(b, part):
                t0, tn = WGROUPS[part]
                pe.wait_ge(tt_done, 2 * b + part + 1)
                for t in range(tn):
                    for w in range(2):
                        last = mm(PS[7][CH * w:CH * w + CH, 0:CH + 1], tsb[part][:, t, w, 0:CH], tsb[part][:, t, w, :],
                                  b == 0 and part == 0 and t == 0, b == PAIRS - 1 and part == 1 and t == tn - 1)
                last.then_inc(cov_ready, 1)

            pe.wait_ge(w_dve, WSTEP["shift"])
            for b in range(PAIRS):
                pe.wait_ge(relay_done, PAIRS + b + 1)
                for part, (t0, tn) in enumerate(WGROUPS):
                    n = 2 * b + part
                    if n >= 2:
                        pe.wait_ge(tt_done, n - 1)
                    for t in range(tn):
                        c0 = (b * TILES + t0 + t) * TILE
                        last = nc.tensor.transpose(PS[4 + part][0:TILE, t * 128:(t + 1) * 128], XR[:, c0:c0 + TILE],
                                                   ident[:, :])
                    last.then_inc(tt_ready, 1)
                    if n >= 1:
                        moments(*divmod(n - 1, 2))
            moments(PAIRS - 1, 1)

            pe.wait_ge(w_dve, WSTEP["fold2"])
            mm(PS[0][:, 0:CH + 1], dup[:, :], fold2[:, :]).then_inc(w_pe, 1)
            pe.wait_ge(w_dve, WSTEP["mom"])
            mm(PS[1][0:1, 0:128], mom[:, CH:CH + 1], ident[:, :]).then_inc(w_pe, 1)
            pe.wait_ge(w_dve, WSTEP["rows"])
            mm(PS[2][:, 0:CH], wrow[:, 0:128], wrow[:, 128:128 + CH]).then_inc(w_pe, 1)
            pe.wait_ge(w_dve, WSTEP["diag"])
            mm(PS[3][:, 0:1], gsum[:, :], wcol[:, DIAG:DIAG + 1]).then_inc(w_pe, 1)
            for i in range(1, WH_ITER):
                pe.wait_ge(w_dve, WSTEP[f"p{i - 1}"])
                mm(PS[4][:, 0:256], psig[:, 0, :], psig[:, :, :].rearrange("p a c -> p (a c)")).then_inc(w_pe, 1)
                pe.wait_ge(w_dve, WSTEP[f"prod{i}"])
                mm(PS[5][:, 0:128], prod[:, 0, :], prod[:, 1, :]).then_inc(w_pe, 1)
            pe.wait_ge(w_dve, WSTEP["wfin"])
            mm(PS[6][0:TILE, 0:128], nmb[:, :], wfin[:, :], True, False)
            mm(PS[6][0:TILE, 0:128], ones1[:, :], bet[:, :], False, True).then_inc(w_pe, 1)

            for b in range(PAIRS):
                for part, (t0, tn) in enumerate(WGROUPS):
                    n = 2 * b + part
                    if n >= 4:
                        pe.wait_ge(o_done, n - 3)
                    for t in range(tn):
                        tile = XR[:, b * IMG_TOK:(b + 1) * IMG_TOK].rearrange("p (n t) -> p n t", t=TILES)[:, :, t0 + t]
                        last = mm(PS[n % 4][0:TILE, 128 * t:128 * (t + 1)], tile, wfin[:, :])
                    last.then_inc(o_ready, 1)


def constants():
    import numpy as np
    f = np.float32
    pw, pc = np.divmod(np.arange(128), CH)
    same_w = (pw[:, None] == pw[None, :])
    c = {}
    c["ident"] = np.eye(128, dtype=f)
    c["centre"] = (np.eye(128) - same_w / CH).astype(f)
    c["avg64"] = (same_w / CH).astype(f)
    c["dup"] = (pc[:, None] == pc[None, :]).astype(f)
    c["gsum"] = (same_w & (pc[:, None] // GROUP == pc[None, :] // GROUP)).astype(f)
    nw, nn = np.divmod(np.arange(NROWS), NTOK)
    fold = np.zeros((NROWS, 50), f)
    fold[np.arange(NROWS), nn] = 1
    c["fold"] = fold
    turn, spread = np.zeros((NTOK, KROWS), f), np.zeros((NTOK, NROWS), f)
    turn[NTOK - 1 - nn, 64 * nw + nn] = 1
    spread[nn, np.arange(NROWS)] = 1
    c["turn"], c["spread"] = turn, spread
    c["nmask"] = (np.arange(128)[:, None] % 32 // HD == np.arange(2)[None]).astype(f)
    for hh in range(2):
        pm = np.zeros((128, 128), f)
        for p in range(128):
            h, dd = divmod(pc[p], HD)
            if h // 4 == hh:
                pm[p, 32 * (h % 4) + HD * pw[p] + dd] = 1
        c[f"perm{hh}"] = pm
    c["wmask"] = np.stack([nw == 0, nw == 1], 1).astype(f)
    c["hmask"] = (pc[:, None] // HD == np.arange(HEADS)[None]).astype(f)
    win, rest = np.divmod(np.arange(128), 2 * HEADS)
    rw, rh = np.divmod(rest, HEADS)
    c["hmask2"] = (rh[:, None] == np.arange(HEADS)[None]).astype(f)
    sel = np.zeros((128, WIN, 128), f)
    for p in range(128):
        sel[p, win[p], 64 * rw[p]:64 * rw[p] + NTOK] = 1
    d = np.zeros((128, 128), f)
    for h4 in range(4):
        for r in range(32):
            d[32 * h4 + 16 + (r // HD if r < 2 * HD else 0), 32 * h4 + r] = 1
    c["dsel"] = d
    r, q = np.divmod(np.arange(NTOK), WS)
    row = (r[:, None] >= WS - SHIFT) != (r[None] >= WS - SHIFT)
    col = (q[:, None] >= WS - SHIFT) != (q[None] >= WS - SHIFT)
    m = np.stack([np.zeros((NTOK, NTOK), bool), col, row, row | col], 1) * f(-100)
    maskn, maskt = np.zeros((NROWS, 4, NTOK), f), np.zeros((KROWS, 4, NTOK), f)
    for w in range(2):
        maskn[NTOK * w:NTOK * w + NTOK] = m
        maskt[64 * w:64 * w + NTOK] = m
    c["maskn"], c["maskt"] = maskn.reshape(NROWS, -1), maskt.reshape(KROWS, -1)
    packed = np.zeros((128, CON_COLS), f)
    for name, (lo, n) in CON_AT.items():
        packed[0:c[name].shape[0], lo:lo + n] = c[name]
    return {"all": packed, "sel": sel.reshape(128, WIN * 128)}


def kernel(**inputs):
    import numpy as _np
    import concourse.bacc as _bacc
    from concourse.bass_utils import run_bass_kernel_spmd as _run

    nc = _bacc.Bacc("TRN2", target_bir_lowering=False, num_devices=1)
    arrays = {}

    def put(name, a):
        a = _np.ascontiguousarray(a)
        arrays[name] = a
        return nc.dram_tensor(name, a.shape, mybir.dt.from_np(a.dtype), kind="ExternalInput").ap()

    x = put("x_dram", inputs["x"])

    def param(name, k):
        return _np.asarray(inputs[f"L0_conv_{name}{k}"])

    weights, vectors = [], []
    for k in range(2):
        fc2 = param("fc2_w", k).reshape(4, CH, CH).transpose(1, 0, 2).reshape(CH, 4 * CH)
        weights.append(_np.concatenate([param("qkv_w", k), param("proj_w", k), param("fc1_w", k), fc2], 1))
        rows = [param(n, k).reshape(-1, CH) for n in VECTORS]
        vectors.append(_np.concatenate(rows, 0).T)
    par = {"w": [put(f"w{k}_dram", _np.concatenate([weights[k]] * 2, 0)) for k in range(2)],
           "vec": put("vec_dram", _np.concatenate([_np.concatenate(vectors, 1)] * 2, 0)),
           "bias_tab": [put(f"bias_tab{k}_dram", param("bias_tab", k)) for k in range(2)]}
    gamma, beta = put("gamma_dram", inputs["L1_conv_gamma"]), put("beta_dram", inputs["L1_conv_beta"])
    con = {n: put(f"c_{n}_dram", a) for n, a in constants().items()}
    out = nc.dram_tensor("out_dram", (IMAGES, SIDE, SIDE, CH), F32, kind="ExternalOutput").ap()
    build(nc, x, par, gamma, beta, con, out)
    r = _run(nc, [arrays], core_ids=[0])
    return r.results[0]["out_dram"]
```
